# Optimizing a Trainium2 kernel written in Bass

```python
import numpy as np
import jax
import jax.numpy as jnp

def _softmax(x, axis=-1):
    return jax.nn.softmax(x, axis=axis)

def _gelu(x):
    return jax.nn.gelu(x, approximate=True)

def _silu(x):
    return jax.nn.silu(x)

def _sigmoid(x):
    return jax.nn.sigmoid(x)

def _layernorm(x, axis=-1, eps=1e-05):
    m = jnp.mean(x, axis=axis, keepdims=True)
    v = jnp.var(x, axis=axis, keepdims=True)
    return (x - m) / jnp.sqrt(v + eps)

def _scatter_add(tgt, idx, src, axis=0):
    return tgt.at[idx].add(src)

def _segment_sum(src, seg, n):
    return jax.ops.segment_sum(src, seg, n)
kernel_name = 'mk_adaln_attn_ffn_d1_seqx_r4_f1e08c'

def setup_inputs(seed: int=0):
    np.random.seed(seed)
    _w = jnp.asarray

    def _rec_inputs():
        import jax
        import jax.numpy as jnp
        _rk = jax.random.key(seed)
        x = -7.109e-05 + 0.9999 * jax.random.normal(jax.random.fold_in(_rk, 1), (32, 64, 1024), jnp.float32)
        _lenS = 64 - jax.random.randint(jax.random.fold_in(_rk, 7), (32,), 0, max(1, 64 // 4) + 1, jnp.int32)
        _lenS2 = 64 - jax.random.randint(jax.random.fold_in(_rk, 8), (32,), 0, max(1, 64 // 4) + 1, jnp.int32)
        itok_B_0_15 = jax.random.randint(jax.random.fold_in(_rk, 11), (32,), 0, 16, jnp.int32)
        itok_B_0_7 = jax.random.randint(jax.random.fold_in(_rk, 12), (32,), 0, 8, jnp.int32)
        itok_B_2182_4065 = jax.random.randint(jax.random.fold_in(_rk, 14), (32,), 2182, 4066, jnp.int32)
        return (x, itok_B_0_15, itok_B_0_7, itok_B_2182_4065, _lenS)
    x, itok_B_0_15, itok_B_0_7, itok_B_2182_4065, _lenS = _rec_inputs()

    def _L0_cond_setup():
        import jax, jax.numpy as jnp
        import numpy as np
        B, C, T = (64, 64, 1024)
        S, D = (16, 64)
        key = jax.random.key(seed)
        k1, k2, k3 = jax.random.split(key, 3)
        x = jax.random.normal(k1, (B, C, T), dtype=jnp.float32)
        condition = jax.random.randint(k2, (B,), 0, S, dtype=jnp.int64)
        bound = float(np.sqrt(6.0 / C))
        weights = jax.random.uniform(k3, (S, C, D), dtype=jnp.float32, minval=-bound, maxval=bound)
        return {'x': x, 'condition': condition, 'weights': weights}
    _L0_cond_all = _L0_cond_setup()
    _L0_cond_in = {k: v for k, v in _L0_cond_all.items() if k in ('weights',)}
    del _L0_cond_all

    def _L0_attn_setup():
        import jax, jax.numpy as jnp
        import numpy as np
        import math
        B, S, H = (1, 512, 1024)
        NH, NKV, HD = (32, 8, 128)
        GS = 128
        WBITS = 4
        ZERO = float(2 ** (WBITS - 1))
        THETA = 10000.0

        def _dequant_matmul(x, qw, scales):
            w = (qw.astype(jnp.float32) - ZERO) * jnp.repeat(scales, GS, axis=0)
            return x @ w

        def _rope_tables(seq_len, dtype):
            inv_freq = 1.0 / THETA ** (jnp.arange(0, HD, 2, dtype=jnp.float32) / HD)
            freqs = jnp.arange(seq_len, dtype=jnp.float32)[:, None] * inv_freq
            emb = jnp.concatenate([freqs, freqs], axis=-1)
            return (jnp.cos(emb).astype(dtype), jnp.sin(emb).astype(dtype))

        def _rotate_half(x):
            x1, x2 = jnp.split(x, 2, axis=-1)
            return jnp.concatenate([-x2, x1], axis=-1)

        def _apply_rope(x, cos, sin):
            return x * cos[None, None] + _rotate_half(x) * sin[None, None]
        key = jax.random.key(seed)
        ks = jax.random.split(key, 9)
        small = lambda k, shp: jax.random.uniform(k, shp, jnp.float32) * 0.01 + 0.001
        return {'hidden_states': jax.random.normal(ks[0], (B, S, H), jnp.float32), 'scales_q': small(ks[1], (H // GS, NH * HD)), 'scales_k': small(ks[2], (H // GS, NKV * HD)), 'scales_v': small(ks[3], (H // GS, NKV * HD)), 'scales_o': small(ks[4], (NH * HD // GS, H)), 'qw_q': jax.random.randint(ks[5], (H, NH * HD), 0, 2 ** WBITS, jnp.int32), 'qw_k': jax.random.randint(ks[6], (H, NKV * HD), 0, 2 ** WBITS, jnp.int32), 'qw_v': jax.random.randint(ks[7], (H, NKV * HD), 0, 2 ** WBITS, jnp.int32), 'qw_o': jax.random.randint(ks[8], (NH * HD, H), 0, 2 ** WBITS, jnp.int32)}
    _L0_attn_all = _L0_attn_setup()
    _L0_attn_in = {k: v for k, v in _L0_attn_all.items() if k in ('scales_q', 'scales_k', 'scales_v', 'scales_o', 'qw_q', 'qw_k', 'qw_v', 'qw_o')}
    del _L0_attn_all

    def _L0_cond2_setup():
        import jax, jax.numpy as jnp
        import numpy as np
        SESSION_CHANNELS = [128, 160, 192, 224, 240, 248, 252, 64]
        N_SESS = len(SESSION_CHANNELS)
        B, MAX_C, MAX_T = (16, 64, 1024)
        HID, N_SRC = (128, 64)
        key = jax.random.key(seed)
        ks = jax.random.split(key, 7)
        session_ids = jax.random.randint(ks[0], (B,), 0, N_SESS)
        chan_table = jnp.asarray(SESSION_CHANNELS)
        channel_counts = chan_table[session_ids]
        seq_lens = jax.random.randint(ks[1], (B,), MAX_T // 2, MAX_T + 1)
        x = jax.random.normal(ks[2], (B, MAX_C, MAX_T), jnp.float32)
        cmask = (jnp.arange(MAX_C)[None, :] < channel_counts[:, None]).astype(x.dtype)
        tmask = (jnp.arange(MAX_T)[None, :] < seq_lens[:, None]).astype(x.dtype)
        x = x * cmask[:, :, None] * tmask[:, None, :]
        lim1 = 1.0 / np.sqrt(MAX_C)
        W_sess = jax.random.uniform(ks[3], (N_SESS, MAX_C, HID), jnp.float32, -lim1, lim1)
        b_sess = jax.random.uniform(ks[4], (N_SESS, HID), jnp.float32, -lim1, lim1)
        lim2 = 1.0 / np.sqrt(HID)
        W2 = jax.random.uniform(ks[5], (HID, N_SRC), jnp.float32, -lim2, lim2)
        b2 = jax.random.uniform(ks[6], (N_SRC,), jnp.float32, -lim2, lim2)
        return dict(x=x, session_ids=session_ids, channel_counts=channel_counts, seq_lens=seq_lens, W_sess=W_sess, b_sess=b_sess, W2=W2, b2=b2)
    _L0_cond2_all = _L0_cond2_setup()
    _L0_cond2_in = {k: v for k, v in _L0_cond2_all.items() if k in ('W_sess', 'b_sess', 'W2', 'b2')}
    del _L0_cond2_all

    def _L0_ffn_setup():
        import jax, jax.numpy as jnp
        import numpy as np
        NUM_EXPERTS = 8
        TOP_K = 2
        RANK = 16
        LORA_ALPHA = 32
        SCALING = LORA_ALPHA / RANK
        key = jax.random.key(seed)
        ks = jax.random.split(key, 6)
        B, S, D_IN, D_OUT = (4, 512, 1024, 1024)
        x = jax.random.normal(ks[0], (B, S, D_IN), dtype=jnp.float32)
        W_base = jax.random.normal(ks[1], (D_OUT, D_IN), dtype=jnp.float32) * 0.02
        b_base = jax.random.normal(ks[2], (D_OUT,), dtype=jnp.float32) * 0.02
        W_router = jax.random.normal(ks[3], (NUM_EXPERTS, D_IN), dtype=jnp.float32) * 0.02
        A = jax.random.normal(ks[4], (NUM_EXPERTS, RANK, D_IN), dtype=jnp.float32) * 0.02
        Bm = jax.random.normal(ks[5], (D_OUT, RANK), dtype=jnp.float32) * 0.02
        Bm = jnp.broadcast_to(Bm, (NUM_EXPERTS, D_OUT, RANK)) * jnp.arange(1, NUM_EXPERTS + 1, dtype=jnp.float32)[:, None, None] * 0.2
        return {'x': x, 'W_base': W_base, 'b_base': b_base, 'W_router': W_router, 'A': A, 'B': Bm}
    _L0_ffn_all = _L0_ffn_setup()
    _L0_ffn_in = {k: v for k, v in _L0_ffn_all.items() if k in ('W_base', 'b_base', 'W_router', 'A', 'B')}
    del _L0_ffn_all
    return {'x': x, 'itok_B_0_15': itok_B_0_15, 'itok_B_0_7': itok_B_0_7, 'itok_B_2182_4065': itok_B_2182_4065, '_lenS': _lenS, 'L0_cond_weights': _L0_cond_in['weights'], 'L0_attn_scales_q': _L0_attn_in['scales_q'], 'L0_attn_scales_k': _L0_attn_in['scales_k'], 'L0_attn_scales_v': _L0_attn_in['scales_v'], 'L0_attn_scales_o': _L0_attn_in['scales_o'], 'L0_attn_qw_q': _L0_attn_in['qw_q'], 'L0_attn_qw_k': _L0_attn_in['qw_k'], 'L0_attn_qw_v': _L0_attn_in['qw_v'], 'L0_attn_qw_o': _L0_attn_in['qw_o'], 'L0_cond2_W_sess': _L0_cond2_in['W_sess'], 'L0_cond2_b_sess': _L0_cond2_in['b_sess'], 'L0_cond2_W2': _L0_cond2_in['W2'], 'L0_cond2_b2': _L0_cond2_in['b2'], 'L0_ffn_W_base': _L0_ffn_in['W_base'], 'L0_ffn_b_base': _L0_ffn_in['b_base'], 'L0_ffn_W_router': _L0_ffn_in['W_router'], 'L0_ffn_A': _L0_ffn_in['A'], 'L0_ffn_B': _L0_ffn_in['B']}

def reference(x, itok_B_0_15, itok_B_0_7, itok_B_2182_4065, _lenS, L0_cond_weights, L0_attn_scales_q, L0_attn_scales_k, L0_attn_scales_v, L0_attn_scales_o, L0_attn_qw_q, L0_attn_qw_k, L0_attn_qw_v, L0_attn_qw_o, L0_cond2_W_sess, L0_cond2_b_sess, L0_cond2_W2, L0_cond2_b2, L0_ffn_W_base, L0_ffn_b_base, L0_ffn_W_router, L0_ffn_A, L0_ffn_B):
    import jax
    import jax.numpy as jnp

    def _L0_cond_ref(x, condition, weights):
        import jax, jax.numpy as jnp
        import numpy as np
        B, C, T = (64, 64, 1024)
        S, D = (16, 64)
        W = weights[condition]
        return jnp.einsum('bct,bcd->bdt', x, W)

    def _L0_attn_ref(hidden_states, scales_q, scales_k, scales_v, scales_o, qw_q, qw_k, qw_v, qw_o):
        import jax, jax.numpy as jnp
        import numpy as np
        import math
        B, S, H = (1, 512, 1024)
        NH, NKV, HD = (32, 8, 128)
        GS = 128
        WBITS = 4
        ZERO = float(2 ** (WBITS - 1))
        THETA = 10000.0

        def _dequant_matmul(x, qw, scales):
            w = (qw.astype(jnp.float32) - ZERO) * jnp.repeat(scales, GS, axis=0)
            return x @ w

        def _rope_tables(seq_len, dtype):
            inv_freq = 1.0 / THETA ** (jnp.arange(0, HD, 2, dtype=jnp.float32) / HD)
            freqs = jnp.arange(seq_len, dtype=jnp.float32)[:, None] * inv_freq
            emb = jnp.concatenate([freqs, freqs], axis=-1)
            return (jnp.cos(emb).astype(dtype), jnp.sin(emb).astype(dtype))

        def _rotate_half(x):
            x1, x2 = jnp.split(x, 2, axis=-1)
            return jnp.concatenate([-x2, x1], axis=-1)

        def _apply_rope(x, cos, sin):
            return x * cos[None, None] + _rotate_half(x) * sin[None, None]
        b, s, _ = hidden_states.shape
        q = _dequant_matmul(hidden_states, qw_q, scales_q).reshape(b, s, NH, HD).transpose(0, 2, 1, 3)
        k = _dequant_matmul(hidden_states, qw_k, scales_k).reshape(b, s, NKV, HD).transpose(0, 2, 1, 3)
        v = _dequant_matmul(hidden_states, qw_v, scales_v).reshape(b, s, NKV, HD).transpose(0, 2, 1, 3)
        cos, sin = _rope_tables(s, hidden_states.dtype)
        q = _apply_rope(q, cos, sin)
        k = _apply_rope(k, cos, sin)
        rep = NH // NKV
        k = jnp.repeat(k, rep, axis=1)
        v = jnp.repeat(v, rep, axis=1)
        scores = jnp.einsum('bhqd,bhkd->bhqk', q, k) / math.sqrt(HD)
        causal = jnp.tril(jnp.ones((s, s), dtype=bool))
        scores = jnp.where(causal[None, None], scores, jnp.finfo(scores.dtype).min)
        attn = jax.nn.softmax(scores.astype(jnp.float32), axis=-1).astype(q.dtype)
        ctx = jnp.einsum('bhqk,bhkd->bhqd', attn, v)
        ctx = ctx.transpose(0, 2, 1, 3).reshape(b, s, NH * HD)
        return _dequant_matmul(ctx, qw_o, scales_o)

    def _L0_cond2_ref(x, session_ids, channel_counts, seq_lens, W_sess, b_sess, W2, b2):
        import jax, jax.numpy as jnp
        import numpy as np
        SESSION_CHANNELS = [128, 160, 192, 224, 240, 248, 252, 64]
        N_SESS = len(SESSION_CHANNELS)
        B, MAX_C, MAX_T = (16, 64, 1024)
        HID, N_SRC = (128, 64)
        cmask = (jnp.arange(x.shape[1])[None, :] < channel_counts[:, None]).astype(x.dtype)
        xm = x * cmask[:, :, None]
        W = W_sess[session_ids]
        b = b_sess[session_ids]
        h = jnp.einsum('bct,bch->bht', xm, W) + b[:, :, None]
        h = jax.nn.gelu(h, approximate=False)
        out = jnp.einsum('bht,hs->bst', h, W2) + b2[None, :, None]
        tmask = (jnp.arange(x.shape[2])[None, :] < seq_lens[:, None]).astype(x.dtype)
        return out * tmask[:, None, :]

    def _L0_ffn_ref(x, W_base, b_base, W_router, A, B):
        import jax, jax.numpy as jnp
        import numpy as np
        NUM_EXPERTS = 8
        TOP_K = 2
        RANK = 16
        LORA_ALPHA = 32
        SCALING = LORA_ALPHA / RANK
        bs, seq, d_in = x.shape
        T = bs * seq
        xf = x.reshape(T, d_in)
        base = xf @ W_base.T + b_base
        logits = xf @ W_router.T
        rw, sel = jax.lax.top_k(logits, TOP_K)
        rw = jax.nn.softmax(rw, axis=-1)
        onehot = jax.nn.one_hot(sel, NUM_EXPERTS, dtype=rw.dtype)
        w = jnp.einsum('tk,tke->te', rw, onehot)
        h = jnp.einsum('td,erd->ter', xf, A)
        lora = jnp.einsum('ter,te,eor->to', h, w, B) * SCALING
        return (base + lora).reshape(bs, seq, -1)
    x = x + _L0_attn_ref(_L0_cond_ref(x, itok_B_0_15, L0_cond_weights), L0_attn_scales_q, L0_attn_scales_k, L0_attn_scales_v, L0_attn_scales_o, L0_attn_qw_q, L0_attn_qw_k, L0_attn_qw_v, L0_attn_qw_o)
    x = x + _L0_ffn_ref(_L0_cond2_ref(x, itok_B_0_7, _lenS, itok_B_2182_4065, L0_cond2_W_sess, L0_cond2_b_sess, L0_cond2_W2, L0_cond2_b2), L0_ffn_W_base, L0_ffn_b_base, L0_ffn_W_router, L0_ffn_A, L0_ffn_B)
    return x

_drawn_inputs = setup_inputs


def setup_inputs(seed=0):
    import zlib

    import numpy as np

    out = dict(_drawn_inputs(seed))
    spreads = {}
    factors = {'L0_cond2_b_sess': 5.488,
     'L0_cond2_b2': 2.782,
     'L0_ffn_b_base': 5.362,
     'L0_ffn_W_router': 3.672,
     'L0_ffn_A': 3.523,
     'L0_ffn_B': 3.444}
    for name, (base, spread) in spreads.items():
        noise = np.random.default_rng([zlib.crc32(name.encode()), seed]).standard_normal(out[name].shape)
        drawn = base * np.exp(spread * noise) if base else spread * noise
        out[name] = jnp.asarray(drawn.astype(out[name].dtype))
    for name, factor in factors.items():
        out[name] = (out[name] * factor).astype(out[name].dtype)
    return out
```

```python
import math
from contextlib import ExitStack

import concourse.bass as bass
from concourse import mybir

B, SEQ, H = 32, 64, 1024
TOK = B * SEQ
HD, NH, NKV = 128, 32, 8
REP = NH // NKV
HID, NEXP, RANK = 128, 8, 16
P = 128
KT = H // P
CH = 512
NC = TOK // CH
CB = CH // SEQ
CT = CH // P
NT = TOK // P
UNITS = ("k", 0, 1, 2, "v", 3)
NU = len(UNITS)
V_AT = UNITS.index("v")
ROPED = [u for u in UNITS if u != "v"]
WO_PIECES = 2 * REP
QKV_PIECES = 2 * NU
PIECES = WO_PIECES + QKV_PIECES
YT = 2 * CT

W_BITS = 11
H_BITS = 14
QKV_DOWN = 2.0 ** -26
P_UP = 2.0 ** 14
TINY = 2.0 ** -100
EXPONENT = 0x7F800000


def build(nc, x, cond_rep, ids_rep, seq_rep, len_rep, cond_w, s_q, s_k, s_v, s_o, q_q, q_k, q_v, q_o,
          w_sess, b_sess, w2, b2, w_base_t, b_base, w_router_t, a_t, b_cat,
          rope_cos, rope_sin, neg_mask, ident16, ident32, row_of, t_of, tri, out):
    f32, f16, i32 = mybir.dt.float32, mybir.dt.float16, mybir.dt.int32
    ALU, ACT, X = mybir.AluOpType, mybir.ActivationFunctionType, mybir.AxisListType.X
    MAX = bass.bass_isa.ReduceOp.max
    ds = bass.ds

    ctx = ExitStack()
    with ctx:
        def sb(name, shape, dt):
            return ctx.enter_context(nc.sbuf_tensor(name, shape, dt))

        def pb(name, shape=(P, CH), dt=f32):
            return ctx.enter_context(nc.psum_tensor(name, list(shape), dt))

        def sem(name):
            return ctx.enter_context(nc.semaphore(name))

        y = sb("y", [P, NT, H], f32)
        hid = sb("hid", [P, 2, KT, TOK], f16)
        wts = sb("wts", [P, 2 * KT * P * NU + 2 * REP * H], f16)
        w_qkv = wts[:, 0:2 * KT * P * NU].rearrange("p (u l k n) -> p u l k n", u=NU, l=2, k=KT)
        w_out = wts[:, 2 * KT * P * NU:].rearrange("p (h l n) -> p h l n", h=REP, l=2)
        stage = sb("stage", [P, 2, 2, 512], f32)
        w32 = sb("w32", [P, 2, 512], f32)
        qb = sb("qb", [P, 2, 2, CB, 2, SEQ], f16)
        kb = sb("kb", [P, 2, CH], f16)
        vb = sb("vb", [P, 2, CT, HD], f16)
        ra = sb("ra", [P, 2, CH], f32)
        rb = sb("rb", [P, CH], f32)
        sm = sb("sm", [P, 2, CB, SEQ], f32)
        pp = sb("pp", [P, 2, CH], f16)
        pt = sb("pt", [P, 2, CT, P], f16)
        cb = sb("cb", [P, 2, REP, CH], f16)
        rmax = sb("rmax", [P, 2, CB], f32)
        rsum = sb("rsum", [P, 2, CB], f32)
        rinv = sb("rinv", [P, 2, CB], f32)
        cos_t = sb("cos_t", [P, SEQ], f32)
        sin_t = sb("sin_t", [P, SEQ], f32)
        mask_t = sb("mask_t", [P, SEQ], f32)
        id16 = sb("id16", [P, P], f16)
        stat = sb("stat", [P, 12], f32)
        top = sb("top", [P, 12], f32)
        sc = sb("sc", [P, 24], f32)
        bits = sb("bits", [P, 8], i32)
        cidx = sb("cidx", [1, B], i32)
        sidx = sb("sidx", [1, B], i32)

        raw_max = sm[:, :, :, :].rearrange("p a b s -> p a (b s)")
        so_raw = ra[:, 0, 0:256]
        wc = cb[:, :, :, :].bitcast(f32).rearrange("p a h c -> p (a h c)").rearrange("p (i d) -> p i d", i=NT)

        pj = [pb("pj0"), pb("pj1")]
        sa, sbk, ex = pb("sa"), pb("sbk"), pb("ex")
        tp = pb("tp", (P, 2, CT, P), f16)
        cx = [pb("cx0"), pb("cx1")]
        score_bank = [sbk, sa]
        out_bank = [ex, sa, sbk]

        names = """x_in consts_in idx_in stats_in table_in wc_zero wc_in
                   stat_w stat_x top_w top_x scal w_scales_ready h_scale_ready
                   cond_done cond_hi cond_split
                   dq_scaled dq_hi w_ready
                   proj_done proj_read rope_sum rope_hi qk_ready v_hi
                   scores_done masked rowmaxed shifted exps summed inverted probs probs_hi probs_split
                   tp_done pt_copied pv_done ctx_hi ctx_split o_done y_added
                   wsess_in masks_made wsess_masked onehot_made bias_done bias_ready c2_in
                   hid_done hid_ready src_done src_biased src_ready ffn_in ffn_in2
                   lgt_done lgt_copied lg_done lg_copied route route_exp route_ready
                   wexp_done wexp_copied lora_done lora_ready base_done base_added result stored"""
        S = {n: sem(n) for n in names.split()}
        staged = [sem("staged0"), sem("staged1")]

        block = ctx.enter_context(nc.Block())

        xf = hid[:, :, :, :].bitcast(f32).rearrange("p l k t -> p (l k t)").rearrange("p (k t) -> p k t", k=KT)
        arena = wts[:, :].bitcast(f32)
        wb = arena[:, 0:8192].rearrange("p (k n) -> p k n", k=KT)
        at_t = arena[:, 8192:9216].rearrange("p (k n) -> p k n", k=KT)
        bc_t = arena[:, 9216:10240]
        ws = qb[:, :, :, :, :, :].bitcast(f32).rearrange("p a l b h s -> p (a l b h s)").rearrange("p (i d) -> p i d", i=NT)
        hw = ws.rearrange("p i d -> p (i d)")
        h2 = [cb[:, :, :, :].bitcast(f32).rearrange("p a h c -> p (a h c)").rearrange("p (e t) -> p e t", e=2),
              stage[:, :, :, :].rearrange("p a b n -> p (a b n)").rearrange("p (e t) -> p e t", e=2)]
        gates = h2[0].rearrange("p e t -> p (e t)").rearrange("p (t e r) -> p t e r", t=NT, e=NEXP)
        bb_t = w32[:, :, :].rearrange("p a n -> p (a n)")
        small = rb[:, :]
        id32 = small[:, 0:128]
        w2_t = small[:, 128:192]
        b2_t = small[:, 192:256]
        wr_t = small[:, 256:320].rearrange("p (k e) -> p k e", k=KT)
        tri_t = small[:, 320:384]
        row_t = small[:, 384:385]
        tt_t = small[:, 385:393]
        len_t = small[:, 393:409].bitcast(i32)
        seq_t = small[:, 409:441].bitcast(i32)
        ids_t = small[0:NEXP, 441:473].bitcast(i32)
        bias_t = small[:, 473:505]
        misc = kb[:, :, :].bitcast(f32).rearrange("p l t -> p (l t)")
        bs_t = misc[0:NEXP, 0:128]
        hot_t = misc[0:NEXP, 128:160]
        cm_t = misc[:, 160:176]
        tm_t = misc[:, 192:448].rearrange("p (k b) -> p k b", k=KT)
        vm = vb[:, :, :, :].bitcast(f32).rearrange("p l t d -> p (l t d)")
        lg = vm[:, 0:128].rearrange("p (t e) -> p t e", t=NT)
        le = vm[:, 128:256].rearrange("p (t e) -> p t e", t=NT)
        rk = vm[:, 256:384].rearrange("p (t e) -> p t e", t=NT)
        l1 = vm[:, 384:400]
        dn = vm[:, 400:416]
        di = vm[:, 416:432]
        big1 = sm[:, :, :, :].rearrange("p a b s -> p (a b s)")
        big2 = ra[:, :, :].rearrange("p a n -> p (a n)")
        lgt = pp[:, :, :].bitcast(f32).rearrange("p l t -> p (l t)")
        wx = pt[:, :, :, :].bitcast(f32).rearrange("p l t n -> p (l t n)")

        SH, ISH, S4, IS4, A, QS, KS, F_SCORE, AV, F_OUT, M = 0, 1, 2, 6, 10, 11, 12, 13, 14, 15, 16

        def col(n, k=1):
            return sc[:, n:n + k]
        UNIT_SCALE = {u: col(S4 + {"k": 1, "v": 2}.get(u, 0)) for u in UNITS}

        def roped_index(j):
            return sum(1 for u in UNITS[:j] if u != "v")

        lg_bank = tp[:, :, :, :].bitcast(f32).rearrange("p l t n -> p (l t n)")
        base_bank = [ex, cx[0], cx[1], sa]
        h_bank = [[pj[0], pj[1]], [cx[0], cx[1]]]

        def cond_bank(n):
            return (pj[0], pj[1], ex, cx[0])[n % 4]

        def ctx_src(e):
            return cx[e][:, :].rearrange("p (m s) -> p m s", s=SEQ)

        def ctx_columns(e, j):
            return cx[e][:, :].rearrange("p (h j s) -> p j h s", h=2, s=SEQ)[:, j]

        def ctx_dst(h, e, part):
            return cb[:, part, 2 * h:2 * h + 2, :].rearrange("p h (j e s) -> p e (h j) s", e=2, s=SEQ)[:, e]

        @block.sync
        def _(sp):
            sp.sem_inc(S["scores_done"], 2)
            sp.sem_inc(S["tp_done"], 2)
            sp.sem_inc(S["probs_split"], 2)
            sp.sem_inc(S["pv_done"], 2)
            sp.sem_inc(S["pt_copied"], 2)
            sp.sem_inc(S["ctx_split"], 2)
            sp.sem_inc(S["o_done"], YT)
            sp.sem_inc(S["y_added"], YT)
            sp.dma_start(raw_max[:, 0, 0:256], s_q.rearrange("a (b n) -> (a b) n", b=16)).then_inc(S["stats_in"], 16)
            sp.dma_start(raw_max[:, 0, 256:320], s_k.rearrange("a (b n) -> (a b) n", b=16)).then_inc(S["stats_in"], 16)
            sp.dma_start(raw_max[:, 0, 320:384], s_v.rearrange("a (b n) -> (a b) n", b=16)).then_inc(S["stats_in"], 16)
            sp.dma_start(so_raw, s_o.rearrange("a (b n) -> (a b) n", b=4)).then_inc(S["stats_in"], 16)
            sp.dma_start(raw_max[:, 1, :], cond_w.rearrange("s (q c) d -> (s q) (c d)", q=8)).then_inc(S["stats_in"], 16)
            sp.dma_start(cidx[:, :], cond_rep).then_inc(S["idx_in"], 16)
            sp.dma_start(sidx[:, :], ids_rep[0:1, :]).then_inc(S["idx_in"], 16)

            def load_piece(g, z):
                slot = z % 2
                if isinstance(g, int):
                    if PIECES * g + z >= 2:
                        sp.wait_ge(S["dq_scaled"], PIECES * g + z - 1)
                else:
                    sp.wait_ge(S["dq_scaled"], g * PIECES + (z - 1))
                if z < QKV_PIECES:
                    u, half = UNITS[z // 2], z % 2
                    qw, s = {"k": (q_k, s_k), "v": (q_v, s_v)}.get(u, (q_q, s_q))
                    col = g * HD if u in ("k", "v") else g * (REP * HD) + u * HD
                    rows = 4 * P * half
                    src = qw[rows:rows + 4 * P, ds(col, HD)].rearrange("(k p) n -> p k n", p=P)
                    scale = s[4 * half:4 * half + 4, ds(col, HD)].partition_broadcast(P)
                    shape = "p (k n) -> p k n"
                    sp.dma_start(stage[:, slot, 0, :].bitcast(i32).rearrange(shape, k=4), src).then_inc(staged[slot], 16)
                    sp.dma_start(stage[:, slot, 1, :].rearrange(shape, k=4), scale).then_inc(staged[slot], 16)
                else:
                    h, half = (z - QKV_PIECES) // 2, z % 2
                    src = q_o[ds(g * (REP * HD) + h * HD, HD), half * 512:half * 512 + 512]
                    scale = s_o[ds(g * REP + h, 1), half * 512:half * 512 + 512].rearrange("a n -> (a n)").partition_broadcast(P)
                    sp.dma_start(stage[:, slot, 0, :].bitcast(i32), src).then_inc(staged[slot], 16)
                    sp.dma_start(stage[:, slot, 1, :], scale).then_inc(staged[slot], 16)

            load_piece(0, 0)
            load_piece(0, 1)
            for part in range(NC):
                sp.dma_start(y[:, CT * part:CT * (part + 1), :],
                             x[CH * part:CH * (part + 1), :].rearrange("(i p) n -> p i n", p=P)).then_inc(S["x_in"], 16)
            sp.wait_ge(S["idx_in"], 32)
            sp.wait_ge(S["wc_zero"], 1)
            for odd in range(2):
                with sp.Fori(0, NT) as i:
                    s = sp.value_load(cidx[0:1, ds(i * 2 + odd, 1)], min_val=0, max_val=15)
                    sp.dma_start(wc[SEQ * odd:SEQ * (odd + 1), ds(i, 1), SEQ * odd:SEQ * (odd + 1)],
                                 cond_w[ds(s, 1), :, :].rearrange("a c d -> c a d")).then_inc(S["wc_in"], 16)
            for dst, src in ((cos_t, rope_cos), (sin_t, rope_sin), (mask_t, neg_mask), (id16, ident16)):
                sp.dma_start(dst[:, :], src).then_inc(S["consts_in"], 16)
            for z in range(2, PIECES):
                load_piece(0, z)
            with sp.Fori(1, NKV) as g:
                for z in range(PIECES):
                    load_piece(g, z)

            sp.wait_ge(S["scores_done"], 2 + 2 * NKV * NC)
            for odd in range(2):
                with sp.Fori(0, NT) as i:
                    s = sp.value_load(sidx[0:1, ds(i * 2 + odd, 1)], min_val=0, max_val=7)
                    sp.dma_start(ws[SEQ * odd:SEQ * (odd + 1), ds(i, 1), :],
                                 w_sess[ds(s, 1), :, :].rearrange("a c d -> c a d")).then_inc(S["wsess_in"], 16)
            sp.wait_ge(S["qk_ready"], 5 * NKV * NC)
            sp.wait_ge(S["probs_split"], 2 + 2 * NKV * NC)
            for dst, src in ((b2_t, b2.partition_broadcast(P)), (w2_t, w2), (bs_t, b_sess), (ids_t, ids_rep),
                             (len_t, len_rep), (seq_t, seq_rep), (row_t, row_of), (tt_t, t_of), (tri_t, tri),
                             (id32, ident32)):
                sp.dma_start(dst, src).then_inc(S["c2_in"], 16)
            sp.dma_start(wr_t, w_router_t.rearrange("(k p) e -> p k e", p=P)).then_inc(S["c2_in"], 16)
            sp.wait_ge(S["proj_done"], NU * NKV * NC)
            sp.dma_start(wb[:, 0:6, :], w_base_t[0:6 * P, :].rearrange("(k p) n -> p k n", p=P)).then_inc(S["ffn_in"], 16)
            sp.wait_ge(S["o_done"], YT + YT * NKV * NC)
            sp.dma_start(at_t, a_t.rearrange("(k p) n -> p k n", p=P)).then_inc(S["ffn_in2"], 16)
            sp.dma_start(wb[:, 6:8, :], w_base_t[6 * P:, :].rearrange("(k p) n -> p k n", p=P)).then_inc(S["ffn_in"], 16)
            sp.dma_start(bc_t, b_cat).then_inc(S["ffn_in"], 16)
            sp.dma_start(bb_t, b_base.partition_broadcast(P)).then_inc(S["ffn_in"], 16)
            for t in range(NT):
                sp.wait_ge(S["result"], 2 * (t + 1))
                sp.dma_start(out[P * t:P * (t + 1), :], y[:, t, :]).then_inc(S["stored"], 16)
            sp.wait_ge(S["stored"], 16 * NT)

        @block.gpsimd
        def _(gp):
            gp.memset(wc, 0.0).then_inc(S["wc_zero"], 1)
            gp.wait_ge(S["stat_w"], 1)
            gp.partition_all_reduce(top[:, 4:9], stat[:, 4:9], P, MAX).then_inc(S["top_w"], 1)
            gp.wait_ge(S["stat_x"], 1)
            gp.partition_all_reduce(top[:, 0:4], stat[:, 0:4], P, MAX).then_inc(S["top_x"], 1)

        @block.vector
        def _(dve):
            chain = [0]

            def link(ins):
                chain[0] += 1
                ins.then_inc(S["scal"], 1)
                dve.wait_ge(S["scal"], chain[0])

            def dequant_scale(g, z):
                slot = z % 2
                dve.wait_ge(staged[slot], 32 * (PIECES // 2) * g + 32 * (z // 2 + 1))
                if not isinstance(g, int) or PIECES * g + z >= 2:
                    dve.wait_ge(S["w_ready"], PIECES * g + (z - 1))
                dve.scalar_tensor_tensor(out=w32[:, slot, :], in0=stage[:, slot, 0, :].bitcast(i32), scalar=-8.0,
                                         in1=stage[:, slot, 1, :], op0=ALU.add, op1=ALU.mult).then_inc(S["dq_scaled"], 1)

            def piece_dst(z, part):
                if z < QKV_PIECES:
                    return w_qkv[:, z // 2, part, 4 * (z % 2):4 * (z % 2) + 4, :].rearrange("p k n -> p (k n)")
                return w_out[:, (z - QKV_PIECES) // 2, part, 512 * (z % 2):512 * (z % 2) + 512]

            def dequant_split(g, z):
                scale = UNIT_SCALE[UNITS[z // 2]] if z < QKV_PIECES else col(S4 + 3)
                dve.wait_ge(S["dq_hi"], PIECES * g + z + 1)
                dve.scalar_tensor_tensor(out=piece_dst(z, 1), in0=w32[:, z % 2, :], scalar=scale,
                                         in1=piece_dst(z, 0), op0=ALU.mult, op1=ALU.subtract).then_inc(S["w_ready"], 1)

            def dequant(g, z):
                dequant_scale(g, z)
                dequant_scale(g, z + 1)
                dequant_split(g, z)
                dequant_split(g, z + 1)

            dve.wait_ge(S["stats_in"], 80)
            for n, src in enumerate((raw_max[:, 1, :], raw_max[:, 0, 0:256], raw_max[:, 0, 256:320],
                                     raw_max[:, 0, 320:384], so_raw)):
                last = dve.tensor_reduce(stat[:, 4 + n:5 + n], src, X, ALU.max, apply_absolute_value=True)
            last.then_inc(S["stat_w"], 1)
            dve.wait_ge(S["top_w"], 1)
            link(dve.tensor_scalar_max(col(M, 4), top[:, 5:9], TINY))
            link(dve.tensor_single_scalar(bits[:, 0:4], col(M, 4).bitcast(i32), EXPONENT, ALU.bitwise_and))
            link(dve.tensor_scalar(col(S4, 4).bitcast(i32), bits[:, 0:4], -1.0, float((254 + W_BITS) << 23), ALU.mult, ALU.add))
            link(dve.tensor_scalar(col(IS4, 4), bits[:, 0:4].bitcast(f32), 2.0 ** -W_BITS, None, ALU.mult))
            dve.sem_inc(S["w_scales_ready"], 1)
            for z in range(0, QKV_PIECES, 2):
                dequant(0, z)
            for part in range(NC):
                dve.wait_ge(S["x_in"], 16 * NC)
                last = dve.tensor_reduce(stat[:, part:part + 1], y[:, CT * part:CT * (part + 1), :].rearrange("p i n -> p (i n)"),
                                         X, ALU.max, apply_absolute_value=True)
            last.then_inc(S["stat_x"], 1)
            dve.wait_ge(S["top_x"], 1)
            link(dve.reduce_max(col(M), top[:, 0:4], X))
            link(dve.scalar_tensor_tensor(out=col(M), in0=col(M), scalar=float(SEQ), in1=top[:, 4:5], op0=ALU.mult, op1=ALU.mult))
            link(dve.tensor_scalar_max(col(M), col(M), TINY))
            link(dve.tensor_single_scalar(bits[:, 4:5], col(M).bitcast(i32), EXPONENT, ALU.bitwise_and))
            link(dve.tensor_scalar(col(SH).bitcast(i32), bits[:, 4:5], -1.0, float((254 + H_BITS) << 23), ALU.mult, ALU.add))
            dve.sem_inc(S["h_scale_ready"], 1)
            link(dve.tensor_scalar(col(ISH), bits[:, 4:5].bitcast(f32), 2.0 ** -H_BITS, None, ALU.mult))
            link(dve.tensor_scalar(col(A), col(ISH), 1.0 / QKV_DOWN, None, ALU.mult))
            link(dve.tensor_tensor(col(QS), col(A), col(IS4), ALU.mult))
            link(dve.scalar_tensor_tensor(out=col(KS), in0=col(A), scalar=HD ** -0.5, in1=col(IS4 + 1), op0=ALU.mult, op1=ALU.mult))
            link(dve.tensor_tensor(col(F_SCORE), col(QS), col(KS), ALU.mult))
            link(dve.tensor_tensor(col(AV), col(A), col(IS4 + 2), ALU.mult))
            link(dve.tensor_tensor(col(F_OUT), col(AV), col(IS4 + 3), ALU.mult))
            for c in range(NC):
                for k in range(KT):
                    n = c * KT + k
                    dve.wait_ge(S["cond_hi"], n + 1)
                    t = slice(CH * c, CH * (c + 1))
                    dve.scalar_tensor_tensor(out=hid[:, 1, k, t], in0=cond_bank(n)[:, :], scalar=col(SH),
                                             in1=hid[:, 0, k, t], op0=ALU.mult, op1=ALU.subtract).then_inc(S["cond_split"], 1)

            def tables(t, b):
                return t[:, :].unsqueeze(1).broadcast_to([P, b, SEQ])

            def rope_write(idx, part):
                u = UNITS[idx]
                if u == "k":
                    return kb[:, part, :].rearrange("p (b s) -> p b s", b=CB)
                return qb[:, u // 2, part, :, u % 2, :]

            def rope(p4, j):
                g, c = p4
                n = NU * NC * g + (NU * c + j)
                m = 5 * NC * g + (5 * c + roped_index(j))
                bank = pj[j % 2]
                a = ra[:, roped_index(j) % 2, :].rearrange("p (b s) -> p b s", b=CB)
                b = rb[:, :].rearrange("p (b s) -> p b s", b=CB)
                src = bank[:, :].rearrange("p (b s) -> p b s", b=CB)
                dve.wait_ge(S["proj_done"], n + 1)
                if not isinstance(g, int) or m >= 2:
                    dve.wait_ge(S["qk_ready"], m - (1 if roped_index(j) else 0))
                dve.tensor_tensor(a, src, tables(cos_t, CB), ALU.mult)
                half = HD // 2
                if not isinstance(g, int) or m >= 1:
                    dve.wait_ge(S["rope_sum"], m)
                dve.tensor_tensor(b[0:half], src[half:HD], sin_t[half:HD, :].unsqueeze(1).broadcast_to([half, CB, SEQ]), ALU.mult)
                dve.tensor_tensor(b[half:HD], src[0:half], sin_t[0:half, :].unsqueeze(1).broadcast_to([half, CB, SEQ]),
                                  ALU.mult).then_inc(S["proj_read"], 1)
                dve.wait_ge(S["proj_read"], n + 1)
                dve.tensor_tensor(a, a, b, ALU.add).then_inc(S["rope_sum"], 1)

            def rope_split(p4, j):
                g, c = p4
                m = 5 * NC * g + (5 * c + roped_index(j))
                a = ra[:, roped_index(j) % 2, :].rearrange("p (b s) -> p b s", b=CB)
                dve.wait_ge(S["rope_hi"], m + 1)
                dve.tensor_tensor(rope_write(j, 1), a, rope_write(j, 0), ALU.subtract).then_inc(S["qk_ready"], 1)

            def v_split(p4):
                g, c = p4
                dve.wait_ge(S["v_hi"], NC * g + (c + 1))
                dve.scalar_tensor_tensor(out=vb[:, 1, :, :].rearrange("p t d -> p (t d)"), in0=pj[V_AT % 2][:, :], scalar=QKV_DOWN,
                                         in1=vb[:, 0, :, :].rearrange("p t d -> p (t d)"), op0=ALU.mult,
                                         op1=ALU.subtract).then_inc(S["proj_read"], 1)

            def soft_shift(g, c, h):
                r = 2 * NC * g + (2 * c + h)
                dve.wait_ge(S["scores_done"], r + 1 + 2)
                dve.wait_ge(S["probs_split"], r + 1)
                dve.scalar_tensor_tensor(out=sm[:, h, :, :], in0=score_bank[h][:, :].rearrange("p (b s) -> p b s", b=CB),
                                         scalar=col(F_SCORE), in1=tables(mask_t, CB), op0=ALU.mult,
                                         op1=ALU.add).then_inc(S["masked"], 1)
                dve.wait_ge(S["masked"], r + 1)
                dve.reduce_max(rmax[:, h, :], sm[:, h, :, :], X).then_inc(S["rowmaxed"], 1)
                dve.wait_ge(S["rowmaxed"], r + 1)
                dve.tensor_tensor(sm[:, h, :, :], sm[:, h, :, :], rmax[:, h, :].unsqueeze(2).broadcast_to([P, CB, SEQ]),
                                  ALU.subtract).then_inc(S["shifted"], 1)

            def soft_norm(g, c, h):
                r = 2 * NC * g + (2 * c + h)
                dve.wait_ge(S["exps"], r + 1)
                dve.reduce_sum(rsum[:, h, :], sm[:, h, :, :], X).then_inc(S["summed"], 1)
                dve.wait_ge(S["summed"], r + 1)
                dve.reciprocal(rinv[:, h, :], rsum[:, h, :]).then_inc(S["inverted"], 1)
                dve.wait_ge(S["inverted"], r + 1)
                dve.scalar_tensor_tensor(out=sm[:, h, :, :], in0=sm[:, h, :, :], scalar=P_UP,
                                         in1=rinv[:, h, :].unsqueeze(2).broadcast_to([P, CB, SEQ]), op0=ALU.mult,
                                         op1=ALU.mult).then_inc(S["probs"], 1)

            def prob_split(g, c, h):
                r = 2 * NC * g + (2 * c + h)
                dve.wait_ge(S["probs_hi"], r + 1)
                dve.tensor_tensor(pp[:, 1, :], sm[:, h, :, :].rearrange("p b s -> p (b s)"), pp[:, 0, :],
                                  ALU.subtract).then_inc(S["probs_split"], 1)

            def pt_copy(g, c, h):
                r = 2 * NC * g + (2 * c + h)
                dve.wait_ge(S["tp_done"], r + 1 + 2)
                dve.wait_ge(S["pv_done"], r + 2)
                dve.tensor_copy(pt[:, :, :, :].rearrange("p l t n -> p (l t n)"),
                                tp[:, :, :, :].rearrange("p l t n -> p (l t n)")).then_inc(S["pt_copied"], 1)

            def ctx_lo(g, c, h):
                r = 2 * NC * g + (2 * c + h)
                for e in range(2):
                    dve.wait_ge(S["ctx_hi"], 4 * NC * g + (4 * c + 2 * h + e + 1))
                    last = dve.scalar_tensor_tensor(out=ctx_dst(h, e, 1), in0=ctx_src(e), scalar=1.0 / P_UP,
                                                    in1=ctx_dst(h, e, 0), op0=ALU.mult, op1=ALU.subtract)
                last.then_inc(S["ctx_split"], 1)

            def add_out(g, c):
                for t in range(YT):
                    dve.wait_ge(S["o_done"], YT * NC * g + (YT * c + t + 1 + YT))
                    dst = y[:, CT * c + t // 2, 512 * (t % 2):512 * (t % 2) + 512]
                    dve.scalar_tensor_tensor(out=dst, in0=out_bank[t % 3][:, :], scalar=col(F_OUT), in1=dst,
                                             op0=ALU.mult, op1=ALU.add).then_inc(S["y_added"], 1)

            dve.wait_ge(S["consts_in"], 64)

            def step(g, c, ahead, extra):
                soft_shift(g, c, 0)
                soft_shift(g, c, 1)
                soft_norm(g, c, 0)
                soft_norm(g, c, 1)
                if ahead:
                    rope(ahead, 0)
                prob_split(g, c, 0)
                if ahead:
                    rope_split(ahead, 0)
                    extra(0)
                    rope(ahead, 1)
                pt_copy(g, c, 0)
                if ahead:
                    rope_split(ahead, 1)
                prob_split(g, c, 1)
                if ahead:
                    extra(1)
                    rope(ahead, 2)
                pt_copy(g, c, 1)
                ctx_lo(g, c, 0)
                if ahead:
                    rope_split(ahead, 2)
                    extra(2)
                    rope(ahead, 3)
                ctx_lo(g, c, 1)
                if ahead:
                    rope_split(ahead, 3)
                    extra(3)
                    v_split(ahead)
                    extra(4)
                    rope(ahead, 5)
                    rope_split(ahead, 5)
                    extra(5)
                add_out(g, c)

            def group(g, last=False):
                def wo(j):
                    if j < REP:
                        dequant(g, QKV_PIECES + 2 * j)

                def nxt(j):
                    dequant(g + 1, 2 * j)
                for c in range(NC):
                    ahead = (g, c + 1) if c + 1 < NC else (None if last else (g + 1, 0))
                    extra = wo if c == 0 else nxt if (c == 2 and not last) else (lambda j: None)
                    step(g, c, ahead, extra)

            for j in range(NU):
                if j == V_AT:
                    v_split((0, 0))
                else:
                    rope((0, 0), j)
                    rope_split((0, 0), j)
            with dve.Fori(0, NKV - 1) as g:
                group(g)
            group(NKV - 1, last=True)

            dve.wait_ge(S["c2_in"], 16 * 11)
            dve.tensor_scalar(hot_t, ids_t, row_t[0:NEXP, :], None, ALU.is_equal).then_inc(S["onehot_made"], 1)
            dve.tensor_scalar(cm_t, len_t, row_t, None, ALU.is_gt)
            dve.tensor_tensor(tm_t, seq_t.unsqueeze(1).broadcast_to([P, KT, B]), tt_t.unsqueeze(2).broadcast_to([P, KT, B]),
                              ALU.is_gt).then_inc(S["masks_made"], 1)
            dve.wait_ge(S["masks_made"], 1)
            dve.wait_ge(S["wsess_in"], 16 * B)
            dve.tensor_tensor(ws, ws, cm_t.unsqueeze(2).broadcast_to([P, NT, HID]), ALU.mult).then_inc(S["wsess_masked"], 1)
            dve.wait_ge(S["bias_done"], 1)
            dve.tensor_copy(bias_t, ex[:, 0:B]).then_inc(S["bias_ready"], 1)
            for i in range(NT):
                for kh in range(2):
                    n = 2 * i + kh
                    dve.wait_ge(S["src_done"], n + 1)
                    tmp = big1[:, 512 * kh:512 * kh + 512].rearrange("p (k s) -> p k s", s=SEQ)
                    dve.tensor_tensor(tmp, score_bank[kh][:, :].rearrange("p (k s) -> p k s", s=SEQ),
                                      b2_t.unsqueeze(1).broadcast_to([P, 8, SEQ]), ALU.add).then_inc(S["src_biased"], 1)
                    dve.wait_ge(S["src_biased"], n + 1)
                    for kk in range(4):
                        k = 4 * kh + kk
                        last = dve.tensor_tensor(xf[:, k, P * i:P * (i + 1)].rearrange("p (e s) -> p e s", e=2),
                                                 tmp[:, 2 * kk:2 * kk + 2, :],
                                                 tm_t[:, k, 2 * i:2 * i + 2].unsqueeze(2).broadcast_to([P, 2, SEQ]), ALU.mult)
                    last.then_inc(S["src_ready"], 1)

            chain[0] = 0
            dve.wait_ge(S["lg_copied"], NC)

            def step_of(ins):
                chain[0] += 1
                ins.then_inc(S["route"], 1)
                dve.wait_ge(S["route"], chain[0])
            step_of(dve.tensor_copy(lg, lg_bank[:, 0:NT * NEXP].rearrange("p (t e) -> p t e", t=NT)))
            shape = [P, NT, NEXP, NEXP]
            mine = lg.unsqueeze(3).broadcast_to(shape)
            other = lg.unsqueeze(2).broadcast_to(shape)
            g4 = big1.rearrange("p (t e j) -> p t e j", t=NT, e=NEXP)
            q4 = big2.rearrange("p (t e j) -> p t e j", t=NT, e=NEXP)
            tri4 = tri_t.rearrange("p (e j) -> p e j", e=NEXP).unsqueeze(1).broadcast_to(shape)
            dve.tensor_tensor(g4, other, mine, ALU.is_gt)
            step_of(dve.tensor_tensor(q4, other, mine, ALU.is_equal))
            step_of(dve.tensor_tensor(q4, q4, tri4, ALU.mult))
            step_of(dve.tensor_tensor(g4, g4, q4, ALU.add))
            dve.reduce_sum(rk, g4, X)
            step_of(dve.reduce_max(l1, lg, X))
            step_of(dve.tensor_tensor(le, lg, l1.unsqueeze(2).broadcast_to([P, NT, NEXP]), ALU.subtract))
            dve.wait_ge(S["route_exp"], 1)
            step_of(dve.scalar_tensor_tensor(out=rk, in0=rk, scalar=2.0, in1=le, op0=ALU.is_lt, op1=ALU.mult))
            step_of(dve.reduce_sum(dn, rk, X))
            step_of(dve.reciprocal(di, dn))
            dve.tensor_tensor(gates, rk.unsqueeze(3).broadcast_to([P, NT, NEXP, RANK]),
                              di.unsqueeze(2).unsqueeze(3).broadcast_to([P, NT, NEXP, RANK]), ALU.mult).then_inc(S["route_ready"], 1)
            for c in range(NC):
                dve.wait_ge(S["wexp_copied"], c + 1)
                dve.wait_ge(S["lora_done"], c + 1)
                dve.scalar_tensor_tensor(out=hw[:, CH * c:CH * (c + 1)], in0=pj[c % 2][:, :], scalar=2.0, in1=wx,
                                         op0=ALU.mult, op1=ALU.mult).then_inc(S["lora_ready"], 1)
            dve.wait_ge(S["ffn_in"], 64)
            for n in range(2 * NT):
                dst = y[:, n // 2, 512 * (n % 2):512 * (n % 2) + 512]
                dve.wait_ge(S["base_done"], n + 1)
                dve.tensor_tensor(dst, base_bank[n % 4][:, :], dst, ALU.add).then_inc(S["base_added"], 1)
                dve.wait_ge(S["base_added"], n + 1)
                dve.tensor_tensor(dst, dst, bb_t[:, 512 * (n % 2):512 * (n % 2) + 512], ALU.add).then_inc(S["result"], 1)

        @block.scalar
        def _(act):
            def piece_dst(z):
                if z < QKV_PIECES:
                    return w_qkv[:, z // 2, 0, 4 * (z % 2):4 * (z % 2) + 4, :].rearrange("p k n -> p (k n)")
                return w_out[:, (z - QKV_PIECES) // 2, 0, 512 * (z % 2):512 * (z % 2) + 512]

            def dequant_hi(g, z):
                scale = UNIT_SCALE[UNITS[z // 2]] if z < QKV_PIECES else col(S4 + 3)
                act.wait_ge(S["dq_scaled"], PIECES * g + z + 1)
                act.activation(piece_dst(z), w32[:, z % 2, :], ACT.Copy, scale=scale).then_inc(S["dq_hi"], 1)

            act.wait_ge(S["w_scales_ready"], 1)
            for z in range(QKV_PIECES):
                dequant_hi(0, z)
            act.wait_ge(S["h_scale_ready"], 1)
            for c in range(NC):
                for k in range(KT):
                    n = c * KT + k
                    act.wait_ge(S["cond_done"], n + 1)
                    act.activation(hid[:, 0, k, CH * c:CH * (c + 1)], cond_bank(n)[:, :], ACT.Copy,
                                   scale=col(SH)).then_inc(S["cond_hi"], 1)

            def rope_hi(p4, j):
                g, c = p4
                m = 5 * NC * g + (5 * c + roped_index(j))
                a = ra[:, roped_index(j) % 2, :].rearrange("p (b s) -> p b s", b=CB)
                u = UNITS[j]
                dst = kb[:, 0, :].rearrange("p (b s) -> p b s", b=CB) if u == "k" else qb[:, u // 2, 0, :, u % 2, :]
                act.wait_ge(S["rope_sum"], m + 1)
                act.wait_ge(S["scores_done"], 2 * NC * g + 2 * c + 2)
                act.activation(dst, a, ACT.Copy).then_inc(S["rope_hi"], 1)

            def v_hi(p4):
                g, c = p4
                act.wait_ge(S["proj_done"], NU * NC * g + (NU * c + V_AT + 1))
                act.wait_ge(S["pv_done"], 2 * NC * g + 2 * c + 2)
                act.activation(vb[:, 0, :, :].rearrange("p t d -> p (t d)"), pj[V_AT % 2][:, :], ACT.Copy,
                               scale=QKV_DOWN).then_inc(S["v_hi"], 1)

            def exps(g, c, h):
                act.wait_ge(S["shifted"], 2 * NC * g + (2 * c + h + 1))
                act.activation(sm[:, h, :, :], sm[:, h, :, :], ACT.Exp).then_inc(S["exps"], 1)

            def prob_hi(g, c, h):
                r = 2 * NC * g + (2 * c + h)
                act.wait_ge(S["probs"], r + 1)
                act.wait_ge(S["tp_done"], r + 2)
                act.activation(pp[:, 0, :], sm[:, h, :, :].rearrange("p b s -> p (b s)"), ACT.Copy).then_inc(S["probs_hi"], 1)

            def ctx_hi(g, c, h):
                r = 2 * NC * g + (2 * c + h)
                act.wait_ge(S["pv_done"], r + 1 + 2)
                act.wait_ge(S["o_done"], YT * NC * g + YT * c + YT)
                for e in range(2):
                    act.activation(ctx_dst(h, e, 0), ctx_src(e), ACT.Copy, scale=1.0 / P_UP).then_inc(S["ctx_hi"], 1)

            def step(g, c, ahead, extra):
                exps(g, c, 0)
                exps(g, c, 1)
                prob_hi(g, c, 0)
                if ahead:
                    rope_hi(ahead, 0)
                    extra(0)
                    rope_hi(ahead, 1)
                prob_hi(g, c, 1)
                if ahead:
                    extra(1)
                    rope_hi(ahead, 2)
                ctx_hi(g, c, 0)
                if ahead:
                    extra(2)
                    rope_hi(ahead, 3)
                ctx_hi(g, c, 1)
                if ahead:
                    extra(3)
                    v_hi(ahead)
                    extra(4)
                    rope_hi(ahead, 5)
                    extra(5)

            def group(g, last=False):
                def wo(j):
                    if j < REP:
                        if j == 0:
                            act.wait_ge(S["o_done"], YT * NC * g + YT)
                        dequant_hi(g, QKV_PIECES + 2 * j)
                        dequant_hi(g, QKV_PIECES + 2 * j + 1)

                def nxt(j):
                    act.wait_ge(S["proj_done"], NU * NC * g + (NU * (NC - 1) + j + 1))
                    dequant_hi(g + 1, 2 * j)
                    dequant_hi(g + 1, 2 * j + 1)
                for c in range(NC):
                    ahead = (g, c + 1) if c + 1 < NC else (None if last else (g + 1, 0))
                    extra = wo if c == 0 else nxt if (c == 2 and not last) else (lambda j: None)
                    step(g, c, ahead, extra)

            for j in range(NU):
                if j == V_AT:
                    v_hi((0, 0))
                else:
                    rope_hi((0, 0), j)
            with act.Fori(0, NKV - 1) as g:
                group(g)
            group(NKV - 1, last=True)

            act.wait_ge(S["bias_ready"], 1)
            for i in range(NT):
                if i >= 2:
                    act.wait_ge(S["src_done"], 2 * (i - 1))
                for e in range(2):
                    for th in range(2):
                        act.wait_ge(S["hid_done"], 4 * i + 2 * e + th + 1)
                        act.activation(h2[i % 2][:, e, 512 * th:512 * th + 512], h_bank[e][th][:, :], ACT.Gelu,
                                       bias=bias_t[:, 2 * i + e:2 * i + e + 1]).then_inc(S["hid_ready"], 1)
            for c in range(NC):
                act.wait_ge(S["lgt_done"], c + 1)
                if c:
                    act.wait_ge(S["lg_copied"], c)
                act.activation(lgt[0:NEXP, :], ex[0:NEXP, :], ACT.Copy).then_inc(S["lgt_copied"], 1)
            act.wait_ge(S["route"], 6)
            act.activation(le, le, ACT.Exp).then_inc(S["route_exp"], 1)
            for c in range(NC):
                act.wait_ge(S["wexp_done"], c + 1)
                if c:
                    act.wait_ge(S["lora_ready"], c)
                act.activation(wx, sa[:, :], ACT.Copy).then_inc(S["wexp_copied"], 1)

        @block.tensor
        def _(pe):
            mm = nc.tensor.matmul
            pe.wait_ge(S["x_in"], 16 * NC)
            pe.wait_ge(S["wc_in"], 16 * B)
            for c in range(NC):
                for k in range(KT):
                    n = c * KT + k
                    if n >= 4:
                        pe.wait_ge(S["cond_split"], n - 3)
                    for i in range(CT):
                        last = mm(cond_bank(n)[:, P * i:P * (i + 1)], y[:, CT * c + i, P * k:P * (k + 1)],
                                  wc[:, CT * c + i, :], start=True, stop=True)
                    last.then_inc(S["cond_done"], 1)

            PARTS = ((0, 0), (0, 1), (1, 0))

            def project(p4, j):
                g, c = p4
                n = NU * NC * g + (NU * c + j)
                pe.wait_ge(S["w_ready"], PIECES * g + 2 * (j + 1))
                if not isinstance(g, int) or NU * (NC * g + c) + j >= 2:
                    pe.wait_ge(S["proj_read"], n - 1)
                bank = pj[j % 2]
                if UNITS[j] == "v":
                    for i in range(CT):
                        for k in range(KT):
                            for lw, lh in PARTS:
                                last = mm(bank[:, P * i:P * (i + 1)], hid[:, lw, k, CH * c + P * i:CH * c + P * (i + 1)],
                                          w_qkv[:, j, lh, k, :], start=(k == 0 and (lw, lh) == (0, 0)),
                                          stop=(k == KT - 1 and (lw, lh) == (1, 0)))
                else:
                    for k in range(KT):
                        for lw, lh in PARTS:
                            last = mm(bank[:, :], w_qkv[:, j, lw, k, :], hid[:, lh, k, CH * c:CH * (c + 1)],
                                      start=(k == 0 and (lw, lh) == (0, 0)), stop=(k == KT - 1 and (lw, lh) == (1, 0)))
                last.then_inc(S["proj_done"], 1)

            def scores(g, c, h):
                r = 2 * NC * g + (2 * c + h)
                pe.wait_ge(S["qk_ready"], 5 * NC * g + (5 * c + (3, 5)[h]))
                pe.wait_ge(S["y_added"], YT * NC * g + YT * c + (YT - 2, YT)[h])
                for b in range(CB):
                    for lq, lk in PARTS:
                        last = mm(score_bank[h][:, SEQ * b:SEQ * (b + 1)], qb[:, h, lq, b, :, :].rearrange("p h s -> p (h s)"),
                                  kb[:, lk, SEQ * b:SEQ * (b + 1)], start=(lq, lk) == (0, 0), stop=(lq, lk) == (1, 0))
                last.then_inc(S["scores_done"], 1)

            def transpose_probs(g, c, h):
                r = 2 * NC * g + (2 * c + h)
                pe.wait_ge(S["probs_split"], r + 1 + 2)
                pe.wait_ge(S["pt_copied"], r + 2)
                for part in range(2):
                    for j in range(CT):
                        last = nc.tensor.transpose(tp[:, part, j, :], pp[:, part, P * j:P * (j + 1)], id16[:, :])
                last.then_inc(S["tp_done"], 1)

            def weigh_values(g, c, h):
                r = 2 * NC * g + (2 * c + h)
                pe.wait_ge(S["proj_read"], NU * NC * g + (NU * c + V_AT + 1))
                pe.wait_ge(S["pt_copied"], r + 1 + 2)
                pe.wait_ge(S["ctx_split"], r + 2)
                for j in range(CT):
                    for lv, lp in PARTS:
                        for e in range(2):
                            rows = slice(SEQ * e, SEQ * (e + 1))
                            last = mm(ctx_columns(e, j), vb[rows, lv, j, :],
                                      pt[rows, lp, j, :].rearrange("k (h s) -> k h s", h=2),
                                      start=(lv, lp) == (0, 0), stop=(lv, lp) == (1, 0))
                last.then_inc(S["pv_done"], 1)

            def project_out(g, c):
                pe.wait_ge(S["ctx_split"], 2 * NC * g + (2 * c + 2 + 2))
                pe.wait_ge(S["w_ready"], PIECES * g + PIECES)
                for t in range(YT):
                    if t == 1:
                        pe.wait_ge(S["masked"], 2 * NC * g + (2 * c + 2))
                    if t == 0 or t >= 3:
                        pe.wait_ge(S["y_added"], YT * NC * g + (YT * c + YT + (t - 2 if t else -1)))
                    i, n0 = t // 2, 512 * (t % 2)
                    for h in range(REP):
                        for lc, lw in PARTS:
                            last = mm(out_bank[t % 3][:, :], cb[:, lc, h, P * i:P * (i + 1)], w_out[:, h, lw, n0:n0 + 512],
                                      start=(h == 0 and (lc, lw) == (0, 0)), stop=(h == REP - 1 and (lc, lw) == (1, 0)))
                    last.then_inc(S["o_done"], 1)

            def step(g, c, ahead):
                scores(g, c, 0)
                scores(g, c, 1)
                if ahead:
                    project(ahead, 0)
                    project(ahead, 1)
                transpose_probs(g, c, 0)
                if ahead:
                    project(ahead, 2)
                weigh_values(g, c, 0)
                transpose_probs(g, c, 1)
                if ahead:
                    project(ahead, 3)
                weigh_values(g, c, 1)
                if ahead:
                    project(ahead, 4)
                    project(ahead, 5)
                project_out(g, c)

            def group(g, last=False):
                for c in range(NC):
                    step(g, c, (g, c + 1) if c + 1 < NC else (None if last else (g + 1, 0)))

            pe.wait_ge(S["consts_in"], 64)
            pe.wait_ge(S["cond_split"], NC * KT)
            for j in range(NU):
                project((0, 0), j)
            with pe.Fori(0, NKV - 1) as g:
                group(g)
            group(NKV - 1, last=True)

            pe.wait_ge(S["onehot_made"], 1)
            pe.wait_ge(S["y_added"], YT + YT * NC * NKV)
            mm(ex[:, 0:B], bs_t, hot_t, start=True, stop=True).then_inc(S["bias_done"], 1)
            pe.wait_ge(S["wsess_masked"], 1)

            def hidden2(i):
                for e in range(2):
                    rows = slice(SEQ * e, SEQ * (e + 1))
                    for th in range(2):
                        if i:
                            pe.wait_ge(S["hid_ready"], 4 * (i - 1) + 2 * e + th + 1)
                        mm(h_bank[e][th][:, :], ws[rows, i, :], y[rows, i, 512 * th:512 * th + 512],
                           start=True, stop=True).then_inc(S["hid_done"], 1)

            def sources(i):
                pe.wait_ge(S["hid_ready"], 4 * (i + 1))
                for kh in range(2):
                    if i:
                        pe.wait_ge(S["src_biased"], 2 * (i - 1) + kh + 1)
                    for kk in range(4):
                        for e in range(2):
                            k = 4 * kh + kk
                            at = SEQ * (2 * kk + e)
                            last = mm(score_bank[kh][:, at:at + SEQ], h2[i % 2][:, e, P * k:P * (k + 1)], w2_t,
                                      start=True, stop=True)
                    last.then_inc(S["src_done"], 1)
            hidden2(0)
            for i in range(NT):
                if i + 1 < NT:
                    hidden2(i + 1)
                sources(i)

            pe.wait_ge(S["bias_ready"], 1)
            for c in range(NC):
                pe.wait_ge(S["src_ready"], 2 * CT * (c + 1))
                if c:
                    pe.wait_ge(S["lgt_copied"], c)
                for k in range(KT):
                    last = mm(ex[0:NEXP, :], wr_t[:, k, :], xf[:, k, CH * c:CH * (c + 1)], start=(k == 0), stop=(k == KT - 1))
                last.then_inc(S["lgt_done"], 1)
                pe.wait_ge(S["lgt_copied"], c + 1)
                for i in range(CT):
                    t = CT * c + i
                    last = mm(lg_bank[:, NEXP * t:NEXP * (t + 1)], lgt[0:NEXP, P * i:P * (i + 1)], id32[0:NEXP, 0:NEXP],
                              start=True, stop=True)
                last.then_inc(S["lg_copied"], 1)
            pe.wait_ge(S["ffn_in2"], 16)

            def lora_hidden(c):
                if c >= 2:
                    pe.wait_ge(S["lora_ready"], c - 1)
                for k in range(KT):
                    last = mm(pj[c % 2][:, :], at_t[:, k, :], xf[:, k, CH * c:CH * (c + 1)], start=(k == 0), stop=(k == KT - 1))
                last.then_inc(S["lora_done"], 1)
            lora_hidden(0)
            lora_hidden(1)
            pe.wait_ge(S["route_ready"], 1)
            for c in range(NC):
                if c >= 2:
                    lora_hidden(c)
                if c:
                    pe.wait_ge(S["wexp_copied"], c)
                for i in range(CT):
                    last = mm(sa[:, P * i:P * (i + 1)], gates[:, CT * c + i, :, :].rearrange("p e r -> p (e r)"), id32, start=True, stop=True)
                last.then_inc(S["wexp_done"], 1)
            pe.wait_ge(S["ffn_in"], 64)
            pe.wait_ge(S["lora_ready"], NC)
            for n in range(2 * NT):
                t, n0 = n // 2, 512 * (n % 2)
                if n >= 4:
                    pe.wait_ge(S["base_added"], n - 3)
                bank = base_bank[n % 4]
                for k in range(KT):
                    mm(bank[:, :], xf[:, k, P * t:P * (t + 1)], wb[:, k, n0:n0 + 512], start=(k == 0), stop=False)
                mm(bank[:, :], hw[:, P * t:P * (t + 1)], bc_t[:, n0:n0 + 512], start=False, stop=True).then_inc(S["base_done"], 1)


def kernel(x, itok_B_0_15, itok_B_0_7, itok_B_2182_4065, _lenS, L0_cond_weights, L0_attn_scales_q,
           L0_attn_scales_k, L0_attn_scales_v, L0_attn_scales_o, L0_attn_qw_q, L0_attn_qw_k, L0_attn_qw_v,
           L0_attn_qw_o, L0_cond2_W_sess, L0_cond2_b_sess, L0_cond2_W2, L0_cond2_b2, L0_ffn_W_base,
           L0_ffn_b_base, L0_ffn_W_router, L0_ffn_A, L0_ffn_B):
    import numpy as np
    import concourse.bacc as bacc
    from concourse.bass_utils import run_bass_kernel_spmd

    def lay(a):
        return np.ascontiguousarray(np.asarray(a))

    f4 = np.float32
    inv_freq = (f4(1.0) / np.power(f4(10000.0), np.arange(0, HD, 2, dtype=f4) / f4(HD))).astype(f4)
    angle = (np.arange(SEQ, dtype=f4)[None, :] * inv_freq[:, None]).astype(f4)
    cos = np.concatenate([np.cos(angle)] * 2, 0).astype(f4) * f4(QKV_DOWN)
    sin = np.concatenate([np.sin(angle), -np.sin(angle)], 0).astype(f4) * f4(QKV_DOWN)
    pos = np.arange(P)
    mask = np.where(pos[:, None] % SEQ >= np.arange(SEQ)[None, :], 0.0, -3.0e38).astype(f4)
    row = (pos % SEQ)[:, None].astype(f4)
    arrays = {
        "x_d": lay(x).reshape(TOK, H),
        "cond_d": lay(itok_B_0_15).reshape(1, B),
        "ids_d": lay(np.broadcast_to(np.asarray(itok_B_0_7), (NEXP, B))),
        "seq_d": lay(np.broadcast_to(np.asarray(itok_B_2182_4065), (P, B))),
        "len_d": lay(np.repeat(np.asarray(_lenS).reshape(NT, 2).T, SEQ, axis=0)),
        "cw_d": lay(L0_cond_weights),
        "sq_d": lay(L0_attn_scales_q), "sk_d": lay(L0_attn_scales_k), "sv_d": lay(L0_attn_scales_v),
        "so_d": lay(L0_attn_scales_o),
        "qq_d": lay(L0_attn_qw_q), "qk_d": lay(L0_attn_qw_k), "qv_d": lay(L0_attn_qw_v), "qo_d": lay(L0_attn_qw_o),
        "wse_d": lay(L0_cond2_W_sess), "bse_d": lay(L0_cond2_b_sess), "w2_d": lay(L0_cond2_W2), "b2_d": lay(L0_cond2_b2),
        "wb_d": lay(np.asarray(L0_ffn_W_base).T), "bb_d": lay(L0_ffn_b_base),
        "wr_d": lay(np.asarray(L0_ffn_W_router).T),
        "a_d": lay(np.asarray(L0_ffn_A).reshape(NEXP * RANK, H).T),
        "bcat_d": lay(np.asarray(L0_ffn_B).transpose(0, 2, 1).reshape(NEXP * RANK, H)),
        "cos_d": cos, "sin_d": sin, "mask_d": mask, "id16_d": np.eye(P, dtype=np.float16),
        "id32_d": np.eye(P, dtype=f4), "row_d": row,
        "t_d": (pos[:, None] + P * np.arange(KT)[None, :]).astype(f4),
        "tri_d": lay(np.broadcast_to(np.tril(np.ones((NEXP, NEXP), f4), -1).reshape(1, -1), (P, NEXP * NEXP))),
    }
    nc = bacc.Bacc("TRN2", target_bir_lowering=False, num_devices=1, dynamic_dma_scratch_size=1024)
    args = [nc.dram_tensor(n, a.shape, mybir.dt.from_np(a.dtype), kind="ExternalInput").ap() for n, a in arrays.items()]
    out = nc.dram_tensor("out_d", (TOK, H), mybir.dt.float32, kind="ExternalOutput").ap()
    build(nc, *args, out)
    result = run_bass_kernel_spmd(nc, [arrays], core_ids=[0])
    return result.results[0]["out_d"].reshape(B, SEQ, H)
```

```python
import math
from contextlib import ExitStack

import concourse.bass as bass
from concourse import mybir

B, SEQ, H = 32, 64, 1024
TOK = B * SEQ
HD, NH, NKV = 128, 32, 8
REP = NH // NKV
HID, NEXP, RANK = 128, 8, 16
P = 128
KT = H // P
CH = 512
NC = TOK // CH
CB = CH // SEQ
CT = CH // P
NT = TOK // P
UNITS = ("k", 0, 1, 2, "v", 3)
NU = len(UNITS)
V_AT = UNITS.index("v")
ROPED = [u for u in UNITS if u != "v"]
WO_PIECES = 2 * REP
QKV_PIECES = 2 * NU
PIECES = WO_PIECES + QKV_PIECES
YT = 2 * CT

W_BITS = 11
H_BITS = 14
QKV_DOWN = 2.0 ** -26
P_UP = 2.0 ** 14
TINY = 2.0 ** -100
EXPONENT = 0x7F800000
WB_STATS = KT
WB_PIECES = 2 * KT
A_PIECES = 2


def build(nc, x, cond_rep, ids_rep, seq_rep, len_rep, cond_w, s_q, s_k, s_v, s_o, q_q, q_k, q_v, q_o,
          w_sess, b_sess, w2, b2, w_base_t, b_base, w_router_t, a_t, b_cat,
          rope_cos, rope_sin, neg_mask, ident16, ident32, row_of, t_of, tri, out):
    f32, f16, i32 = mybir.dt.float32, mybir.dt.float16, mybir.dt.int32
    ALU, ACT, X = mybir.AluOpType, mybir.ActivationFunctionType, mybir.AxisListType.X
    MAX = bass.bass_isa.ReduceOp.max
    ds = bass.ds

    ctx = ExitStack()
    with ctx:
        def sb(name, shape, dt):
            return ctx.enter_context(nc.sbuf_tensor(name, shape, dt))

        def pb(name, shape=(P, CH), dt=f32):
            return ctx.enter_context(nc.psum_tensor(name, list(shape), dt))

        def sem(name):
            return ctx.enter_context(nc.semaphore(name))

        y = sb("y", [P, NT, H], f32)
        hid = sb("hid", [P, 2, KT, TOK], f16)
        wts = sb("wts", [P, 2 * KT * P * NU + 2 * REP * H], f16)
        w_qkv = wts[:, 0:2 * KT * P * NU].rearrange("p (u l k n) -> p u l k n", u=NU, l=2, k=KT)
        w_out = wts[:, 2 * KT * P * NU:].rearrange("p (h l n) -> p h l n", h=REP, l=2)
        work = sb("work", [P, 5632], f32)
        stage = work[:, 0:2048].rearrange("p (s w n) -> p s w n", s=2, w=2)
        w32 = work[:, 2048:3072].rearrange("p (s n) -> p s n", s=2)
        ra = work[:, 3072:4096].rearrange("p (s n) -> p s n", s=2)
        rb = work[:, 4096:4608]
        sm = work[:, 4608:5632].rearrange("p (h b s) -> p h b s", h=2, b=CB)
        qb = sb("qb", [P, 2, 2, CB, 2, SEQ], f16)
        kb = sb("kb", [P, 2, CH], f16)
        vb = sb("vb", [P, 2, CT, HD], f16)
        pp = sb("pp", [P, 2, CH], f16)
        pt = sb("pt", [P, 2, CT, P], f16)
        cb = sb("cb", [P, 2, REP, CH], f16)
        rmax = sb("rmax", [P, 2, CB], f32)
        rsum = sb("rsum", [P, 2, CB], f32)
        rinv = sb("rinv", [P, 2, CB], f32)
        cos_t = sb("cos_t", [P, SEQ], f32)
        sin_t = sb("sin_t", [P, SEQ], f32)
        mask_t = sb("mask_t", [P, SEQ], f32)
        id16 = sb("id16", [P, P], f16)
        small = sb("small", [P, 512], f32)
        misc = sb("misc", [P, 640], f32)
        stat = sb("stat", [P, 32], f32)
        top = sb("top", [P, 32], f32)
        x1max = sb("x1max", [P, NC * YT], f32)
        sc = sb("sc", [P, 80], f32)
        bits = sb("bits", [P, 16], i32)
        cidx = sb("cidx", [1, B], i32)
        sidx = sb("sidx", [1, B], i32)

        raw = hid[:, :, :, :].bitcast(f32).rearrange("p l k t -> p (l k t)")
        wc = cb[:, :, :, :].bitcast(f32).rearrange("p a h c -> p (a h c)").rearrange("p (i d) -> p i d", i=NT)

        pj = [pb("pj0"), pb("pj1")]
        sa, sbk, ex = pb("sa"), pb("sbk"), pb("ex")
        tp = pb("tp", (P, 2, CT, P), f16)
        cx = [pb("cx0"), pb("cx1")]
        score_bank = [sbk, sa]
        out_bank = [ex, sa, sbk, pj[0]]

        early_bank = [ex, pj[0], pj[1], cx[0]]

        names = """consts_in idx_in stats_in stats2_in wc_zero
                   stat_w stat_x stat_c2 stat_wb stat_x1 top_w top_x top_c2 top_wb top_x1
                   scal w_scales_ready h_scale_ready scales_ready
                   cond_done cond_hi cond_split
                   dq_scaled dq_hi w_ready
                   proj_done proj_read rope_sum rope_hi qk_ready v_hi
                   scores_done masked rowmaxed shifted exps summed inverted probs probs_hi probs_split
                   tp_done pt_copied pv_done ctx_hi ctx_split o_done y_added wb_read
                   wsess_in masks_made wsess_masked onehot_made bias_done bias_ready c2_in small_split small_hi
                   h2_scale_ready wb_scale_ready x1_maxed hid_done gelu_done h2_hi h2_split src_done src_biased src_ready
                   wf_hi wf_split bcat_in bb_in xf_hi xf_split
                   lg_done route route_exp route_ready lora_done lora_copied wexp_done lora_ready
                   base_done base_added result stored"""
        S = {n: sem(n) for n in names.split()}
        staged = [sem("staged0"), sem("staged1")]
        x_in = [sem(f"x_in{c}") for c in range(NC)]
        wc_in = [sem(f"wc_in{c}") for c in range(NC)]
        wb_in = [sem("wb_in0"), sem("wb_in1")]
        wf_in = [sem("wf_in0"), sem("wf_in1")]

        block = ctx.enter_context(nc.Block())

        arena = wts[:, :].bitcast(f32)
        wb16 = wts[:, 0:2 * KT * H].rearrange("p (l k n) -> p l k n", l=2, k=KT)
        a16 = wts[:, 2 * KT * H:2 * KT * H + 2 * KT * P].rearrange("p (l k n) -> p l k n", l=2, k=KT)
        bc_t = arena[:, 9216:10240]
        hw = work[:, 2048:4096]
        ws = hw.rearrange("p (i d) -> p i d", i=NT)
        cb32 = cb[:, :, :, :].bitcast(f32).rearrange("p a h c -> p (a h c)")
        g32 = cb32.rearrange("p (e t) -> p e t", e=2)
        gates = cb32.rearrange("p (t e r) -> p t e r", t=NT, e=NEXP)
        big1, big2 = cb32[:, 0:1024], cb32[:, 1024:2048]
        h2 = [work[:, 0:2048].bitcast(f16).rearrange("p (l e t) -> p l e t", l=2, e=2),
              qb[:, :, :, :, :, :].rearrange("p a l b h s -> p (a l b h s)").rearrange("p (l e t) -> p l e t", l=2, e=2)]
        wstage = sm.rearrange("p h b s -> p h (b s)")
        vm = rb
        lg = vm[:, 0:128].rearrange("p (t e) -> p t e", t=NT)
        le = vm[:, 128:256].rearrange("p (t e) -> p t e", t=NT)
        rk = vm[:, 256:384].rearrange("p (t e) -> p t e", t=NT)
        l1 = vm[:, 384:400]
        dn = vm[:, 400:416]
        di = vm[:, 416:432]
        bb = [kb[:, :, :].bitcast(f32).rearrange("p l t -> p (l t)"),
              vb[:, :, :, :].bitcast(f32).rearrange("p l t d -> p (l t d)")]
        src_tmp = [[pp[:, :, :].bitcast(f32).rearrange("p l t -> p (l t)"),
                    pt[:, :, :, :].bitcast(f32).rearrange("p l t n -> p (l t n)")], bb]

        def xpart(c, part):
            return hid[:, part, :, CH * c:CH * (c + 1)]

        def source_dst(i, kh, part):
            return hid[:, part, 4 * kh:4 * kh + 4, P * i:P * (i + 1)]
        id32 = small[:, 0:128]
        w2_t = small[:, 128:192]
        b2_t = small[:, 192:256]
        wr_t = small[:, 256:320].rearrange("p (k e) -> p k e", k=KT)
        tri_t = small[:, 320:384]
        row_t = small[:, 384:385]
        tt_t = small[:, 385:393]
        len_t = small[:, 393:409].bitcast(i32)
        seq_t = small[:, 409:441].bitcast(i32)
        ids_t = small[0:NEXP, 441:473].bitcast(i32)
        bias_t = small[:, 473:505]
        bs_t = misc[0:NEXP, 0:128]
        hot_t = misc[0:NEXP, 128:160]
        cm_t = misc[:, 160:176]
        tm_t = misc[:, 192:448].rearrange("p (k b) -> p k b", k=KT)
        w2h = misc[:, 448:512].bitcast(f16).rearrange("p (l s) -> p l s", l=2)
        wrh = misc[:, 512:576].bitcast(f16).rearrange("p (l k e) -> p l k e", l=2, k=KT)

        SH, S4, IS4, ISH, A, QS, KS, F_SCORE, AV, F_OUT, M = 0, 4, 8, 12, 16, 20, 24, 28, 32, 36, 40
        SC2, ISC2 = 44, 48
        SH2, ISH2, SX, ISX, F_SRC, F_LG, F_LORA, F_BASE, BOUND, BOUND_X = 52, 53, 54, 55, 56, 57, 58, 59, 60, 64
        T_X, T_CW, T_S4, T_A, T_R, T_W2, T_WB, T_WS, T_BS, T_X1, T_B2, T_WBS = 0, 4, 5, 9, 10, 11, 12, 13, 14, 15, 16, 17

        def col(n, k=1):
            return sc[:, n:n + k]
        UNIT_SCALE = {u: col(S4 + {"k": 1, "v": 2}.get(u, 0)) for u in UNITS}

        def roped_index(j):
            return sum(1 for u in UNITS[:j] if u != "v")

        lg_bank = tp[:, :, :, :].bitcast(f32).rearrange("p l t n -> p (l t n)")
        base_bank = [cx[0], cx[1], sa, ex]
        gate_bank = [sbk, pj[0]]
        h_bank = [[cx[0], cx[1]], [pj[0], pj[1]]]

        def wf_dst(z, part):
            if z < A_PIECES:
                return a16[:, part, 4 * z:4 * (z + 1), :].rearrange("p k n -> p (k n)")
            z -= A_PIECES
            return wb16[:, part, z // 2, 512 * (z % 2):512 * (z % 2) + 512]

        def wf_scale(z):
            return col(SC2) if z < A_PIECES else col(SC2 + 3)

        def w_out_piece(n, part):
            half, h = n // REP, n % REP
            return w_out[:, h, part, 512 * half:512 * half + 512]

        def out_tile(t):
            return t % CT, t // CT

        def small_parts():
            return ((lambda part: w2h[:, part, :], w2_t, col(SC2 + 2)),
                    (lambda part: wrh[:, part, :, :].rearrange("p k e -> p (k e)"), small[:, 256:320], col(SC2 + 1)))

        cond_banks = [pj[0], pj[1], ex, cx[0], cx[1], sa, sbk]

        def cond_bank(n):
            return cond_banks[n % len(cond_banks)]

        def ctx_src(e):
            return cx[e][:, :].rearrange("p (m s) -> p m s", s=SEQ)

        def ctx_columns(e, j):
            return cx[e][:, :].rearrange("p (h j s) -> p j h s", h=2, s=SEQ)[:, j]

        def ctx_dst(h, e, part):
            return cb[:, part, 2 * h:2 * h + 2, :].rearrange("p h (j e s) -> p e (h j) s", e=2, s=SEQ)[:, e]

        ACT_CHUNKS = 2

        def load_cond(queue, i, odd, c):
            s = queue.value_load(cidx[0:1, ds(i * 2 + odd, 1)], min_val=0, max_val=15)
            queue.dma_start(wc[SEQ * odd:SEQ * (odd + 1), ds(i, 1), SEQ * odd:SEQ * (odd + 1)],
                            cond_w[ds(s, 1), :, :].rearrange("a c d -> c a d")).then_inc(wc_in[c], 16)

        @block.sync
        def _(sp):
            sp.sem_inc(S["scores_done"], 2)
            sp.sem_inc(S["tp_done"], 2)
            sp.sem_inc(S["probs_split"], 2)
            sp.sem_inc(S["pv_done"], 2)
            sp.sem_inc(S["pt_copied"], 2)
            sp.sem_inc(S["ctx_split"], 2)
            sp.sem_inc(S["o_done"], YT)
            sp.sem_inc(S["y_added"], YT)
            at = [0]

            def load_stats(src, n, name, place=raw):
                sp.dma_start(place[:, at[0]:at[0] + n], src).then_inc(S[name], 16)
                at[0] += n
            load_stats(cond_w.rearrange("s (q c) d -> (s q) (c d)", q=8), 512, "stats_in")
            load_stats(s_q.rearrange("a (b n) -> (a b) n", b=16), 256, "stats_in")
            load_stats(s_k.rearrange("a (b n) -> (a b) n", b=16), 64, "stats_in")
            load_stats(s_v.rearrange("a (b n) -> (a b) n", b=16), 64, "stats_in")
            load_stats(s_o.rearrange("a (b n) -> (a b) n", b=4), 256, "stats_in")
            sp.dma_start(cidx[:, :], cond_rep).then_inc(S["idx_in"], 16)
            sp.dma_start(sidx[:, :], ids_rep[0:1, :]).then_inc(S["idx_in"], 16)

            def load_x(c):
                sp.dma_start(y[:, CT * c:CT * (c + 1), :],
                             x[CH * c:CH * (c + 1), :].rearrange("(i p) n -> p i n", p=P)).then_inc(x_in[c], 16)
            load_x(0)

            def load_piece(g, z):
                slot = z % 2
                if isinstance(g, int):
                    if PIECES * g + z >= 2:
                        sp.wait_ge(S["dq_scaled"], PIECES * g + z - 1)
                else:
                    sp.wait_ge(S["dq_scaled"], g * PIECES + (z - 1))
                if z < QKV_PIECES:
                    u, half = UNITS[z // 2], z % 2
                    qw, s = {"k": (q_k, s_k), "v": (q_v, s_v)}.get(u, (q_q, s_q))
                    col = g * HD if u in ("k", "v") else g * (REP * HD) + u * HD
                    rows = 4 * P * half
                    src = qw[rows:rows + 4 * P, ds(col, HD)].rearrange("(k p) n -> p k n", p=P)
                    scale = s[4 * half:4 * half + 4, ds(col, HD)].partition_broadcast(P)
                    shape = "p (k n) -> p k n"
                    sp.dma_start(stage[:, slot, 0, :].bitcast(i32).rearrange(shape, k=4), src).then_inc(staged[slot], 16)
                    sp.dma_start(stage[:, slot, 1, :].rearrange(shape, k=4), scale).then_inc(staged[slot], 16)
                else:
                    half, h = (z - QKV_PIECES) // REP, (z - QKV_PIECES) % REP
                    src = q_o[ds(g * (REP * HD) + h * HD, HD), half * 512:half * 512 + 512]
                    scale = s_o[ds(g * REP + h, 1), half * 512:half * 512 + 512].rearrange("a n -> (a n)").partition_broadcast(P)
                    sp.dma_start(stage[:, slot, 0, :].bitcast(i32), src).then_inc(staged[slot], 16)
                    sp.dma_start(stage[:, slot, 1, :], scale).then_inc(staged[slot], 16)

            sp.wait_ge(S["idx_in"], 32)
            sp.wait_ge(S["wc_zero"], 1)
            for c in range(NC):
                with sp.Fori(CT * c, CT * (c + 1)) as i:
                    load_cond(sp, i, 0, c)
                    if c >= ACT_CHUNKS:
                        load_cond(sp, i, 1, c)
                if c + 1 < NC:
                    load_x(c + 1)
                if c == 0:
                    load_piece(0, 0)
                    load_piece(0, 1)
            for dst, src in ((cos_t, rope_cos), (sin_t, rope_sin), (mask_t, neg_mask), (id16, ident16)):
                sp.dma_start(dst[:, :], src).then_inc(S["consts_in"], 16)
            for z in range(2, 2 * NU):
                load_piece(0, z)
            for dst, src in ((b2_t, b2.partition_broadcast(P)), (w2_t, w2), (bs_t, b_sess), (ids_t, ids_rep),
                             (len_t, len_rep), (seq_t, seq_rep), (row_t, row_of), (tt_t, t_of), (tri_t, tri),
                             (id32, ident32), (wr_t, w_router_t.rearrange("(k p) e -> p k e", p=P))):
                sp.dma_start(dst, src).then_inc(S["c2_in"], 16)
            for z in range(2 * NU, PIECES):
                load_piece(0, z)
            with sp.Fori(1, NKV) as g:
                for z in range(PIECES):
                    load_piece(g, z)

            sp.wait_ge(S["dq_scaled"], PIECES * NKV)
            for k in range(WB_STATS):
                if k >= 2:
                    sp.wait_ge(S["wb_read"], k - 1)
                sp.dma_start(work[:, H * (k % 2):H * (k % 2 + 1)], w_base_t[P * k:P * (k + 1), :]).then_inc(wb_in[k % 2], 16)
            sp.wait_ge(S["wb_read"], WB_STATS)
            at[0] = 0
            load_stats(a_t.rearrange("(k p) n -> p k n", p=P), 1024, "stats2_in", work)
            load_stats(w_router_t.rearrange("(k p) e -> p k e", p=P), 64, "stats2_in", work)
            load_stats(w2, 64, "stats2_in", work)
            load_stats(w_sess.rearrange("s (q c) d -> (s q) (c d)", q=16), 512, "stats2_in", work)
            load_stats(b_sess.rearrange("s (q d) -> (s q) d", q=16), 8, "stats2_in", work)
            sp.wait_ge(S["qk_ready"], len(ROPED) * NKV * NC)
            with sp.Fori(0, NT) as i:
                for odd in range(2):
                    s = sp.value_load(sidx[0:1, ds(i * 2 + odd, 1)], min_val=0, max_val=7)
                    sp.dma_start(ws[SEQ * odd:SEQ * (odd + 1), ds(i, 1), :],
                                 w_sess[ds(s, 1), :, :].rearrange("a c d -> c a d")).then_inc(S["wsess_in"], 16)
            sp.wait_ge(S["probs_split"], 2 + 2 * NKV * NC)
            for z in range(WB_PIECES + A_PIECES):
                if z >= 2:
                    sp.wait_ge(S["wf_split"], z - 1)
                dst = wstage[:, z % 2, :]
                if z < A_PIECES:
                    dst = dst.rearrange("p (k n) -> p k n", k=4)
                    src = a_t[CH * z:CH * (z + 1), :].rearrange("(k p) n -> p k n", p=P)
                else:
                    k, n0 = (z - A_PIECES) // 2, 512 * (z % 2)
                    src = w_base_t[P * k:P * (k + 1), n0:n0 + 512]
                sp.dma_start(dst, src).then_inc(wf_in[z % 2], 16)
                if z == 1:
                    sp.wait_ge(S["o_done"], YT + YT * NKV * NC)
                    sp.dma_start(bc_t, b_cat).then_inc(S["bcat_in"], 16)
            sp.wait_ge(S["xf_split"], 2 * NT)
            for n in range(2):
                sp.dma_start(bb[n], b_base[512 * n:512 * (n + 1)].partition_broadcast(P)).then_inc(S["bb_in"], 16)
            for t in range(NT):
                sp.wait_ge(S["result"], 2 * (t + 1))
                sp.dma_start(out[P * t:P * (t + 1), :], y[:, t, :]).then_inc(S["stored"], 16)
            sp.wait_ge(S["stored"], 16 * NT)

        FIRST_PIECES = ((0,), (), (), (2, 4))
        LATE_PIECES = (6, 8, 10)

        @block.gpsimd
        def _(gp):
            gp.memset(wc, 0.0).then_inc(S["wc_zero"], 1)

            def over_partitions(ready, count, lo, hi, done):
                gp.wait_ge(S[ready], count)
                gp.partition_all_reduce(top[:, lo:hi], stat[:, lo:hi], P, MAX).then_inc(S[done], 1)
            over_partitions("stat_w", 1, T_CW, T_S4 + 4, "top_w")
            for c in range(NC):
                over_partitions("stat_x", c + 1, T_X + c, T_X + c + 1, "top_x")
            over_partitions("stat_wb", 1, T_WB, T_WB + 1, "top_wb")
            over_partitions("stat_c2", 1, T_A, T_W2 + 1, "top_c2")
            over_partitions("stat_c2", 1, T_WS, T_BS + 1, "top_c2")
            over_partitions("stat_x1", 1, T_X1, T_X1 + 1, "top_x1")
            for i in range(NT):
                for kh in range(2):
                    gp.wait_ge(S["src_biased"], 2 * i + kh + 1)
                    tmp = src_tmp[i % 2][kh].rearrange("p (k e s) -> p k e s", e=2, s=SEQ)
                    gp.tensor_tensor(tmp, tmp, tm_t[:, 4 * kh:4 * kh + 4, 2 * i:2 * i + 2].unsqueeze(3).broadcast_to([P, 4, 2, SEQ]),
                                     ALU.mult).then_inc(S["src_ready"], 1)

        @block.vector
        def _(dve):
            chain = [0]

            def link(ins):
                chain[0] += 1
                ins.then_inc(S["scal"], 1)
                dve.wait_ge(S["scal"], chain[0])

            def dequant_scale(g, z):
                slot = z % 2
                dve.wait_ge(staged[slot], 32 * (PIECES // 2) * g + 32 * (z // 2 + 1))
                if not isinstance(g, int) or PIECES * g + z >= 2:
                    dve.wait_ge(S["w_ready"], PIECES * g + (z - 1))
                dve.scalar_tensor_tensor(out=w32[:, slot, :], in0=stage[:, slot, 0, :].bitcast(i32), scalar=-8.0,
                                         in1=stage[:, slot, 1, :], op0=ALU.add, op1=ALU.mult).then_inc(S["dq_scaled"], 1)

            def piece_dst(z, part):
                if z < QKV_PIECES:
                    return w_qkv[:, z // 2, part, 4 * (z % 2):4 * (z % 2) + 4, :].rearrange("p k n -> p (k n)")
                return w_out_piece(z - QKV_PIECES, part)

            def dequant_split(g, z):
                scale = UNIT_SCALE[UNITS[z // 2]] if z < QKV_PIECES else col(S4 + 3)
                dve.wait_ge(S["dq_hi"], PIECES * g + z + 1)
                dve.scalar_tensor_tensor(out=piece_dst(z, 1), in0=w32[:, z % 2, :], scalar=scale,
                                         in1=piece_dst(z, 0), op0=ALU.mult, op1=ALU.subtract).then_inc(S["w_ready"], 1)

            def dequant(g, z):
                dequant_scale(g, z)
                dequant_scale(g, z + 1)
                dequant_split(g, z)
                dequant_split(g, z + 1)

            def absmax(to, src, axis=X):
                return dve.tensor_reduce(to, src, axis, ALU.max, apply_absolute_value=True)

            def pow2(scale, inverse, of, n, b, bits_up):
                link(dve.tensor_scalar_max(of, of, TINY))
                link(dve.tensor_single_scalar(bits[:, b:b + n], of.bitcast(i32), EXPONENT, ALU.bitwise_and))
                link(dve.tensor_scalar(col(scale, n).bitcast(i32), bits[:, b:b + n], -1.0, float((254 + bits_up) << 23), ALU.mult, ALU.add))
                return dve.tensor_scalar(col(inverse, n), bits[:, b:b + n].bitcast(f32), 2.0 ** -bits_up, None, ALU.mult)

            dve.wait_ge(S["stats_in"], 80)
            at = 0
            for n, size in ((T_CW, 512), (T_S4, 256), (T_S4 + 1, 64), (T_S4 + 2, 64), (T_S4 + 3, 256)):
                last = absmax(stat[:, n:n + 1], raw[:, at:at + size])
                at += size
            last.then_inc(S["stat_w"], 1)

            def chunk_max(c):
                dve.wait_ge(x_in[c], 16)
                absmax(stat[:, T_X + c:T_X + c + 1], y[:, CT * c:CT * (c + 1), :].rearrange("p i n -> p (i n)")).then_inc(S["stat_x"], 1)

            def chunk_scale(c):
                dve.wait_ge(S["top_x"], c + 1)
                m = col(BOUND + c)
                link(dve.scalar_tensor_tensor(out=m, in0=top[:, T_X + c:T_X + c + 1], scalar=float(SEQ),
                                              in1=top[:, T_CW:T_CW + 1], op0=ALU.mult, op1=ALU.mult))
                pow2(SH + c, ISH + c, m, 1, 4 + c, H_BITS).then_inc(S["h_scale_ready"], 1)
                dve.wait_ge(S["h_scale_ready"], c + 1)

            dve.wait_ge(S["top_w"], 1)
            link(dve.tensor_copy(col(M, 4), top[:, T_S4:T_S4 + 4]))
            pow2(S4, IS4, col(M, 4), 4, 0, W_BITS).then_inc(S["w_scales_ready"], 1)
            dve.wait_ge(S["w_scales_ready"], 1)
            chunk_max(0)
            chunk_scale(0)
            for c in range(NC):
                for k in range(KT):
                    n = c * KT + k
                    if k == (KT // 4 if c == 0 else 0) and c + 1 < NC:
                        chunk_max(c + 1)
                    dve.wait_ge(S["cond_hi"], n + 1)
                    t = slice(CH * c, CH * (c + 1))
                    dve.scalar_tensor_tensor(out=hid[:, 1, k, t], in0=cond_bank(n)[:, :], scalar=col(SH + c),
                                             in1=hid[:, 0, k, t], op0=ALU.mult, op1=ALU.subtract).then_inc(S["cond_split"], 1)
                if c + 1 < NC:
                    chunk_scale(c + 1)
                for z in FIRST_PIECES[c]:
                    dequant(0, z)
            def score_factors():
                link(dve.tensor_scalar(col(A, NC), col(ISH, NC), 1.0 / QKV_DOWN, None, ALU.mult))
                link(dve.tensor_scalar(col(QS, NC), col(A, NC), col(IS4), None, ALU.mult))
                link(dve.tensor_scalar(col(KS, NC), col(A, NC), col(IS4 + 1), HD ** -0.5, ALU.mult, ALU.mult))
                link(dve.tensor_tensor(col(F_SCORE, NC), col(QS, NC), col(KS, NC), ALU.mult))
                link(dve.tensor_scalar(col(AV, NC), col(A, NC), col(IS4 + 2), None, ALU.mult))
                link(dve.tensor_scalar(col(F_OUT, NC), col(AV, NC), col(IS4 + 3), None, ALU.mult))

            def small_stats():
                dve.reduce_max(stat[:, T_WB:T_WB + 1], stat[:, T_WBS:T_WBS + WB_STATS], X).then_inc(S["stat_wb"], 1)
                dve.wait_ge(S["c2_in"], 16 * 11)
                absmax(stat[:, T_B2:T_B2 + 1], b2_t)
                dve.wait_ge(S["stats2_in"], 80)
                at = 0
                for n, size in ((T_A, 1024), (T_R, 64), (T_W2, 64), (T_WS, 512), (T_BS, 8)):
                    last = absmax(stat[:, n:n + 1], work[:, at:at + size])
                    at += size
                last.then_inc(S["stat_c2"], 1)

            def small_scales():
                dve.wait_ge(S["top_wb"], 1)
                dve.wait_ge(S["top_c2"], 2)
                dve.tensor_copy(col(M + 3), top[:, T_WB:T_WB + 1])
                link(dve.tensor_copy(col(M, 3), top[:, T_A:T_A + 3]))
                pow2(SC2, ISC2, col(M, 4), 4, 8, H_BITS).then_inc(S["scales_ready"], 1)
                dve.wait_ge(S["scales_ready"], 1)

            def small_operands():
                for n, (dst, src, scale) in enumerate(small_parts()):
                    dve.wait_ge(S["small_hi"], n + 1)
                    dve.scalar_tensor_tensor(out=dst(1), in0=src, scalar=scale, in1=dst(0), op0=ALU.mult,
                                             op1=ALU.subtract).then_inc(S["small_split"], 1)
                dve.tensor_scalar(hot_t, ids_t, row_t[0:NEXP, :], None, ALU.is_equal).then_inc(S["onehot_made"], 1)
                dve.tensor_scalar(cm_t, len_t, row_t, None, ALU.is_gt)
                dve.tensor_tensor(tm_t, seq_t.unsqueeze(1).broadcast_to([P, KT, B]), tt_t.unsqueeze(2).broadcast_to([P, KT, B]),
                                  ALU.is_gt).then_inc(S["masks_made"], 1)

            def mask_sessions():
                dve.wait_ge(S["masks_made"], 1)
                dve.wait_ge(S["wsess_in"], 16 * B)
                dve.tensor_tensor(ws, ws, cm_t.unsqueeze(2).broadcast_to([P, NT, HID]), ALU.mult).then_inc(S["wsess_masked"], 1)

            def tables(t, b):
                return t[:, :].unsqueeze(1).broadcast_to([P, b, SEQ])

            def rope_write(idx, part):
                u = UNITS[idx]
                if u == "k":
                    return kb[:, part, :].rearrange("p (b s) -> p b s", b=CB)
                return qb[:, u // 2, part, :, u % 2, :]

            def rope(p4, j):
                g, c = p4
                n = NU * NC * g + (NU * c + j)
                m = 5 * NC * g + (5 * c + roped_index(j))
                bank = pj[j % 2]
                a = ra[:, roped_index(j) % 2, :].rearrange("p (b s) -> p b s", b=CB)
                b = rb[:, :].rearrange("p (b s) -> p b s", b=CB)
                src = bank[:, :].rearrange("p (b s) -> p b s", b=CB)
                dve.wait_ge(S["proj_done"], n + 1)
                if not isinstance(g, int) or m >= 2:
                    dve.wait_ge(S["qk_ready"], m - (1 if roped_index(j) else 0))
                dve.tensor_tensor(a, src, tables(cos_t, CB), ALU.mult)
                half = HD // 2
                if not isinstance(g, int) or m >= 1:
                    dve.wait_ge(S["rope_sum"], m)
                dve.tensor_tensor(b[0:half], src[half:HD], sin_t[half:HD, :].unsqueeze(1).broadcast_to([half, CB, SEQ]), ALU.mult)
                dve.tensor_tensor(b[half:HD], src[0:half], sin_t[0:half, :].unsqueeze(1).broadcast_to([half, CB, SEQ]),
                                  ALU.mult).then_inc(S["proj_read"], 1)
                dve.wait_ge(S["proj_read"], n + 1)
                dve.tensor_tensor(a, a, b, ALU.add).then_inc(S["rope_sum"], 1)

            def rope_split(p4, j):
                g, c = p4
                m = 5 * NC * g + (5 * c + roped_index(j))
                a = ra[:, roped_index(j) % 2, :].rearrange("p (b s) -> p b s", b=CB)
                dve.wait_ge(S["rope_hi"], m + 1)
                dve.tensor_tensor(rope_write(j, 1), a, rope_write(j, 0), ALU.subtract).then_inc(S["qk_ready"], 1)

            def v_split(p4):
                g, c = p4
                dve.wait_ge(S["v_hi"], NC * g + (c + 1))
                dve.scalar_tensor_tensor(out=vb[:, 1, :, :].rearrange("p t d -> p (t d)"), in0=pj[V_AT % 2][:, :], scalar=QKV_DOWN,
                                         in1=vb[:, 0, :, :].rearrange("p t d -> p (t d)"), op0=ALU.mult,
                                         op1=ALU.subtract).then_inc(S["proj_read"], 1)

            def soft_shift(g, c, h):
                r = 2 * NC * g + (2 * c + h)
                dve.wait_ge(S["scores_done"], r + 1 + 2)
                dve.wait_ge(S["probs_split"], r + 1)
                dve.scalar_tensor_tensor(out=sm[:, h, :, :], in0=score_bank[h][:, :].rearrange("p (b s) -> p b s", b=CB),
                                         scalar=col(F_SCORE + c), in1=tables(mask_t, CB), op0=ALU.mult,
                                         op1=ALU.add).then_inc(S["masked"], 1)
                dve.wait_ge(S["masked"], r + 1)
                dve.reduce_max(rmax[:, h, :], sm[:, h, :, :], X).then_inc(S["rowmaxed"], 1)
                dve.wait_ge(S["rowmaxed"], r + 1)
                dve.tensor_tensor(sm[:, h, :, :], sm[:, h, :, :], rmax[:, h, :].unsqueeze(2).broadcast_to([P, CB, SEQ]),
                                  ALU.subtract).then_inc(S["shifted"], 1)

            def soft_norm(g, c, h):
                r = 2 * NC * g + (2 * c + h)
                dve.wait_ge(S["exps"], r + 1)
                dve.reduce_sum(rsum[:, h, :], sm[:, h, :, :], X).then_inc(S["summed"], 1)
                dve.wait_ge(S["summed"], r + 1)
                dve.reciprocal(rinv[:, h, :], rsum[:, h, :]).then_inc(S["inverted"], 1)
                dve.wait_ge(S["inverted"], r + 1)
                dve.scalar_tensor_tensor(out=sm[:, h, :, :], in0=sm[:, h, :, :], scalar=P_UP,
                                         in1=rinv[:, h, :].unsqueeze(2).broadcast_to([P, CB, SEQ]), op0=ALU.mult,
                                         op1=ALU.mult).then_inc(S["probs"], 1)

            def prob_split(g, c, h):
                r = 2 * NC * g + (2 * c + h)
                dve.wait_ge(S["probs_hi"], r + 1)
                dve.tensor_tensor(pp[:, 1, :], sm[:, h, :, :].rearrange("p b s -> p (b s)"), pp[:, 0, :],
                                  ALU.subtract).then_inc(S["probs_split"], 1)

            def pt_copy(g, c, h):
                r = 2 * NC * g + (2 * c + h)
                dve.wait_ge(S["tp_done"], r + 1 + 2)
                dve.wait_ge(S["pv_done"], r + 2)
                dve.tensor_copy(pt[:, :, :, :].rearrange("p l t n -> p (l t n)"),
                                tp[:, :, :, :].rearrange("p l t n -> p (l t n)")).then_inc(S["pt_copied"], 1)

            def ctx_lo(g, c, h):
                r = 2 * NC * g + (2 * c + h)
                for e in range(2):
                    dve.wait_ge(S["ctx_hi"], 4 * NC * g + (4 * c + 2 * h + e + 1))
                    last = dve.scalar_tensor_tensor(out=ctx_dst(h, e, 1), in0=ctx_src(e), scalar=1.0 / P_UP,
                                                    in1=ctx_dst(h, e, 0), op0=ALU.mult, op1=ALU.subtract)
                last.then_inc(S["ctx_split"], 1)

            def x1_max(c, t):
                dve.wait_ge(S["y_added"], YT * NC * (NKV - 1) + (YT * c + t + 1 + YT))
                i, half = out_tile(t)
                return absmax(x1max[:, YT * c + t:YT * c + t + 1], y[:, CT * c + i, 512 * half:512 * half + 512])

            def add_out(g, c, between, last=False):
                banks = early_bank if last and c == NC - 2 else out_bank
                for t in range(YT):
                    dve.wait_ge(S["o_done"], YT * NC * g + (YT * c + t + 1 + YT))
                    i, half = out_tile(t)
                    dst = y[:, CT * c + i, 512 * half:512 * half + 512]
                    dve.scalar_tensor_tensor(out=dst, in0=banks[t % len(banks)][:, :], scalar=col(F_OUT + c), in1=dst,
                                             op0=ALU.mult, op1=ALU.add).then_inc(S["y_added"], 1)
                    if last and t:
                        x1_max(c, t - 1)
                    between(t)
                if last:
                    return x1_max(c, YT - 1)

            dve.wait_ge(S["consts_in"], 64)

            def step(g, c, ahead, extra, between, last=False):
                if ahead or not last:
                    soft_shift(g, c, 0)
                    soft_shift(g, c, 1)
                    soft_norm(g, c, 0)
                    soft_norm(g, c, 1)
                if ahead:
                    rope(ahead, 0)
                prob_split(g, c, 0)
                if ahead:
                    rope_split(ahead, 0)
                    extra(0)
                    rope(ahead, 1)
                pt_copy(g, c, 0)
                if ahead:
                    rope_split(ahead, 1)
                prob_split(g, c, 1)
                if ahead:
                    extra(1)
                    rope(ahead, 2)
                pt_copy(g, c, 1)
                ctx_lo(g, c, 0)
                if ahead:
                    rope_split(ahead, 2)
                    extra(2)
                    rope(ahead, 3)
                ctx_lo(g, c, 1)
                if ahead:
                    rope_split(ahead, 3)
                    extra(3)
                    v_split(ahead)
                    extra(4)
                    rope(ahead, 5)
                    rope_split(ahead, 5)
                    extra(5)
                if last and c == NC - 2:
                    soft_shift(g, c + 1, 0)
                return add_out(g, c, between, last)

            def group(g, last=False):
                def nothing(j):
                    pass

                def wo(j):
                    if j >= 3:
                        dequant(g, QKV_PIECES + 2 * (j - 3))

                def wo_between(t):
                    if t == 0:
                        dequant(g, PIECES - 2)

                def nxt(j):
                    if j >= 3:
                        dequant(g + 1, 2 * (j - 3))

                def nxt_between(t):
                    if t in (0, 3):
                        dequant(g + 1, 6 if t == 0 else 8)

                def nxt_last(j):
                    if j == 2:
                        dequant(g + 1, 10)

                def wb_stats(j):
                    k = REP * (c - 1) + j
                    if j < REP:
                        dve.wait_ge(wb_in[k % 2], 16 * (k // 2 + 1))
                        absmax(stat[:, T_WBS + k:T_WBS + k + 1], work[:, H * (k % 2):H * (k % 2 + 1)]).then_inc(S["wb_read"], 1)

                def soft_between(t):
                    if t == 0:
                        soft_shift(g, NC - 1, 1)
                    elif t == 1:
                        soft_norm(g, NC - 1, 0)
                    elif t == 2:
                        soft_norm(g, NC - 1, 1)

                def small_between(t):
                    if t == 0:
                        small_stats()
                    elif t == 3:
                        small_scales()
                    elif t == 5:
                        small_operands()
                    elif t == 6:
                        mask_sessions()
                for c in range(NC):
                    ahead = (g, c + 1) if c + 1 < NC else (None if last else (g + 1, 0))
                    extra = wo if c == 0 else wb_stats if last and c in (1, 2) else nothing
                    if not last and c >= 2:
                        extra = (nxt, nxt_last)[c - 2]
                    between = wo_between if c == 0 else nxt_between if (c == 2 and not last) else small_between if last and c == 3 else soft_between if last and c == 2 else nothing
                    end = step(g, c, ahead, extra, between, last)
                return end

            for j in range(NU):
                if j == V_AT:
                    v_split((0, 0))
                else:
                    rope((0, 0), j)
                    rope_split((0, 0), j)
                if j < len(LATE_PIECES):
                    dequant(0, LATE_PIECES[j])
            score_factors()
            with dve.Fori(0, NKV - 1) as g:
                group(g)
            group(NKV - 1, last=True).then_inc(S["x1_maxed"], 1)

            dve.wait_ge(S["x1_maxed"], 1)
            dve.reduce_max(stat[:, T_X1:T_X1 + 1], x1max[:, :], X).then_inc(S["stat_x1"], 1)
            dve.wait_ge(S["top_x1"], 1)
            m, mx = col(BOUND), col(BOUND_X)
            link(dve.scalar_tensor_tensor(out=m, in0=top[:, T_X1:T_X1 + 1], scalar=float(SEQ), in1=top[:, T_WS:T_WS + 1],
                                          op0=ALU.mult, op1=ALU.mult))
            link(dve.tensor_tensor(m, m, top[:, T_BS:T_BS + 1], ALU.add))
            pow2(SH2, ISH2, m, 1, 0, H_BITS).then_inc(S["h2_scale_ready"], 1)
            dve.wait_ge(S["h2_scale_ready"], 1)
            dve.wait_ge(S["bias_done"], 1)
            dve.tensor_copy(bias_t, ex[:, 0:B]).then_inc(S["bias_ready"], 1)

            def h2_lo(i):
                for e in range(2):
                    for th in range(2):
                        dve.wait_ge(S["h2_hi"], 4 * i + 2 * e + th + 1)
                        t = slice(512 * th, 512 * th + 512)
                        dve.scalar_tensor_tensor(out=h2[i % 2][:, 1, e, t], in0=g32[:, e, t], scalar=col(SH2),
                                                 in1=h2[i % 2][:, 0, e, t], op0=ALU.mult, op1=ALU.subtract).then_inc(S["h2_split"], 1)

            def wf_lo(z):
                dve.wait_ge(S["wf_hi"], z + 1)
                dve.scalar_tensor_tensor(out=wf_dst(z, 1), in0=wstage[:, z % 2, :], scalar=wf_scale(z), in1=wf_dst(z, 0),
                                         op0=ALU.mult, op1=ALU.subtract).then_inc(S["wf_split"], 1)

            def source_bias(i):
                if i >= 2:
                    dve.wait_ge(S["xf_split"], 2 * (i - 1))
                for kh in range(2):
                    dve.wait_ge(S["src_done"], 2 * i + kh + 1)
                    dve.scalar_tensor_tensor(out=src_tmp[i % 2][kh].rearrange("p (m s) -> p m s", s=SEQ),
                                             in0=score_bank[kh][:, :].rearrange("p (m s) -> p m s", s=SEQ),
                                             scalar=col(F_SRC), in1=b2_t.unsqueeze(1).broadcast_to([P, 8, SEQ]),
                                             op0=ALU.mult, op1=ALU.add).then_inc(S["src_biased"], 1)

            def source_lo(i):
                for kh in range(2):
                    dve.wait_ge(S["xf_hi"], 2 * i + kh + 1)
                    dve.tensor_tensor(source_dst(i, kh, 1), src_tmp[i % 2][kh].rearrange("p (k t) -> p k t", k=4),
                                      source_dst(i, kh, 0), ALU.subtract).then_inc(S["xf_split"], 1)

            link(dve.scalar_tensor_tensor(out=mx, in0=top[:, T_W2:T_W2 + 1], scalar=float(HID), in1=m, op0=ALU.mult, op1=ALU.mult))
            link(dve.tensor_tensor(mx, mx, stat[:, T_B2:T_B2 + 1], ALU.add))
            link(pow2(SX, ISX, mx, 1, 1, H_BITS))
            link(dve.tensor_tensor(col(F_SRC), col(ISH2), col(ISC2 + 2), ALU.mult))
            link(dve.tensor_tensor(col(F_SRC), col(F_SRC), col(SX), ALU.mult))
            link(dve.tensor_scalar(b2_t, b2_t, col(SX), None, ALU.mult))
            link(dve.tensor_tensor(col(F_LG), col(ISX), col(ISC2 + 1), ALU.mult))
            link(dve.scalar_tensor_tensor(out=col(F_LORA), in0=col(SC2 + 3), scalar=2.0, in1=col(ISC2), op0=ALU.mult, op1=ALU.mult))
            link(dve.tensor_tensor(col(F_BASE), col(ISX), col(ISC2 + 3), ALU.mult))
            h2_lo(0)
            for i in range(NT):
                if i + 1 < NT:
                    h2_lo(i + 1)
                wf_lo(i)
                if i:
                    source_lo(i - 1)
                source_bias(i)
            for z in range(NT, A_PIECES + WB_PIECES):
                wf_lo(z)
            source_lo(NT - 1)

            routed = [0]
            dve.wait_ge(S["lg_done"], NT)

            def step_of(ins):
                routed[0] += 1
                ins.then_inc(S["route"], 1)
                dve.wait_ge(S["route"], routed[0])
            step_of(dve.tensor_scalar(lg, lg_bank[:, 0:NT * NEXP].rearrange("p (t e) -> p t e", t=NT), col(F_LG), None, ALU.mult))
            shape = [P, NT, NEXP, NEXP]
            mine = lg.unsqueeze(3).broadcast_to(shape)
            other = lg.unsqueeze(2).broadcast_to(shape)
            g4 = big1.rearrange("p (t e j) -> p t e j", t=NT, e=NEXP)
            q4 = big2.rearrange("p (t e j) -> p t e j", t=NT, e=NEXP)
            tri4 = tri_t.rearrange("p (e j) -> p e j", e=NEXP).unsqueeze(1).broadcast_to(shape)
            dve.reduce_max(l1, lg, X)
            step_of(dve.tensor_tensor(q4, other, mine, ALU.is_equal))
            step_of(dve.tensor_tensor(le, lg, l1.unsqueeze(2).broadcast_to([P, NT, NEXP]), ALU.subtract))
            dve.tensor_tensor(g4, other, mine, ALU.is_gt)
            step_of(dve.tensor_tensor(q4, q4, tri4, ALU.mult))
            step_of(dve.tensor_tensor(g4, g4, q4, ALU.add))
            step_of(dve.reduce_sum(rk, g4, X))
            dve.wait_ge(S["route_exp"], 1)
            step_of(dve.scalar_tensor_tensor(out=rk, in0=rk, scalar=2.0, in1=le, op0=ALU.is_lt, op1=ALU.mult))
            step_of(dve.reduce_sum(dn, rk, X))
            step_of(dve.reciprocal(di, dn))
            dve.tensor_tensor(gates, rk.unsqueeze(3).broadcast_to([P, NT, NEXP, RANK]),
                              di.unsqueeze(2).unsqueeze(3).broadcast_to([P, NT, NEXP, RANK]), ALU.mult).then_inc(S["route_ready"], 1)
            dve.wait_ge(S["lora_copied"], NC)
            for c in range(NC):
                dve.wait_ge(S["wexp_done"], c + 1)
                dve.scalar_tensor_tensor(out=hw[:, CH * c:CH * (c + 1)], in0=hw[:, CH * c:CH * (c + 1)], scalar=col(F_LORA),
                                         in1=gate_bank[c % 2][:, :], op0=ALU.mult, op1=ALU.mult).then_inc(S["lora_ready"], 1)
            dve.wait_ge(S["bb_in"], 32)
            for n in range(2 * NT):
                dst = y[:, n // 2, 512 * (n % 2):512 * (n % 2) + 512]
                dve.wait_ge(S["base_done"], n + 1)
                dve.scalar_tensor_tensor(out=dst, in0=base_bank[n % 4][:, :], scalar=col(F_BASE), in1=dst,
                                         op0=ALU.mult, op1=ALU.add).then_inc(S["base_added"], 1)
                dve.wait_ge(S["base_added"], n + 1)
                dve.tensor_tensor(dst, dst, bb[n % 2], ALU.add).then_inc(S["result"], 1)

        @block.scalar
        def _(act):
            def piece_dst(z):
                if z < QKV_PIECES:
                    return w_qkv[:, z // 2, 0, 4 * (z % 2):4 * (z % 2) + 4, :].rearrange("p k n -> p (k n)")
                return w_out_piece(z - QKV_PIECES, 0)

            def dequant_hi(g, z):
                scale = UNIT_SCALE[UNITS[z // 2]] if z < QKV_PIECES else col(S4 + 3)
                act.wait_ge(S["dq_scaled"], PIECES * g + z + 1)
                act.activation(piece_dst(z), w32[:, z % 2, :], ACT.Copy, scale=scale).then_inc(S["dq_hi"], 1)

            act.wait_ge(S["idx_in"], 32)
            act.wait_ge(S["wc_zero"], 1)

            for c in range(ACT_CHUNKS):
                with act.Fori(CT * c, CT * (c + 1)) as i:
                    load_cond(act, i, 1, c)
            for c in range(NC):
                act.wait_ge(S["h_scale_ready"], c + 1)
                for k in range(KT):
                    n = c * KT + k
                    act.wait_ge(S["cond_done"], n + 1)
                    act.activation(hid[:, 0, k, CH * c:CH * (c + 1)], cond_bank(n)[:, :], ACT.Copy,
                                   scale=col(SH + c)).then_inc(S["cond_hi"], 1)
                act.wait_ge(S["w_scales_ready"], 1)
                for z in FIRST_PIECES[c]:
                    dequant_hi(0, z)
                    dequant_hi(0, z + 1)
            def rope_hi(p4, j):
                g, c = p4
                m = 5 * NC * g + (5 * c + roped_index(j))
                a = ra[:, roped_index(j) % 2, :].rearrange("p (b s) -> p b s", b=CB)
                u = UNITS[j]
                dst = kb[:, 0, :].rearrange("p (b s) -> p b s", b=CB) if u == "k" else qb[:, u // 2, 0, :, u % 2, :]
                act.wait_ge(S["rope_sum"], m + 1)
                act.wait_ge(S["scores_done"], 2 * NC * g + 2 * c + 2)
                act.activation(dst, a, ACT.Copy).then_inc(S["rope_hi"], 1)

            def v_hi(p4):
                g, c = p4
                act.wait_ge(S["proj_done"], NU * NC * g + (NU * c + V_AT + 1))
                act.wait_ge(S["pv_done"], 2 * NC * g + 2 * c + 2)
                act.activation(vb[:, 0, :, :].rearrange("p t d -> p (t d)"), pj[V_AT % 2][:, :], ACT.Copy,
                               scale=QKV_DOWN).then_inc(S["v_hi"], 1)

            def exps(g, c, h):
                act.wait_ge(S["shifted"], 2 * NC * g + (2 * c + h + 1))
                act.activation(sm[:, h, :, :], sm[:, h, :, :], ACT.Exp).then_inc(S["exps"], 1)

            def prob_hi(g, c, h):
                r = 2 * NC * g + (2 * c + h)
                act.wait_ge(S["probs"], r + 1)
                act.wait_ge(S["tp_done"], r + 2)
                act.activation(pp[:, 0, :], sm[:, h, :, :].rearrange("p b s -> p (b s)"), ACT.Copy).then_inc(S["probs_hi"], 1)

            def ctx_hi(g, c, h):
                r = 2 * NC * g + (2 * c + h)
                act.wait_ge(S["pv_done"], r + 1 + 2)
                act.wait_ge(S["o_done"], YT * NC * g + YT * c + YT)
                for e in range(2):
                    act.activation(ctx_dst(h, e, 0), ctx_src(e), ACT.Copy, scale=1.0 / P_UP).then_inc(S["ctx_hi"], 1)

            def step(g, c, ahead, extra, after, scored=False):
                if not scored:
                    exps(g, c, 0)
                    exps(g, c, 1)
                prob_hi(g, c, 0)
                if ahead:
                    rope_hi(ahead, 0)
                    extra(0)
                    rope_hi(ahead, 1)
                prob_hi(g, c, 1)
                if ahead:
                    extra(1)
                    rope_hi(ahead, 2)
                ctx_hi(g, c, 0)
                if ahead:
                    extra(2)
                    rope_hi(ahead, 3)
                ctx_hi(g, c, 1)
                if ahead:
                    extra(3)
                    v_hi(ahead)
                    extra(4)
                    rope_hi(ahead, 5)
                    extra(5)
                after()

            def group(g, last=False):
                def nothing(j=0):
                    pass

                def wo(j):
                    if j >= 3:
                        if j == 3:
                            act.wait_ge(S["o_done"], YT * NC * g + YT)
                        dequant_hi(g, QKV_PIECES + 2 * (j - 3))
                        dequant_hi(g, QKV_PIECES + 2 * (j - 3) + 1)

                def wo_after():
                    for z in (PIECES - 2, PIECES - 1):
                        dequant_hi(g, z)

                def next_unit(j):
                    act.wait_ge(S["proj_done"], NU * NC * g + (NU * (NC - 1) + j + 1))
                    dequant_hi(g + 1, 2 * j)
                    dequant_hi(g + 1, 2 * j + 1)

                def nxt(j):
                    if j >= 3:
                        next_unit(j - 3)

                def nxt_after():
                    for j in (3, 4):
                        next_unit(j)

                def nxt_last(j):
                    if j == 2:
                        next_unit(5)

                def exps_after():
                    exps(g, NC - 1, 0)
                    exps(g, NC - 1, 1)

                def small_after():
                    act.wait_ge(S["scales_ready"], 1)
                    for dst, src, scale in small_parts():
                        act.activation(dst(0), src, ACT.Copy, scale=scale).then_inc(S["small_hi"], 1)
                for c in range(NC):
                    ahead = (g, c + 1) if c + 1 < NC else (None if last else (g + 1, 0))
                    extra = wo if c == 0 else nothing
                    if not last and c >= 2:
                        extra = (nxt, nxt_last)[c - 2]
                    after = wo_after if c == 0 else nxt_after if (c == 2 and not last) else small_after if last and c == 3 else exps_after if last and c == 2 else nothing
                    step(g, c, ahead, extra, after, scored=last and c == NC - 1)

            for j in range(NU):
                if j == V_AT:
                    v_hi((0, 0))
                else:
                    rope_hi((0, 0), j)
                if j < len(LATE_PIECES):
                    dequant_hi(0, LATE_PIECES[j])
                    dequant_hi(0, LATE_PIECES[j] + 1)
            with act.Fori(0, NKV - 1) as g:
                group(g)
            group(NKV - 1, last=True)

            act.wait_ge(S["bias_ready"], 1)
            act.wait_ge(S["h2_scale_ready"], 1)

            def wf_hi(z):
                act.wait_ge(wf_in[z % 2], 16 * (z // 2 + 1))
                act.activation(wf_dst(z, 0), wstage[:, z % 2, :], ACT.Copy, scale=wf_scale(z)).then_inc(S["wf_hi"], 1)

            def source_hi(i):
                for kh in range(2):
                    act.wait_ge(S["src_ready"], 2 * i + kh + 1)
                    act.activation(source_dst(i, kh, 0), src_tmp[i % 2][kh].rearrange("p (k t) -> p k t", k=4),
                                   ACT.Copy).then_inc(S["xf_hi"], 1)

            def copy_lora(c):
                act.wait_ge(S["lora_done"], CT * (c + 1))
                act.activation(hw[:, CH * c:CH * (c + 1)], ex[:, :], ACT.Copy).then_inc(S["lora_copied"], 1)
            for i in range(NT):
                tiles = [(e, th) for e in range(2) for th in range(2)]
                for n, (e, th) in enumerate(tiles):
                    act.wait_ge(S["hid_done"], 4 * i + n + 1)
                    if i:
                        act.wait_ge(S["h2_split"], 4 * (i - 1) + n + 1)
                    act.activation(g32[:, e, 512 * th:512 * th + 512], h_bank[e][th][:, :], ACT.Gelu,
                                   bias=bias_t[:, 2 * i + e:2 * i + e + 1]).then_inc(S["gelu_done"], 1)
                if i >= 2:
                    act.wait_ge(S["src_done"], 2 * (i - 1))
                for n, (e, th) in enumerate(tiles):
                    act.wait_ge(S["gelu_done"], 4 * i + n + 1)
                    act.activation(h2[i % 2][:, 0, e, 512 * th:512 * th + 512], g32[:, e, 512 * th:512 * th + 512],
                                   ACT.Copy, scale=col(SH2)).then_inc(S["h2_hi"], 1)
                wf_hi(i)
                if i >= 2:
                    source_hi(i - 2)
                if i >= CT and i % CT == 2:
                    copy_lora(i // CT - 1)
            wf_hi(NT)
            source_hi(NT - 2)
            for z in range(NT + 1, A_PIECES + WB_PIECES):
                wf_hi(z)
            source_hi(NT - 1)
            copy_lora(NC - 1)
            act.wait_ge(S["route"], 3)
            act.activation(le, le, ACT.Exp).then_inc(S["route_exp"], 1)

        @block.tensor
        def _(pe):
            mm = nc.tensor.matmul
            for c in range(NC):
                pe.wait_ge(x_in[c], 16)
                pe.wait_ge(wc_in[c], 16 * CB)
                for k in range(KT):
                    n = c * KT + k
                    if n >= len(cond_banks):
                        pe.wait_ge(S["cond_split"], n - len(cond_banks) + 1)
                    for i in range(CT):
                        last = mm(cond_bank(n)[:, P * i:P * (i + 1)], y[:, CT * c + i, P * k:P * (k + 1)],
                                  wc[:, CT * c + i, :], start=True, stop=True)
                    last.then_inc(S["cond_done"], 1)

            PARTS = ((0, 0), (0, 1), (1, 0))

            def project(p4, j):
                g, c = p4
                n = NU * NC * g + (NU * c + j)
                pe.wait_ge(S["w_ready"], PIECES * g + 2 * (j + 1))
                if not isinstance(g, int) or NU * (NC * g + c) + j >= 2:
                    pe.wait_ge(S["proj_read"], n - 1)
                if j == 0 and not (isinstance(g, int) and g == c == 0):
                    pe.wait_ge(S["y_added"], YT * NC * g + YT * c)
                bank = pj[j % 2]
                if UNITS[j] == "v":
                    for i in range(CT):
                        for k in range(KT):
                            for lw, lh in PARTS:
                                last = mm(bank[:, P * i:P * (i + 1)], hid[:, lw, k, CH * c + P * i:CH * c + P * (i + 1)],
                                          w_qkv[:, j, lh, k, :], start=(k == 0 and (lw, lh) == (0, 0)),
                                          stop=(k == KT - 1 and (lw, lh) == (1, 0)))
                else:
                    for k in range(KT):
                        for lw, lh in PARTS:
                            last = mm(bank[:, :], w_qkv[:, j, lw, k, :], hid[:, lh, k, CH * c:CH * (c + 1)],
                                      start=(k == 0 and (lw, lh) == (0, 0)), stop=(k == KT - 1 and (lw, lh) == (1, 0)))
                last.then_inc(S["proj_done"], 1)

            def scores(g, c, h, early=False):
                pe.wait_ge(S["qk_ready"], 5 * NC * g + (5 * c + (3, 5)[h]))
                pe.wait_ge(S["y_added"], YT * NC * g + YT * c + (0 if early else (YT - 1, YT - 2)[h]))
                for b in range(CB):
                    for lq, lk in PARTS:
                        last = mm(score_bank[h][:, SEQ * b:SEQ * (b + 1)], qb[:, h, lq, b, :, :].rearrange("p h s -> p (h s)"),
                                  kb[:, lk, SEQ * b:SEQ * (b + 1)], start=(lq, lk) == (0, 0), stop=(lq, lk) == (1, 0))
                last.then_inc(S["scores_done"], 1)

            def transpose_probs(g, c, h):
                r = 2 * NC * g + (2 * c + h)
                pe.wait_ge(S["probs_split"], r + 1 + 2)
                pe.wait_ge(S["pt_copied"], r + 2)
                for part in range(2):
                    for j in range(CT):
                        last = nc.tensor.transpose(tp[:, part, j, :], pp[:, part, P * j:P * (j + 1)], id16[:, :])
                last.then_inc(S["tp_done"], 1)

            def weigh_values(g, c, h):
                r = 2 * NC * g + (2 * c + h)
                pe.wait_ge(S["proj_read"], NU * NC * g + (NU * c + V_AT + 1))
                pe.wait_ge(S["pt_copied"], r + 1 + 2)
                pe.wait_ge(S["ctx_split"], r + 2)
                for j in range(CT):
                    for lv, lp in PARTS:
                        for e in range(2):
                            rows = slice(SEQ * e, SEQ * (e + 1))
                            last = mm(ctx_columns(e, j), vb[rows, lv, j, :],
                                      pt[rows, lp, j, :].rearrange("k (h s) -> k h s", h=2),
                                      start=(lv, lp) == (0, 0), stop=(lv, lp) == (1, 0))
                last.then_inc(S["pv_done"], 1)

            def project_out(g, c, ahead, early=False):
                banks = early_bank if early else out_bank
                pe.wait_ge(S["ctx_split"], 2 * NC * g + (2 * c + 2 + 2))
                for t in range(YT):
                    if t % CT == 0:
                        pe.wait_ge(S["w_ready"], PIECES * g + (QKV_PIECES + REP * (1 + t // CT)))
                    if t == 1 and early:
                        scores(*ahead, 1, early=True)
                        pe.wait_ge(S["proj_read"], NU * NC * g + NU * (c + 2))
                    elif t == 1:
                        pe.wait_ge(S["masked"], 2 * NC * g + (2 * c + 2))
                    if t == 3 and ahead and not early:
                        pe.wait_ge(S["proj_read"], NU * NC * g + (NU * (c + 1) + V_AT + 1))
                    if t == 0 or t >= len(banks):
                        pe.wait_ge(S["y_added"], YT * NC * g + (YT * c + YT + (t - len(banks) + 1 if t else -1)))
                    i, half = out_tile(t)
                    n0 = 512 * half
                    for h in range(REP):
                        for lc, lw in PARTS:
                            last = mm(banks[t % len(banks)][:, :], cb[:, lc, h, P * i:P * (i + 1)], w_out[:, h, lw, n0:n0 + 512],
                                      start=(h == 0 and (lc, lw) == (0, 0)), stop=(h == REP - 1 and (lc, lw) == (1, 0)))
                    last.then_inc(S["o_done"], 1)

            def step(g, c, ahead, early=False, scored=False):
                if not scored:
                    scores(g, c, 0)
                    scores(g, c, 1)
                if ahead:
                    project(ahead, 0)
                    project(ahead, 1)
                transpose_probs(g, c, 0)
                if ahead:
                    project(ahead, 2)
                weigh_values(g, c, 0)
                transpose_probs(g, c, 1)
                if ahead:
                    project(ahead, 3)
                weigh_values(g, c, 1)
                if ahead:
                    project(ahead, 4)
                    project(ahead, 5)
                if early:
                    scores(*ahead, 0, early=True)
                project_out(g, c, ahead, early)

            def group(g, last=False):
                for c in range(NC):
                    step(g, c, (g, c + 1) if c + 1 < NC else (None if last else (g + 1, 0)),
                         early=last and c == NC - 2, scored=last and c == NC - 1)

            pe.wait_ge(S["consts_in"], 64)
            pe.wait_ge(S["cond_split"], NC * KT)
            for j in range(NU):
                project((0, 0), j)
            with pe.Fori(0, NKV - 1) as g:
                group(g)
            group(NKV - 1, last=True)

            pe.wait_ge(S["onehot_made"], 1)
            pe.wait_ge(S["y_added"], YT * NC * NKV + YT - 3)
            mm(ex[:, 0:B], bs_t, hot_t, start=True, stop=True).then_inc(S["bias_done"], 1)
            pe.wait_ge(S["wsess_masked"], 1)

            def hidden2(i):
                for e in range(2):
                    rows = slice(SEQ * e, SEQ * (e + 1))
                    if i == 0 and e == 1:
                        pe.wait_ge(S["y_added"], YT * NC * NKV + YT)
                    for th in range(2):
                        if i:
                            pe.wait_ge(S["gelu_done"], 4 * (i - 1) + 2 * e + th + 1)
                        mm(h_bank[e][th][:, :], ws[rows, i, :], y[rows, i, 512 * th:512 * th + 512],
                           start=True, stop=True).then_inc(S["hid_done"], 1)

            def sources(i):
                pe.wait_ge(S["h2_split"], 4 * (i + 1))
                for kh in range(2):
                    if i:
                        pe.wait_ge(S["src_biased"], 2 * (i - 1) + kh + 1)
                    for kk in range(4):
                        for e in range(2):
                            k = 4 * kh + kk
                            at = SEQ * (2 * kk + e)
                            for lh, lw in PARTS:
                                last = mm(score_bank[kh][:, at:at + SEQ], h2[i % 2][:, lh, e, P * k:P * (k + 1)], w2h[:, lw, :],
                                          start=(lh, lw) == (0, 0), stop=(lh, lw) == (1, 0))
                    last.then_inc(S["src_done"], 1)

            def route_and_lora(i):
                c, i0 = i // CT, i % CT
                tokens = slice(P * i0, P * (i0 + 1))
                if i == 0:
                    pe.wait_ge(S["wf_split"], A_PIECES)
                pe.wait_ge(S["xf_split"], 2 * (i + 1))
                for k in range(KT):
                    for lx, lw in PARTS:
                        last = mm(lg_bank[:, NEXP * i:NEXP * (i + 1)], xpart(c, lx)[:, k, tokens], wrh[:, lw, k, :],
                                  start=(k == 0 and (lx, lw) == (0, 0)), stop=(k == KT - 1 and (lx, lw) == (1, 0)))
                last.then_inc(S["lg_done"], 1)
                if c and i0 == 0:
                    pe.wait_ge(S["lora_copied"], c)
                for k in range(KT):
                    for la, lx in PARTS:
                        last = mm(ex[:, tokens], a16[:, la, k, :], xpart(c, lx)[:, k, tokens],
                                  start=(k == 0 and (la, lx) == (0, 0)), stop=(k == KT - 1 and (la, lx) == (1, 0)))
                last.then_inc(S["lora_done"], 1)
            hidden2(0)
            for i in range(NT):
                if i + 1 < NT:
                    hidden2(i + 1)
                sources(i)
                if i >= 2:
                    route_and_lora(i - 2)
            route_and_lora(NT - 2)
            route_and_lora(NT - 1)
            pe.wait_ge(S["wf_split"], WB_PIECES + A_PIECES)
            pe.wait_ge(S["bcat_in"], 16)

            def base(n):
                c, i, n0 = n // YT, (n // 2) % CT, 512 * (n % 2)
                if n >= 4:
                    pe.wait_ge(S["base_added"], n - 3)
                for k in range(KT):
                    for lx, lw in PARTS:
                        mm(base_bank[n % 4][:, :], xpart(c, lx)[:, k, P * i:P * (i + 1)], wb16[:, lw, k, n0:n0 + 512],
                           start=(k == 0 and (lx, lw) == (0, 0)), stop=False)

            def add_lora(n):
                t, n0 = n // 2, 512 * (n % 2)
                mm(base_bank[n % 4][:, :], hw[:, P * t:P * (t + 1)], bc_t[:, n0:n0 + 512], start=False,
                   stop=True).then_inc(S["base_done"], 1)
            for n in range(4):
                if n == 3:
                    pe.wait_ge(S["lora_copied"], NC)
                base(n)
            pe.wait_ge(S["route_ready"], 1)
            pe.wait_ge(S["lora_copied"], NC)
            for c in range(NC):
                if c >= 2:
                    pe.wait_ge(S["lora_ready"], c - 1)
                for i in range(CT):
                    last = mm(gate_bank[c % 2][:, P * i:P * (i + 1)], gates[:, CT * c + i, :, :].rearrange("p e r -> p (e r)"),
                              id32, start=True, stop=True)
                last.then_inc(S["wexp_done"], 1)
            for n in range(2 * NT):
                if n >= 4:
                    base(n)
                pe.wait_ge(S["lora_ready"], n // YT + 1)
                add_lora(n)


def kernel(x, itok_B_0_15, itok_B_0_7, itok_B_2182_4065, _lenS, L0_cond_weights, L0_attn_scales_q,
           L0_attn_scales_k, L0_attn_scales_v, L0_attn_scales_o, L0_attn_qw_q, L0_attn_qw_k, L0_attn_qw_v,
           L0_attn_qw_o, L0_cond2_W_sess, L0_cond2_b_sess, L0_cond2_W2, L0_cond2_b2, L0_ffn_W_base,
           L0_ffn_b_base, L0_ffn_W_router, L0_ffn_A, L0_ffn_B):
    import numpy as np
    import concourse.bacc as bacc
    from concourse.bass_utils import run_bass_kernel_spmd

    def lay(a):
        return np.ascontiguousarray(np.asarray(a))

    f4 = np.float32
    inv_freq = (f4(1.0) / np.power(f4(10000.0), np.arange(0, HD, 2, dtype=f4) / f4(HD))).astype(f4)
    angle = (np.arange(SEQ, dtype=f4)[None, :] * inv_freq[:, None]).astype(f4)
    cos = np.concatenate([np.cos(angle)] * 2, 0).astype(f4) * f4(QKV_DOWN)
    sin = np.concatenate([np.sin(angle), -np.sin(angle)], 0).astype(f4) * f4(QKV_DOWN)
    pos = np.arange(P)
    mask = np.where(pos[:, None] % SEQ >= np.arange(SEQ)[None, :], 0.0, -3.0e38).astype(f4)
    row = (pos % SEQ)[:, None].astype(f4)
    arrays = {
        "x_d": lay(x).reshape(TOK, H),
        "cond_d": lay(itok_B_0_15).reshape(1, B),
        "ids_d": lay(np.broadcast_to(np.asarray(itok_B_0_7), (NEXP, B))),
        "seq_d": lay(np.broadcast_to(np.asarray(itok_B_2182_4065), (P, B))),
        "len_d": lay(np.repeat(np.asarray(_lenS).reshape(NT, 2).T, SEQ, axis=0)),
        "cw_d": lay(L0_cond_weights),
        "sq_d": lay(L0_attn_scales_q), "sk_d": lay(L0_attn_scales_k), "sv_d": lay(L0_attn_scales_v),
        "so_d": lay(L0_attn_scales_o),
        "qq_d": lay(L0_attn_qw_q), "qk_d": lay(L0_attn_qw_k), "qv_d": lay(L0_attn_qw_v), "qo_d": lay(L0_attn_qw_o),
        "wse_d": lay(L0_cond2_W_sess), "bse_d": lay(L0_cond2_b_sess), "w2_d": lay(L0_cond2_W2), "b2_d": lay(L0_cond2_b2),
        "wb_d": lay(np.asarray(L0_ffn_W_base).T), "bb_d": lay(L0_ffn_b_base),
        "wr_d": lay(np.asarray(L0_ffn_W_router).T),
        "a_d": lay(np.asarray(L0_ffn_A).reshape(NEXP * RANK, H).T),
        "bcat_d": lay(np.asarray(L0_ffn_B).transpose(0, 2, 1).reshape(NEXP * RANK, H)),
        "cos_d": cos, "sin_d": sin, "mask_d": mask, "id16_d": np.eye(P, dtype=np.float16),
        "id32_d": np.eye(P, dtype=f4), "row_d": row,
        "t_d": (pos[:, None] + P * np.arange(KT)[None, :]).astype(f4),
        "tri_d": lay(np.broadcast_to(np.tril(np.ones((NEXP, NEXP), f4), -1).reshape(1, -1), (P, NEXP * NEXP))),
    }
    nc = bacc.Bacc("TRN2", target_bir_lowering=False, num_devices=1, dynamic_dma_scratch_size=1024)
    args = [nc.dram_tensor(n, a.shape, mybir.dt.from_np(a.dtype), kind="ExternalInput").ap() for n, a in arrays.items()]
    out = nc.dram_tensor("out_d", (TOK, H), mybir.dt.float32, kind="ExternalOutput").ap()
    build(nc, *args, out)
    result = run_bass_kernel_spmd(nc, [arrays], core_ids=[0])
    return result.results[0]["out_d"].reshape(B, SEQ, H)
```

```python
import math
from contextlib import ExitStack

import concourse.bass as bass
from concourse import mybir

B, SEQ, H = 32, 64, 1024
TOK = B * SEQ
HD, NH, NKV = 128, 32, 8
REP = NH // NKV
HID, NEXP, RANK = 128, 8, 16
P = 128
KT = H // P
CH = 512
NC = TOK // CH
CB = CH // SEQ
CT = CH // P
NT = TOK // P
UNITS = ("k", 0, 1, "v", 2, 3)
NU, NI = 4, 2
V_AT = UNITS.index("v")
NKT = NI * KT
NADD = NI * (KT - 1)
ROPED = [u for u in UNITS if u != "v"]
WO_PIECES = 2 * REP
QKV_PIECES = 2 * NU
PIECES = WO_PIECES + QKV_PIECES
INT_PIECES = 2 * NI
YT = 2 * CT
TILE_STARTS = (2, 4, 7, 10, 12, 14, 16, 16, 16)

W_BITS = 11
H_BITS = 14
QKV_DOWN = 2.0 ** -26
P_UP = 2.0 ** 14
TINY = 2.0 ** -100
EXPONENT = 0x7F800000
WB_STATS = 2 * KT
WB_PIECES = 2 * KT
A_PIECES = 2


def build(nc, x, cond_rep, ids_rep, seq_rep, len_rep, cond_w, s_q, s_q_cols, s_k, s_v, s_o, q_q, q_k, q_v, q_o,
          w_sess, b_sess, w2, b2, w_base_t, b_base, w_router_t, a_t, b_cat,
          rope_cos, rope_sin, neg_mask, ident16, ident32, row_of, t_of, tri, out):
    f32, f16, i32 = mybir.dt.float32, mybir.dt.float16, mybir.dt.int32
    ALU, ACT, X = mybir.AluOpType, mybir.ActivationFunctionType, mybir.AxisListType.X
    MAX = bass.bass_isa.ReduceOp.max
    ds = bass.ds

    ctx = ExitStack()
    with ctx:
        def sb(name, shape, dt):
            return ctx.enter_context(nc.sbuf_tensor(name, shape, dt))

        def pb(name, shape=(P, CH), dt=f32):
            return ctx.enter_context(nc.psum_tensor(name, list(shape), dt))

        def sem(name):
            return ctx.enter_context(nc.semaphore(name))

        y = sb("y", [P, NT, H], f32)
        hid = sb("hid", [P, 2, KT, TOK], f16)
        QKV_END = 2 * KT * P * NU
        INT_END = QKV_END + KT * P * NI
        ACC_END = INT_END + 2 * CH * NI
        wts = sb("wts", [P, ACC_END + 2 * REP * H], f16)
        w_qkv = wts[:, 0:QKV_END].rearrange("p (u l k n) -> p u l k n", u=NU, l=2, k=KT)
        w_int = wts[:, QKV_END:INT_END].rearrange("p (u k n) -> p u k n", u=NI, k=KT)
        acc = wts[:, INT_END:ACC_END].bitcast(f32).rearrange("p (u n) -> p u n", u=NI)
        w_out = wts[:, ACC_END:].rearrange("p (h l n) -> p h l n", h=REP, l=2)
        int_stage = sb("int_stage", [P, CH], i32)
        int_raw = sb("int_raw", [P, NI * KT], f32)
        int_scale = sb("int_scale", [P, NI * KT], f32)
        work = sb("work", [P, 5632], f32)
        stage = work[:, 0:2048].rearrange("p (s w n) -> p s w n", s=2, w=2)
        w32 = work[:, 2048:3072].rearrange("p (s n) -> p s n", s=2)
        ra = work[:, 3072:4096].rearrange("p (s n) -> p s n", s=2)
        rb = work[:, 4096:4608]
        sm = work[:, 4608:5632].rearrange("p (h b s) -> p h b s", h=2, b=CB)
        qb = sb("qb", [P, 2, 2, CB, 2, SEQ], f16)
        kb = sb("kb", [P, 2, CH], f16)
        vb = sb("vb", [P, 2, CT, HD], f16)
        pp = sb("pp", [P, 2, CH], f16)
        pt = sb("pt", [P, 2, CT, P], f16)
        cb = sb("cb", [P, 2, REP, CH], f16)
        rmax = sb("rmax", [P, 2, CB], f32)
        rsum = sb("rsum", [P, 2, CB], f32)
        rinv = sb("rinv", [P, 2, CB], f32)
        cos_t = sb("cos_t", [P, SEQ], f32)
        sin_t = sb("sin_t", [P, SEQ], f32)
        mask_t = sb("mask_t", [P, SEQ], f32)
        id16 = sb("id16", [P, P], f16)
        small = sb("small", [P, 512], f32)
        misc = sb("misc", [P, 640], f32)
        stat = sb("stat", [P, 17 + WB_STATS], f32)
        top = sb("top", [P, 17], f32)
        wbmax = stat[:, 17:17 + WB_STATS]
        x1max = sb("x1max", [P, NC * YT], f32)
        sc = sb("sc", [P, 80], f32)
        bits = sb("bits", [P, 16], i32)
        cidx = sb("cidx", [1, B], i32)
        sidx = sb("sidx", [1, B], i32)

        raw = hid[:, :, :, :].bitcast(f32).rearrange("p l k t -> p (l k t)")
        wc = cb[:, :, :, :].bitcast(f32).rearrange("p a h c -> p (a h c)").rearrange("p (i d) -> p i d", i=NT)

        tile_buf = [small[:, 0:CH], misc[:, 0:CH]]

        pj = [pb("pj0"), pb("pj1")]
        sa, sbk, ex = pb("sa"), pb("sbk"), pb("ex")
        tp = pb("tp", (P, 2, CT, P), f16)
        cx = [pb("cx0"), pb("cx1")]
        score_bank = [sbk, sa]
        unit_bank = [pj[0], pj[1], pj[0], ex]
        out_bank = [sbk, sa, ex]

        early_bank = [cx[0], cx[1], ex]

        names = """consts_in idx_in stats_in stats2_in wc_zero
                   stat_w stat_x stat_c2 stat_wb stat_x1 top_w top_x top_c2 top_wb top_x1
                   scal w_scales_ready h_scale_ready scales_ready
                   cond_done cond_hi cond_split
                   dq_scaled dq_hi w_ready int_in int_ready int_raw_in int_scaled kt_done kt_read added acc_read
                   proj_done proj_read rope_sum rope_hi qk_ready v_hi
                   scores_done masked rowmaxed shifted exps summed inverted probs probs_hi probs_split
                   tp_done pt_copied pv_done ctx_hi ctx_split o_done y_added wb_read
                   wsess_in masks_made wsess_masked onehot_made bias_done bias_ready c2_in small_split small_hi
                   h2_scale_ready x1_maxed hid_done gelu_done h2_hi h2_split src_done src_biased src_ready
                   wf_hi wf_split bcat_in bb_in xf_hi xf_split
                   lg_done route route_exp route_ready lora_done lora_copied wexp_done lora_ready
                   base_done base_added result stored"""
        S = {n: sem(n) for n in names.split()}
        staged = [sem("staged0"), sem("staged1")]
        x_in = [sem(f"x_in{c}") for c in range(NC)]
        wc_in = [sem(f"wc_in{c}") for c in range(NC)]
        wb_in = [sem("wb_in0"), sem("wb_in1")]
        wf_in = [sem("wf_in0"), sem("wf_in1")]

        block = ctx.enter_context(nc.Block())

        arena = wts[:, :].bitcast(f32)
        wb16 = wts[:, 0:2 * KT * H].rearrange("p (l k n) -> p l k n", l=2, k=KT)
        a16 = wts[:, 2 * KT * H:2 * KT * H + 2 * KT * P].rearrange("p (l k n) -> p l k n", l=2, k=KT)
        bc_t = arena[:, 9216:10240]
        hw = work[:, 0:2048]
        ws = hw.rearrange("p (i d) -> p i d", i=NT)
        cb32 = cb[:, :, :, :].bitcast(f32).rearrange("p a h c -> p (a h c)")
        g32 = cb32.rearrange("p (e t) -> p e t", e=2)
        gates = cb32.rearrange("p (t e r) -> p t e r", t=NT, e=NEXP)
        big1, big2 = cb32[:, 0:1024], cb32[:, 1024:2048]
        h2 = [work[:, 2048:4096].bitcast(f16).rearrange("p (l e t) -> p l e t", l=2, e=2),
              qb[:, :, :, :, :, :].rearrange("p a l b h s -> p (a l b h s)").rearrange("p (l e t) -> p l e t", l=2, e=2)]
        wstage = sm.rearrange("p h b s -> p h (b s)")
        vm = rb
        lg = vm[:, 0:128].rearrange("p (t e) -> p t e", t=NT)
        le = vm[:, 128:256].rearrange("p (t e) -> p t e", t=NT)
        rk = vm[:, 256:384].rearrange("p (t e) -> p t e", t=NT)
        l1 = vm[:, 384:400]
        dn = vm[:, 400:416]
        di = vm[:, 416:432]
        bb = [kb[:, :, :].bitcast(f32).rearrange("p l t -> p (l t)"),
              vb[:, :, :, :].bitcast(f32).rearrange("p l t d -> p (l t d)")]
        src_tmp = [[pp[:, :, :].bitcast(f32).rearrange("p l t -> p (l t)"),
                    pt[:, :, :, :].bitcast(f32).rearrange("p l t n -> p (l t n)")], bb]

        def xpart(c, part):
            return hid[:, part, :, CH * c:CH * (c + 1)]

        def source_dst(i, kh, part):
            return hid[:, part, 4 * kh:4 * kh + 4, P * i:P * (i + 1)]
        id32 = small[:, 0:128]
        w2_t = small[:, 128:192]
        b2_t = small[:, 192:256]
        wr_t = small[:, 256:320].rearrange("p (k e) -> p k e", k=KT)
        tri_t = small[:, 320:384]
        row_t = small[:, 384:385]
        tt_t = small[:, 385:393]
        len_t = small[:, 393:409].bitcast(i32)
        seq_t = small[:, 409:441].bitcast(i32)
        ids_t = small[0:NEXP, 441:473].bitcast(i32)
        bias_t = small[:, 473:505]
        bs_t = misc[0:NEXP, 0:128]
        hot_t = misc[0:NEXP, 128:160]
        cm_t = misc[:, 160:176]
        tm_t = misc[:, 192:448].rearrange("p (k b) -> p k b", k=KT)
        w2h = misc[:, 448:512].bitcast(f16).rearrange("p (l s) -> p l s", l=2)
        wrh = misc[:, 512:576].bitcast(f16).rearrange("p (l k e) -> p l k e", l=2, k=KT)

        SH, S4, IS4, ISH, A, QS, KS, F_SCORE, AV, F_OUT, M = 0, 4, 8, 12, 16, 20, 24, 28, 32, 36, 40
        SC2, ISC2 = 44, 48
        SH2, ISH2, SX, ISX, F_SRC, F_LG, F_LORA, F_BASE, BOUND, BOUND_X = 52, 53, 54, 55, 56, 57, 58, 59, 60, 64
        T_X, T_CW, T_S4, T_A, T_R, T_W2, T_WB, T_WS, T_BS, T_X1, T_B2 = 0, 4, 5, 9, 10, 11, 12, 13, 14, 15, 16

        def col(n, k=1):
            return sc[:, n:n + k]
        UNIT_SCALE = {u: col(S4 + {"k": 1, "v": 2}.get(u, 0)) for u in UNITS}

        def roped_index(j):
            return sum(1 for u in UNITS[:j] if u != "v")

        lg_bank = tp[:, :, :, :].bitcast(f32).rearrange("p l t n -> p (l t n)")
        base_bank = [cx[0], cx[1], sa, ex]
        gate_bank = [sbk, pj[0]]
        h_bank = [[cx[0], cx[1]], [pj[0], pj[1]]]

        def wf_dst(z, part):
            if z < A_PIECES:
                return a16[:, part, 4 * z:4 * (z + 1), :].rearrange("p k n -> p (k n)")
            z -= A_PIECES
            return wb16[:, part, z // 2, 512 * (z % 2):512 * (z % 2) + 512]

        def wf_scale(z):
            return col(SC2) if z < A_PIECES else col(SC2 + 3)

        def w_out_piece(n, part):
            half, h = n // REP, n % REP
            return w_out[:, h, part, 512 * half:512 * half + 512]

        def out_tile(t):
            return t % CT, t // CT

        def small_parts():
            return ((lambda part: w2h[:, part, :], w2_t, col(SC2 + 2)),
                    (lambda part: wrh[:, part, :, :].rearrange("p k e -> p (k e)"), small[:, 256:320], col(SC2 + 1)))

        cond_banks = [pj[0], pj[1], ex, cx[0], cx[1], sa, sbk]

        def tile_bank(n, first):
            return cx[n % 2] if first else pj[1 - n % 2]

        def tiles_at(t):
            return range(TILE_STARTS[t], TILE_STARTS[t + 1])

        def cond_bank(n):
            return cond_banks[n % len(cond_banks)]

        def ctx_src(e):
            return cx[e][:, :].rearrange("p (m s) -> p m s", s=SEQ)

        def ctx_columns(e, j):
            return cx[e][:, :].rearrange("p (h j s) -> p j h s", h=2, s=SEQ)[:, j]

        def ctx_dst(h, e, part):
            return cb[:, part, 2 * h:2 * h + 2, :].rearrange("p h (j e s) -> p e (h j) s", e=2, s=SEQ)[:, e]

        ACT_CHUNKS = 2

        def load_cond(queue, i, odd, c):
            s = queue.value_load(cidx[0:1, ds(i * 2 + odd, 1)], min_val=0, max_val=15)
            queue.dma_start(wc[SEQ * odd:SEQ * (odd + 1), ds(i, 1), SEQ * odd:SEQ * (odd + 1)],
                            cond_w[ds(s, 1), :, :].rearrange("a c d -> c a d")).then_inc(wc_in[c], 16)

        @block.sync
        def _(sp):
            sp.sem_inc(S["scores_done"], 2)
            sp.sem_inc(S["tp_done"], 2)
            sp.sem_inc(S["probs_split"], 2)
            sp.sem_inc(S["pv_done"], 2)
            sp.sem_inc(S["pt_copied"], 2)
            sp.sem_inc(S["ctx_split"], 2)
            sp.sem_inc(S["o_done"], YT)
            sp.sem_inc(S["y_added"], YT)
            at = [0]

            def load_stats(src, n, name, place=raw):
                sp.dma_start(place[:, at[0]:at[0] + n], src).then_inc(S[name], 16)
                at[0] += n
            load_stats(cond_w.rearrange("s (q c) d -> (s q) (c d)", q=8), 512, "stats_in")
            load_stats(s_q.rearrange("a (b n) -> (a b) n", b=16), 256, "stats_in")
            load_stats(s_k.rearrange("a (b n) -> (a b) n", b=16), 64, "stats_in")
            load_stats(s_v.rearrange("a (b n) -> (a b) n", b=16), 64, "stats_in")
            load_stats(s_o.rearrange("a (b n) -> (a b) n", b=4), 256, "stats_in")
            sp.dma_start(cidx[:, :], cond_rep).then_inc(S["idx_in"], 16)
            sp.dma_start(sidx[:, :], ids_rep[0:1, :]).then_inc(S["idx_in"], 16)

            def load_x(c):
                sp.dma_start(y[:, CT * c:CT * (c + 1), :],
                             x[CH * c:CH * (c + 1), :].rearrange("(i p) n -> p i n", p=P)).then_inc(x_in[c], 16)
            load_x(0)

            def load_piece(g, z):
                slot = z % 2
                if isinstance(g, int):
                    if PIECES * g + z >= 2:
                        sp.wait_ge(S["dq_scaled"], PIECES * g + z - 1)
                else:
                    sp.wait_ge(S["dq_scaled"], g * PIECES + (z - 1))
                if z < QKV_PIECES:
                    u, half = UNITS[z // 2], z % 2
                    qw, s = {"k": (q_k, s_k), "v": (q_v, s_v)}.get(u, (q_q, s_q))
                    col = g * HD if u in ("k", "v") else g * (REP * HD) + u * HD
                    rows = 4 * P * half
                    src = qw[rows:rows + 4 * P, ds(col, HD)].rearrange("(k p) n -> p k n", p=P)
                    scale = s[4 * half:4 * half + 4, ds(col, HD)].partition_broadcast(P)
                    shape = "p (k n) -> p k n"
                    sp.dma_start(stage[:, slot, 0, :].bitcast(i32).rearrange(shape, k=4), src).then_inc(staged[slot], 16)
                    sp.dma_start(stage[:, slot, 1, :].rearrange(shape, k=4), scale).then_inc(staged[slot], 16)
                else:
                    half, h = (z - QKV_PIECES) // REP, (z - QKV_PIECES) % REP
                    src = q_o[ds(g * (REP * HD) + h * HD, HD), half * 512:half * 512 + 512]
                    scale = s_o[ds(g * REP + h, 1), half * 512:half * 512 + 512].rearrange("a n -> (a n)").partition_broadcast(P)
                    sp.dma_start(stage[:, slot, 0, :].bitcast(i32), src).then_inc(staged[slot], 16)
                    sp.dma_start(stage[:, slot, 1, :], scale).then_inc(staged[slot], 16)

            def load_int(g, p):
                rows, at = 4 * P * (p % 2), g * (REP * HD) + (REP - NI + p // 2) * HD
                if not isinstance(g, int) or p:
                    sp.wait_ge(S["int_ready"], INT_PIECES * g + p)
                sp.dma_start(int_stage[:, :].rearrange("p (k n) -> p k n", k=4),
                             q_q[rows:rows + 4 * P, ds(at, HD)].rearrange("(k p) n -> p k n", p=P)).then_inc(S["int_in"], 16)

            def load_int_scales(g):
                at = g * HD
                if not isinstance(g, int):
                    sp.wait_ge(S["int_scaled"], g * 1)
                sp.dma_start(int_raw[:, :], s_q_cols[ds(at, HD), :]).then_inc(S["int_raw_in"], 16)

            sp.wait_ge(S["idx_in"], 32)
            sp.wait_ge(S["wc_zero"], 1)
            for c in range(NC):
                with sp.Fori(CT * c, CT * (c + 1)) as i:
                    load_cond(sp, i, 0, c)
                    if c >= ACT_CHUNKS:
                        load_cond(sp, i, 1, c)
                if c + 1 < NC:
                    load_x(c + 1)
                if c == 0:
                    load_piece(0, 0)
                    load_piece(0, 1)
                    load_int_scales(0)
                    load_int(0, 0)
            for dst, src in ((cos_t, rope_cos), (sin_t, rope_sin), (mask_t, neg_mask), (id16, ident16)):
                sp.dma_start(dst[:, :], src).then_inc(S["consts_in"], 16)
            load_int(0, 1)
            for z in range(2, PIECES):
                load_piece(0, z)
                if z in (5, 7):
                    load_int(0, (z - 1) // 2)
            with sp.Fori(1, NKV) as g:
                for z in range(PIECES):
                    if z == QKV_PIECES:
                        load_int_scales(g)
                        for p in range(INT_PIECES):
                            load_int(g, p)
                    load_piece(g, z)

            sp.wait_ge(S["w_ready"], PIECES * NKV)
            for k in range(WB_STATS):
                if k >= 2:
                    sp.wait_ge(S["wb_read"], k - 1)
                sp.dma_start(w32[:, k % 2, :], w_base_t[P * (k // 2):P * (k // 2 + 1), CH * (k % 2):CH * (k % 2 + 1)]).then_inc(wb_in[k % 2], 16)
            with sp.Fori(0, NT) as i:
                for odd in range(2):
                    s = sp.value_load(sidx[0:1, ds(i * 2 + odd, 1)], min_val=0, max_val=7)
                    sp.dma_start(ws[SEQ * odd:SEQ * (odd + 1), ds(i, 1), :],
                                 w_sess[ds(s, 1), :, :].rearrange("a c d -> c a d")).then_inc(S["wsess_in"], 16)
            sp.wait_ge(S["qk_ready"], len(ROPED) * NKV * NC)
            for dst, src in ((b2_t, b2.partition_broadcast(P)), (w2_t, w2), (bs_t, b_sess), (ids_t, ids_rep),
                             (len_t, len_rep), (seq_t, seq_rep), (row_t, row_of), (tt_t, t_of), (tri_t, tri),
                             (id32, ident32), (wr_t, w_router_t.rearrange("(k p) e -> p k e", p=P))):
                sp.dma_start(dst, src).then_inc(S["c2_in"], 16)
            at[0] = 2048
            load_stats(a_t.rearrange("(k p) n -> p k n", p=P), 1024, "stats2_in", work)
            load_stats(w_router_t.rearrange("(k p) e -> p k e", p=P), 64, "stats2_in", work)
            load_stats(w2, 64, "stats2_in", work)
            load_stats(w_sess.rearrange("s (q c) d -> (s q) (c d)", q=16), 512, "stats2_in", work)
            load_stats(b_sess.rearrange("s (q d) -> (s q) d", q=16), 8, "stats2_in", work)
            sp.wait_ge(S["probs_split"], 2 + 2 * NKV * NC)
            for z in range(WB_PIECES + A_PIECES):
                if z >= 2:
                    sp.wait_ge(S["wf_split"], z - 1)
                dst = wstage[:, z % 2, :]
                if z < A_PIECES:
                    dst = dst.rearrange("p (k n) -> p k n", k=4)
                    src = a_t[CH * z:CH * (z + 1), :].rearrange("(k p) n -> p k n", p=P)
                else:
                    k, n0 = (z - A_PIECES) // 2, 512 * (z % 2)
                    src = w_base_t[P * k:P * (k + 1), n0:n0 + 512]
                sp.dma_start(dst, src).then_inc(wf_in[z % 2], 16)
                if z == 1:
                    sp.wait_ge(S["o_done"], YT + YT * NKV * NC)
                    sp.dma_start(bc_t, b_cat).then_inc(S["bcat_in"], 16)
            sp.wait_ge(S["xf_split"], 2 * NT)
            for n in range(2):
                sp.dma_start(bb[n], b_base[512 * n:512 * (n + 1)].partition_broadcast(P)).then_inc(S["bb_in"], 16)
            for t in range(NT):
                sp.wait_ge(S["result"], 2 * (t + 1))
                sp.dma_start(out[P * t:P * (t + 1), :], y[:, t, :]).then_inc(S["stored"], 16)
            sp.wait_ge(S["stored"], 16 * NT)

        NEXT_AT = (0, 1, 2, 4)
        FIRST_PIECES = ((0,), (), (), (2,))

        @block.gpsimd
        def _(gp):
            gp.memset(wc, 0.0).then_inc(S["wc_zero"], 1)

            def over_partitions(ready, count, lo, hi, done):
                gp.wait_ge(S[ready], count)
                gp.partition_all_reduce(top[:, lo:hi], stat[:, lo:hi], P, MAX).then_inc(S[done], 1)
            over_partitions("stat_w", 1, T_CW, T_S4 + 4, "top_w")
            for c in range(NC):
                over_partitions("stat_x", c + 1, T_X + c, T_X + c + 1, "top_x")
            with gp.Fori(0, NC * NKV) as s:
                for n in range(NKT):
                    i, k = n // KT, n % KT
                    if k == 0:
                        continue
                    a = (KT - 1) * i + k - 1
                    gp.wait_ge(S["kt_read"], NKT * s + (n + 1))
                    if k > 1:
                        gp.wait_ge(S["added"], NADD * s + a)
                    gp.tensor_tensor(acc[:, i, :], acc[:, i, :], tile_buf[a % 2], ALU.add).then_inc(S["added"], 1)
            over_partitions("stat_wb", 1, T_WB, T_WB + 1, "top_wb")
            over_partitions("stat_c2", 1, T_A, T_W2 + 1, "top_c2")
            over_partitions("stat_c2", 1, T_WS, T_BS + 1, "top_c2")
            over_partitions("stat_x1", 1, T_X1, T_X1 + 1, "top_x1")
            for i in range(NT):
                for kh in range(2):
                    gp.wait_ge(S["src_biased"], 2 * i + kh + 1)
                    tmp = src_tmp[i % 2][kh].rearrange("p (k e s) -> p k e s", e=2, s=SEQ)
                    gp.tensor_tensor(tmp, tmp, tm_t[:, 4 * kh:4 * kh + 4, 2 * i:2 * i + 2].unsqueeze(3).broadcast_to([P, 4, 2, SEQ]),
                                     ALU.mult).then_inc(S["src_ready"], 1)

        @block.vector
        def _(dve):
            chain = [0]

            def link(ins):
                chain[0] += 1
                ins.then_inc(S["scal"], 1)
                dve.wait_ge(S["scal"], chain[0])

            def dequant_scale(g, z):
                slot = z % 2
                dve.wait_ge(staged[slot], 32 * (PIECES // 2) * g + 32 * (z // 2 + 1))
                if not isinstance(g, int) or PIECES * g + z >= 2:
                    dve.wait_ge(S["w_ready"], PIECES * g + (z - 1))
                dve.scalar_tensor_tensor(out=w32[:, slot, :], in0=stage[:, slot, 0, :].bitcast(i32), scalar=-8.0,
                                         in1=stage[:, slot, 1, :], op0=ALU.add, op1=ALU.mult).then_inc(S["dq_scaled"], 1)

            def piece_dst(z, part):
                if z < QKV_PIECES:
                    return w_qkv[:, z // 2, part, 4 * (z % 2):4 * (z % 2) + 4, :].rearrange("p k n -> p (k n)")
                return w_out_piece(z - QKV_PIECES, part)

            def dequant_split(g, z):
                scale = UNIT_SCALE[UNITS[z // 2]] if z < QKV_PIECES else col(S4 + 3)
                dve.wait_ge(S["dq_hi"], PIECES * g + z + 1)
                dve.scalar_tensor_tensor(out=piece_dst(z, 1), in0=w32[:, z % 2, :], scalar=scale,
                                         in1=piece_dst(z, 0), op0=ALU.mult, op1=ALU.subtract).then_inc(S["w_ready"], 1)

            def dequant(g, z):
                dequant_scale(g, z)
                dequant_scale(g, z + 1)
                dequant_split(g, z)
                dequant_split(g, z + 1)

            def absmax(to, src, axis=X):
                return dve.tensor_reduce(to, src, axis, ALU.max, apply_absolute_value=True)

            def pow2(scale, inverse, of, n, b, bits_up):
                link(dve.tensor_scalar_max(of, of, TINY))
                link(dve.tensor_single_scalar(bits[:, b:b + n], of.bitcast(i32), EXPONENT, ALU.bitwise_and))
                link(dve.tensor_scalar(col(scale, n).bitcast(i32), bits[:, b:b + n], -1.0, float((254 + bits_up) << 23), ALU.mult, ALU.add))
                return dve.tensor_scalar(col(inverse, n), bits[:, b:b + n].bitcast(f32), 2.0 ** -bits_up, None, ALU.mult)

            dve.wait_ge(S["stats_in"], 80)
            at = 0
            for n, size in ((T_CW, 512), (T_S4, 256), (T_S4 + 1, 64), (T_S4 + 2, 64), (T_S4 + 3, 256)):
                last = absmax(stat[:, n:n + 1], raw[:, at:at + size])
                at += size
            last.then_inc(S["stat_w"], 1)

            def scale_ints(g):
                dve.wait_ge(S["int_raw_in"], 16 * g + 16)
                if not isinstance(g, int):
                    dve.wait_ge(S["kt_read"], NKT * NC * g)
                dve.tensor_scalar(int_scale[:, :], int_raw[:, :], UNIT_SCALE[0], None, ALU.mult).then_inc(S["int_scaled"], 1)

            def chunk_max(c):
                dve.wait_ge(x_in[c], 16)
                absmax(stat[:, T_X + c:T_X + c + 1], y[:, CT * c:CT * (c + 1), :].rearrange("p i n -> p (i n)")).then_inc(S["stat_x"], 1)

            def chunk_scale(c):
                dve.wait_ge(S["top_x"], c + 1)
                m = col(BOUND + c)
                link(dve.scalar_tensor_tensor(out=m, in0=top[:, T_X + c:T_X + c + 1], scalar=float(SEQ),
                                              in1=top[:, T_CW:T_CW + 1], op0=ALU.mult, op1=ALU.mult))
                pow2(SH + c, ISH + c, m, 1, 4 + c, H_BITS).then_inc(S["h_scale_ready"], 1)
                dve.wait_ge(S["h_scale_ready"], c + 1)

            dve.wait_ge(S["top_w"], 1)
            link(dve.tensor_copy(col(M, 4), top[:, T_S4:T_S4 + 4]))
            pow2(S4, IS4, col(M, 4), 4, 0, W_BITS).then_inc(S["w_scales_ready"], 1)
            dve.wait_ge(S["w_scales_ready"], 1)
            chunk_max(0)
            chunk_scale(0)
            for c in range(NC):
                for k in range(KT):
                    n = c * KT + k
                    if k == (KT // 4 if c == 0 else 0) and c + 1 < NC:
                        chunk_max(c + 1)
                    dve.wait_ge(S["cond_hi"], n + 1)
                    t = slice(CH * c, CH * (c + 1))
                    dve.scalar_tensor_tensor(out=hid[:, 1, k, t], in0=cond_bank(n)[:, :], scalar=col(SH + c),
                                             in1=hid[:, 0, k, t], op0=ALU.mult, op1=ALU.subtract).then_inc(S["cond_split"], 1)
                if c == 0:
                    scale_ints(0)
                if c + 1 < NC:
                    chunk_scale(c + 1)
                for z in FIRST_PIECES[c]:
                    dequant(0, z)
            def score_factors():
                link(dve.tensor_scalar(col(A, NC), col(ISH, NC), 1.0 / QKV_DOWN, None, ALU.mult))
                link(dve.tensor_scalar(col(QS, NC), col(A, NC), col(IS4), None, ALU.mult))
                link(dve.tensor_scalar(col(KS, NC), col(A, NC), col(IS4 + 1), HD ** -0.5, ALU.mult, ALU.mult))
                link(dve.tensor_tensor(col(F_SCORE, NC), col(QS, NC), col(KS, NC), ALU.mult))
                link(dve.tensor_scalar(col(AV, NC), col(A, NC), col(IS4 + 2), None, ALU.mult))
                link(dve.tensor_scalar(col(F_OUT, NC), col(AV, NC), col(IS4 + 3), None, ALU.mult))

            def small_stats():
                dve.reduce_max(stat[:, T_WB:T_WB + 1], wbmax, X).then_inc(S["stat_wb"], 1)
                dve.wait_ge(S["c2_in"], 16 * 11)
                absmax(stat[:, T_B2:T_B2 + 1], b2_t)
                dve.wait_ge(S["stats2_in"], 80)
                at = 2048
                for n, size in ((T_A, 1024), (T_R, 64), (T_W2, 64), (T_WS, 512), (T_BS, 8)):
                    last = absmax(stat[:, n:n + 1], work[:, at:at + size])
                    at += size
                last.then_inc(S["stat_c2"], 1)

            def small_scales():
                dve.wait_ge(S["top_wb"], 1)
                dve.wait_ge(S["top_c2"], 2)
                dve.tensor_copy(col(M + 3), top[:, T_WB:T_WB + 1])
                link(dve.tensor_copy(col(M, 3), top[:, T_A:T_A + 3]))
                pow2(SC2, ISC2, col(M, 4), 4, 8, H_BITS).then_inc(S["scales_ready"], 1)
                dve.wait_ge(S["scales_ready"], 1)

            def small_operands():
                for n, (dst, src, scale) in enumerate(small_parts()):
                    dve.wait_ge(S["small_hi"], n + 1)
                    dve.scalar_tensor_tensor(out=dst(1), in0=src, scalar=scale, in1=dst(0), op0=ALU.mult,
                                             op1=ALU.subtract).then_inc(S["small_split"], 1)
                dve.tensor_scalar(hot_t, ids_t, row_t[0:NEXP, :], None, ALU.is_equal).then_inc(S["onehot_made"], 1)
                dve.tensor_scalar(cm_t, len_t, row_t, None, ALU.is_gt)
                dve.tensor_tensor(tm_t, seq_t.unsqueeze(1).broadcast_to([P, KT, B]), tt_t.unsqueeze(2).broadcast_to([P, KT, B]),
                                  ALU.is_gt).then_inc(S["masks_made"], 1)

            def mask_sessions():
                dve.wait_ge(S["masks_made"], 1)
                dve.wait_ge(S["wsess_in"], 16 * B)
                dve.tensor_tensor(ws, ws, cm_t.unsqueeze(2).broadcast_to([P, NT, HID]), ALU.mult).then_inc(S["wsess_masked"], 1)

            def tables(t, b):
                return t[:, :].unsqueeze(1).broadcast_to([P, b, SEQ])

            def rope_write(idx, part):
                u = UNITS[idx]
                if u == "k":
                    return kb[:, part, :].rearrange("p (b s) -> p b s", b=CB)
                return qb[:, u // 2, part, :, u % 2, :]

            def rope(p4, j):
                g, c = p4
                m = 5 * NC * g + (5 * c + roped_index(j))
                if j < NU:
                    bank, ready, count = unit_bank[j], "proj_done", NU * NC * g + (NU * c + j + 1)
                    read, read_count = "proj_read", count
                else:
                    bank, ready, count = acc[:, j - NU, :], "added", NADD * NC * g + (NADD * c + (KT - 1) * (j - NU + 1))
                    read, read_count = "acc_read", NI * NC * g + (NI * c + j - NU + 1)
                a = ra[:, roped_index(j) % 2, :].rearrange("p (b s) -> p b s", b=CB)
                b = rb[:, :].rearrange("p (b s) -> p b s", b=CB)
                src = bank[:, :].rearrange("p (b s) -> p b s", b=CB)
                dve.wait_ge(S[ready], count)
                if not isinstance(g, int) or m >= 2:
                    dve.wait_ge(S["qk_ready"], m - (1 if roped_index(j) else 0))
                dve.tensor_tensor(a, src, tables(cos_t, CB), ALU.mult)
                half = HD // 2
                if not isinstance(g, int) or m >= 1:
                    dve.wait_ge(S["rope_sum"], m)
                dve.tensor_tensor(b[0:half], src[half:HD], sin_t[half:HD, :].unsqueeze(1).broadcast_to([half, CB, SEQ]), ALU.mult)
                dve.tensor_tensor(b[half:HD], src[0:half], sin_t[0:half, :].unsqueeze(1).broadcast_to([half, CB, SEQ]),
                                  ALU.mult).then_inc(S[read], 1)
                dve.wait_ge(S[read], read_count)
                dve.tensor_tensor(a, a, b, ALU.add).then_inc(S["rope_sum"], 1)

            def rope_split(p4, j):
                g, c = p4
                m = 5 * NC * g + (5 * c + roped_index(j))
                a = ra[:, roped_index(j) % 2, :].rearrange("p (b s) -> p b s", b=CB)
                dve.wait_ge(S["rope_hi"], m + 1)
                dve.tensor_tensor(rope_write(j, 1), a, rope_write(j, 0), ALU.subtract).then_inc(S["qk_ready"], 1)

            def v_split(p4):
                g, c = p4
                dve.wait_ge(S["v_hi"], NC * g + (c + 1))
                dve.scalar_tensor_tensor(out=vb[:, 1, :, :].rearrange("p t d -> p (t d)"), in0=unit_bank[V_AT][:, :], scalar=QKV_DOWN,
                                         in1=vb[:, 0, :, :].rearrange("p t d -> p (t d)"), op0=ALU.mult,
                                         op1=ALU.subtract).then_inc(S["proj_read"], 1)

            def soft_mask(g, c, h):
                r = 2 * NC * g + (2 * c + h)
                dve.wait_ge(S["scores_done"], r + 1 + 2)
                dve.wait_ge(S["probs_split"], r + 1)
                dve.scalar_tensor_tensor(out=sm[:, h, :, :], in0=score_bank[h][:, :].rearrange("p (b s) -> p b s", b=CB),
                                         scalar=col(F_SCORE + c), in1=tables(mask_t, CB), op0=ALU.mult,
                                         op1=ALU.add).then_inc(S["masked"], 1)

            def soft_shift(g, c, h):
                r = 2 * NC * g + (2 * c + h)
                dve.wait_ge(S["masked"], r + 1)
                dve.reduce_max(rmax[:, h, :], sm[:, h, :, :], X).then_inc(S["rowmaxed"], 1)
                dve.wait_ge(S["rowmaxed"], r + 1)
                dve.tensor_tensor(sm[:, h, :, :], sm[:, h, :, :], rmax[:, h, :].unsqueeze(2).broadcast_to([P, CB, SEQ]),
                                  ALU.subtract).then_inc(S["shifted"], 1)

            def soft_norm(g, c, h):
                r = 2 * NC * g + (2 * c + h)
                dve.wait_ge(S["exps"], r + 1)
                dve.reduce_sum(rsum[:, h, :], sm[:, h, :, :], X).then_inc(S["summed"], 1)
                dve.wait_ge(S["summed"], r + 1)
                dve.reciprocal(rinv[:, h, :], rsum[:, h, :]).then_inc(S["inverted"], 1)
                dve.wait_ge(S["inverted"], r + 1)
                dve.scalar_tensor_tensor(out=sm[:, h, :, :], in0=sm[:, h, :, :], scalar=P_UP,
                                         in1=rinv[:, h, :].unsqueeze(2).broadcast_to([P, CB, SEQ]), op0=ALU.mult,
                                         op1=ALU.mult).then_inc(S["probs"], 1)

            def prob_split(g, c, h):
                r = 2 * NC * g + (2 * c + h)
                dve.wait_ge(S["probs_hi"], r + 1)
                dve.tensor_tensor(pp[:, 1, :], sm[:, h, :, :].rearrange("p b s -> p (b s)"), pp[:, 0, :],
                                  ALU.subtract).then_inc(S["probs_split"], 1)

            def pt_copy(g, c, h):
                r = 2 * NC * g + (2 * c + h)
                dve.wait_ge(S["tp_done"], r + 1 + 2)
                dve.wait_ge(S["pv_done"], r + 2)
                dve.tensor_copy(pt[:, :, :, :].rearrange("p l t n -> p (l t n)"),
                                tp[:, :, :, :].rearrange("p l t n -> p (l t n)")).then_inc(S["pt_copied"], 1)

            def ctx_lo(g, c, h):
                r = 2 * NC * g + (2 * c + h)
                for e in range(2):
                    dve.wait_ge(S["ctx_hi"], 4 * NC * g + (4 * c + 2 * h + e + 1))
                    last = dve.scalar_tensor_tensor(out=ctx_dst(h, e, 1), in0=ctx_src(e), scalar=1.0 / P_UP,
                                                    in1=ctx_dst(h, e, 0), op0=ALU.mult, op1=ALU.subtract)
                last.then_inc(S["ctx_split"], 1)

            def x1_max(c, t):
                dve.wait_ge(S["y_added"], YT * NC * (NKV - 1) + (YT * c + t + 1 + YT))
                i, half = out_tile(t)
                return absmax(x1max[:, YT * c + t:YT * c + t + 1], y[:, CT * c + i, 512 * half:512 * half + 512])

            def add_out(g, c, ahead, between, last=False):
                banks = early_bank if last and c == NC - 2 else out_bank
                for t in range(YT):
                    dve.wait_ge(S["o_done"], YT * NC * g + (YT * c + t + 1 + YT))
                    i, half = out_tile(t)
                    dst = y[:, CT * c + i, 512 * half:512 * half + 512]
                    dve.scalar_tensor_tensor(out=dst, in0=banks[t % len(banks)][:, :], scalar=col(F_OUT + c), in1=dst,
                                             op0=ALU.mult, op1=ALU.add).then_inc(S["y_added"], 1)
                    if last and t:
                        x1_max(c, t - 1)
                    if ahead and t in ROPE_AFTER:
                        rope(ahead, NU + ROPE_AFTER.index(t))
                    if ahead and t - 1 in ROPE_AFTER:
                        rope_split(ahead, NU + int(t == YT - 1))
                    between(t)
                if last:
                    return x1_max(c, YT - 1)

            dve.wait_ge(S["consts_in"], 64)

            ROPE_AFTER = (3, 6)

            def step(g, c, ahead, extra, between, last=False):
                if ahead or not last:
                    soft_mask(g, c, 0)
                    soft_shift(g, c, 0)
                if ahead:
                    rope(ahead, 0)
                if ahead or not last:
                    soft_norm(g, c, 0)
                soft_mask(g, c, 1)
                prob_split(g, c, 0)
                soft_shift(g, c, 1)
                if ahead:
                    extra(0)
                pt_copy(g, c, 0)
                soft_norm(g, c, 1)
                if ahead:
                    rope_split(ahead, 0)
                prob_split(g, c, 1)
                if ahead:
                    rope(ahead, 1)
                pt_copy(g, c, 1)
                if ahead:
                    rope_split(ahead, 1)
                    extra(1)
                    rope(ahead, 2)
                ctx_lo(g, c, 0)
                if ahead:
                    rope_split(ahead, 2)
                    extra(2)
                ctx_lo(g, c, 1)
                if ahead:
                    v_split(ahead)
                if last and c == NC - 2:
                    soft_mask(g, c + 1, 0)
                    soft_shift(g, c + 1, 0)
                return add_out(g, c, ahead, between, last)

            def group(g, last=False):
                def nothing(j):
                    pass

                def wo_between(t):
                    if t < 2:
                        dequant(g, PIECES - REP + 2 * t)

                def nxt_between(t):
                    if t in NEXT_AT:
                        dequant(g + 1, 2 * NEXT_AT.index(t))

                def scales(j):
                    if j == 1:
                        scale_ints(g + 1)

                def wo_next(t):
                    if t in (3, 4):
                        dequant(g + 1, QKV_PIECES + 2 * (t - 3))

                def wb_stats(t):
                    for k in (2 * t, 2 * t + 1):
                        dve.wait_ge(wb_in[k % 2], 16 * (k // 2 + 1))
                        absmax(wbmax[:, k:k + 1], w32[:, k % 2, :]).then_inc(S["wb_read"], 1)

                def soft_between(t):
                    if t == 1:
                        soft_norm(g, NC - 1, 0)

                def small_between(t):
                    if t == 1:
                        small_stats()
                    elif t == 4:
                        small_scales()
                    elif t == 5:
                        small_operands()
                    elif t == 6:
                        mask_sessions()
                for c in range(NC):
                    ahead = (g, c + 1) if c + 1 < NC else (None if last else (g + 1, 0))
                    extra = scales if not last and c == 3 else nothing
                    if last:
                        between = (wo_between, wb_stats, soft_between, small_between)[c]
                    else:
                        between = (wo_between, nothing, nxt_between, wo_next)[c]
                    end = step(g, c, ahead, extra, between, last)
                return end

            for j in range(NU):
                if j == V_AT:
                    score_factors()
                    v_split((0, 0))
                else:
                    rope((0, 0), j)
                    rope_split((0, 0), j)
                if j < 3:
                    dequant(0, 4 + 2 * j)
            rope((0, 0), NU)
            rope_split((0, 0), NU)
            dequant(0, PIECES - REP - 2)
            rope((0, 0), NU + 1)
            rope_split((0, 0), NU + 1)
            with dve.Fori(0, NKV - 1) as g:
                group(g)
            group(NKV - 1, last=True).then_inc(S["x1_maxed"], 1)

            dve.wait_ge(S["x1_maxed"], 1)
            dve.reduce_max(stat[:, T_X1:T_X1 + 1], x1max[:, :], X).then_inc(S["stat_x1"], 1)
            dve.wait_ge(S["bias_done"], 1)
            dve.tensor_copy(bias_t, ex[:, 0:B]).then_inc(S["bias_ready"], 1)
            dve.wait_ge(S["top_x1"], 1)
            m, mx = col(BOUND), col(BOUND_X)
            link(dve.scalar_tensor_tensor(out=m, in0=top[:, T_X1:T_X1 + 1], scalar=float(SEQ), in1=top[:, T_WS:T_WS + 1],
                                          op0=ALU.mult, op1=ALU.mult))
            link(dve.tensor_tensor(m, m, top[:, T_BS:T_BS + 1], ALU.add))
            pow2(SH2, ISH2, m, 1, 0, H_BITS).then_inc(S["h2_scale_ready"], 1)
            dve.wait_ge(S["h2_scale_ready"], 1)

            def h2_lo(i):
                for e in range(2):
                    for th in range(2):
                        dve.wait_ge(S["h2_hi"], 4 * i + 2 * e + th + 1)
                        t = slice(512 * th, 512 * th + 512)
                        dve.scalar_tensor_tensor(out=h2[i % 2][:, 1, e, t], in0=g32[:, e, t], scalar=col(SH2),
                                                 in1=h2[i % 2][:, 0, e, t], op0=ALU.mult, op1=ALU.subtract).then_inc(S["h2_split"], 1)

            def wf_lo(z):
                dve.wait_ge(S["wf_hi"], z + 1)
                dve.scalar_tensor_tensor(out=wf_dst(z, 1), in0=wstage[:, z % 2, :], scalar=wf_scale(z), in1=wf_dst(z, 0),
                                         op0=ALU.mult, op1=ALU.subtract).then_inc(S["wf_split"], 1)

            def source_bias(i):
                if i >= 2:
                    dve.wait_ge(S["xf_split"], 2 * (i - 1))
                for kh in range(2):
                    dve.wait_ge(S["src_done"], 2 * i + kh + 1)
                    dve.scalar_tensor_tensor(out=src_tmp[i % 2][kh].rearrange("p (m s) -> p m s", s=SEQ),
                                             in0=score_bank[kh][:, :].rearrange("p (m s) -> p m s", s=SEQ),
                                             scalar=col(F_SRC), in1=b2_t.unsqueeze(1).broadcast_to([P, 8, SEQ]),
                                             op0=ALU.mult, op1=ALU.add).then_inc(S["src_biased"], 1)

            def source_lo(i):
                for kh in range(2):
                    dve.wait_ge(S["xf_hi"], 2 * i + kh + 1)
                    dve.tensor_tensor(source_dst(i, kh, 1), src_tmp[i % 2][kh].rearrange("p (k t) -> p k t", k=4),
                                      source_dst(i, kh, 0), ALU.subtract).then_inc(S["xf_split"], 1)

            link(dve.scalar_tensor_tensor(out=mx, in0=top[:, T_W2:T_W2 + 1], scalar=float(HID), in1=m, op0=ALU.mult, op1=ALU.mult))
            link(dve.tensor_tensor(mx, mx, stat[:, T_B2:T_B2 + 1], ALU.add))
            link(pow2(SX, ISX, mx, 1, 1, H_BITS))
            link(dve.tensor_tensor(col(F_SRC), col(ISH2), col(ISC2 + 2), ALU.mult))
            link(dve.tensor_tensor(col(F_SRC), col(F_SRC), col(SX), ALU.mult))
            link(dve.tensor_scalar(b2_t, b2_t, col(SX), None, ALU.mult))
            link(dve.tensor_tensor(col(F_LG), col(ISX), col(ISC2 + 1), ALU.mult))
            link(dve.scalar_tensor_tensor(out=col(F_LORA), in0=col(SC2 + 3), scalar=2.0, in1=col(ISC2), op0=ALU.mult, op1=ALU.mult))
            link(dve.tensor_tensor(col(F_BASE), col(ISX), col(ISC2 + 3), ALU.mult))
            h2_lo(0)
            for i in range(NT):
                if i + 1 < NT:
                    h2_lo(i + 1)
                wf_lo(i)
                if i:
                    source_lo(i - 1)
                source_bias(i)
            for z in range(NT, A_PIECES + WB_PIECES):
                wf_lo(z)
            source_lo(NT - 1)

            routed = [0]
            dve.wait_ge(S["lg_done"], NT)

            def step_of(ins):
                routed[0] += 1
                ins.then_inc(S["route"], 1)
                dve.wait_ge(S["route"], routed[0])
            step_of(dve.tensor_scalar(lg, lg_bank[:, 0:NT * NEXP].rearrange("p (t e) -> p t e", t=NT), col(F_LG), None, ALU.mult))
            shape = [P, NT, NEXP, NEXP]
            mine = lg.unsqueeze(3).broadcast_to(shape)
            other = lg.unsqueeze(2).broadcast_to(shape)
            g4 = big1.rearrange("p (t e j) -> p t e j", t=NT, e=NEXP)
            q4 = big2.rearrange("p (t e j) -> p t e j", t=NT, e=NEXP)
            tri4 = tri_t.rearrange("p (e j) -> p e j", e=NEXP).unsqueeze(1).broadcast_to(shape)
            dve.reduce_max(l1, lg, X)
            step_of(dve.tensor_tensor(q4, other, mine, ALU.is_equal))
            step_of(dve.tensor_tensor(le, lg, l1.unsqueeze(2).broadcast_to([P, NT, NEXP]), ALU.subtract))
            dve.tensor_tensor(g4, other, mine, ALU.is_gt)
            step_of(dve.tensor_tensor(q4, q4, tri4, ALU.mult))
            step_of(dve.tensor_tensor(g4, g4, q4, ALU.add))
            step_of(dve.reduce_sum(rk, g4, X))
            dve.wait_ge(S["route_exp"], 1)
            step_of(dve.scalar_tensor_tensor(out=rk, in0=rk, scalar=2.0, in1=le, op0=ALU.is_lt, op1=ALU.mult))
            step_of(dve.reduce_sum(dn, rk, X))
            step_of(dve.reciprocal(di, dn))
            dve.tensor_tensor(gates, rk.unsqueeze(3).broadcast_to([P, NT, NEXP, RANK]),
                              di.unsqueeze(2).unsqueeze(3).broadcast_to([P, NT, NEXP, RANK]), ALU.mult).then_inc(S["route_ready"], 1)
            dve.wait_ge(S["lora_copied"], NC)
            for c in range(NC):
                dve.wait_ge(S["wexp_done"], c + 1)
                dve.scalar_tensor_tensor(out=hw[:, CH * c:CH * (c + 1)], in0=hw[:, CH * c:CH * (c + 1)], scalar=col(F_LORA),
                                         in1=gate_bank[c % 2][:, :], op0=ALU.mult, op1=ALU.mult).then_inc(S["lora_ready"], 1)
            dve.wait_ge(S["bb_in"], 32)
            for n in range(2 * NT):
                dst = y[:, n // 2, 512 * (n % 2):512 * (n % 2) + 512]
                dve.wait_ge(S["base_done"], n + 1)
                dve.scalar_tensor_tensor(out=dst, in0=base_bank[n % 4][:, :], scalar=col(F_BASE), in1=dst,
                                         op0=ALU.mult, op1=ALU.add).then_inc(S["base_added"], 1)
                dve.wait_ge(S["base_added"], n + 1)
                dve.tensor_tensor(dst, dst, bb[n % 2], ALU.add).then_inc(S["result"], 1)

        @block.scalar
        def _(act):
            def piece_dst(z):
                if z < QKV_PIECES:
                    return w_qkv[:, z // 2, 0, 4 * (z % 2):4 * (z % 2) + 4, :].rearrange("p k n -> p (k n)")
                return w_out_piece(z - QKV_PIECES, 0)

            def dequant_hi(g, z):
                scale = UNIT_SCALE[UNITS[z // 2]] if z < QKV_PIECES else col(S4 + 3)
                act.wait_ge(S["dq_scaled"], PIECES * g + z + 1)
                act.activation(piece_dst(z), w32[:, z % 2, :], ACT.Copy, scale=scale).then_inc(S["dq_hi"], 1)

            act.wait_ge(S["idx_in"], 32)
            act.wait_ge(S["wc_zero"], 1)

            for c in range(ACT_CHUNKS):
                with act.Fori(CT * c, CT * (c + 1)) as i:
                    load_cond(act, i, 1, c)

            def int_piece(g, p):
                act.wait_ge(S["int_in"], 16 * INT_PIECES * g + 16 * (p + 1))
                act.activation(w_int[:, p // 2, 4 * (p % 2):4 * (p % 2) + 4, :].rearrange("p k n -> p (k n)"), int_stage[:, :],
                               ACT.Copy, bias=-8.0).then_inc(S["int_ready"], 1)

            for c in range(NC):
                act.wait_ge(S["h_scale_ready"], c + 1)
                for k in range(KT):
                    n = c * KT + k
                    act.wait_ge(S["cond_done"], n + 1)
                    act.activation(hid[:, 0, k, CH * c:CH * (c + 1)], cond_bank(n)[:, :], ACT.Copy,
                                   scale=col(SH + c)).then_inc(S["cond_hi"], 1)
                act.wait_ge(S["w_scales_ready"], 1)
                for z in FIRST_PIECES[c]:
                    dequant_hi(0, z)
                    dequant_hi(0, z + 1)
                if c in (0, NC - 1):
                    int_piece(0, int(c > 0))
            def rope_hi(p4, j):
                g, c = p4
                m = 5 * NC * g + (5 * c + roped_index(j))
                a = ra[:, roped_index(j) % 2, :].rearrange("p (b s) -> p b s", b=CB)
                u = UNITS[j]
                dst = kb[:, 0, :].rearrange("p (b s) -> p b s", b=CB) if u == "k" else qb[:, u // 2, 0, :, u % 2, :]
                act.wait_ge(S["rope_sum"], m + 1)
                act.wait_ge(S["scores_done"], 2 * NC * g + 2 * c + 2)
                act.activation(dst, a, ACT.Copy).then_inc(S["rope_hi"], 1)

            def v_hi(p4):
                g, c = p4
                act.wait_ge(S["proj_done"], NU * NC * g + (NU * c + V_AT + 1))
                act.wait_ge(S["pv_done"], 2 * NC * g + 2 * c + 2)
                act.activation(vb[:, 0, :, :].rearrange("p t d -> p (t d)"), unit_bank[V_AT][:, :], ACT.Copy,
                               scale=QKV_DOWN).then_inc(S["v_hi"], 1)

            def exps(g, c, h):
                act.wait_ge(S["shifted"], 2 * NC * g + (2 * c + h + 1))
                act.activation(sm[:, h, :, :], sm[:, h, :, :], ACT.Exp).then_inc(S["exps"], 1)

            def prob_hi(g, c, h):
                r = 2 * NC * g + (2 * c + h)
                act.wait_ge(S["probs"], r + 1)
                act.wait_ge(S["tp_done"], r + 2)
                act.activation(pp[:, 0, :], sm[:, h, :, :].rearrange("p b s -> p (b s)"), ACT.Copy).then_inc(S["probs_hi"], 1)

            def ctx_hi(g, c, h):
                r = 2 * NC * g + (2 * c + h)
                act.wait_ge(S["pv_done"], r + 1 + 2)
                act.wait_ge(S["o_done"], YT * NC * g + YT * c + YT)
                for e in range(2):
                    act.activation(ctx_dst(h, e, 0), ctx_src(e), ACT.Copy, scale=1.0 / P_UP).then_inc(S["ctx_hi"], 1)

            def read_tile(p4, n):
                g, c = p4
                i, k = n // KT, n % KT
                first = isinstance(g, int) and g == c == 0
                a = (KT - 1) * i + k - 1
                if n == 0:
                    act.wait_ge(S["int_scaled"], g + 1)
                act.wait_ge(S["kt_done"], NKT * NC * g + (NKT * c + n + 1))
                if k == 0:
                    dst = acc[:, i, :]
                    if not first:
                        act.wait_ge(S["acc_read"], NI * NC * g + (NI * c + i - 1))
                else:
                    dst = tile_buf[a % 2]
                    if not first or a >= 2:
                        act.wait_ge(S["added"], NADD * NC * g + (NADD * c + a - 1))
                act.activation(dst, tile_bank(n, first)[:, :], ACT.Copy, scale=int_scale[:, n:n + 1]).then_inc(S["kt_read"], 1)

            def step(g, c, ahead, extra, tail, last=False):
                if ahead or not last:
                    exps(g, c, 0)
                prob_hi(g, c, 0)
                exps(g, c, 1)
                if ahead:
                    rope_hi(ahead, 0)
                    extra(0)
                prob_hi(g, c, 1)
                if ahead:
                    rope_hi(ahead, 1)
                    extra(1)
                ctx_hi(g, c, 0)
                if ahead:
                    rope_hi(ahead, 2)
                    extra(2)
                    read_tile(ahead, 0)
                    read_tile(ahead, 1)
                ctx_hi(g, c, 1)
                if ahead:
                    v_hi(ahead)
                if last and c == NC - 2:
                    exps(g, c + 1, 0)
                for t in range(YT):
                    if ahead:
                        for n in tiles_at(t):
                            read_tile(ahead, n)
                        if t == 4:
                            rope_hi(ahead, NU)
                        if t == 7:
                            rope_hi(ahead, NU + 1)
                    if t:
                        tail(t - 1)
                tail(YT - 1)

            def group(g, last=False):
                def nothing(j=0):
                    pass

                def pair(g, z):
                    dequant_hi(g, z)
                    dequant_hi(g, z + 1)

                def wo_tail(t):
                    if t == 0:
                        act.wait_ge(S["o_done"], YT * NC * g + YT)
                    if t < 2:
                        pair(g, PIECES - REP + 2 * t)

                def next_int(p):
                    act.wait_ge(S["kt_done"], NKT * NC * g + (NKT * (NC - 1) + KT * (p // 2 + 1)))
                    int_piece(g + 1, p)

                def nxt_tail(t):
                    if t in NEXT_AT:
                        j = NEXT_AT.index(t)
                        act.wait_ge(S["proj_done"], NU * NC * g + (NU * (NC - 1) + j + 1))
                        pair(g + 1, 2 * j)
                    if t == YT - 1:
                        next_int(0)

                def ints(j):
                    next_int(j + 1)

                def wo_next(t):
                    if t in (3, 4):
                        act.wait_ge(S["o_done"], YT * NC * g + (YT * (NC - 1) + YT + CT))
                        pair(g + 1, QKV_PIECES + 2 * (t - 3))

                def small_tail(t):
                    if t == YT - 1:
                        act.wait_ge(S["scales_ready"], 1)
                        for dst, src, scale in small_parts():
                            act.activation(dst(0), src, ACT.Copy, scale=scale).then_inc(S["small_hi"], 1)
                for c in range(NC):
                    ahead = (g, c + 1) if c + 1 < NC else (None if last else (g + 1, 0))
                    if last:
                        step(g, c, ahead, nothing, (wo_tail, nothing, nothing, small_tail)[c], last)
                    else:
                        step(g, c, ahead, ints if c == 3 else nothing, (wo_tail, nothing, nxt_tail, wo_next)[c])

            for j in range(NU):
                for n in (4 * j, 4 * j + 1):
                    read_tile((0, 0), n)
                if j == V_AT:
                    v_hi((0, 0))
                else:
                    rope_hi((0, 0), j)
                for n in (4 * j + 2, 4 * j + 3):
                    read_tile((0, 0), n)
                if j < 3:
                    dequant_hi(0, 4 + 2 * j)
                    dequant_hi(0, 5 + 2 * j)
                if j < 2:
                    int_piece(0, 2 + j)
            rope_hi((0, 0), NU)
            for z in (PIECES - REP - 2, PIECES - REP - 1):
                dequant_hi(0, z)
            rope_hi((0, 0), NU + 1)
            with act.Fori(0, NKV - 1) as g:
                group(g)
            group(NKV - 1, last=True)

            act.wait_ge(S["bias_ready"], 1)

            def wf_hi(z):
                act.wait_ge(wf_in[z % 2], 16 * (z // 2 + 1))
                act.activation(wf_dst(z, 0), wstage[:, z % 2, :], ACT.Copy, scale=wf_scale(z)).then_inc(S["wf_hi"], 1)

            def source_hi(i):
                for kh in range(2):
                    act.wait_ge(S["src_ready"], 2 * i + kh + 1)
                    act.activation(source_dst(i, kh, 0), src_tmp[i % 2][kh].rearrange("p (k t) -> p k t", k=4),
                                   ACT.Copy).then_inc(S["xf_hi"], 1)

            def copy_lora(c):
                act.wait_ge(S["lora_done"], CT * (c + 1))
                act.activation(hw[:, CH * c:CH * (c + 1)], ex[:, :], ACT.Copy).then_inc(S["lora_copied"], 1)
            for i in range(NT):
                tiles = [(e, th) for e in range(2) for th in range(2)]
                for n, (e, th) in enumerate(tiles):
                    act.wait_ge(S["hid_done"], 4 * i + n + 1)
                    if i:
                        act.wait_ge(S["h2_split"], 4 * (i - 1) + n + 1)
                    act.activation(g32[:, e, 512 * th:512 * th + 512], h_bank[e][th][:, :], ACT.Gelu,
                                   bias=bias_t[:, 2 * i + e:2 * i + e + 1]).then_inc(S["gelu_done"], 1)
                if i >= 2:
                    act.wait_ge(S["src_done"], 2 * (i - 1))
                if i == 0:
                    act.wait_ge(S["h2_scale_ready"], 1)
                for n, (e, th) in enumerate(tiles):
                    act.wait_ge(S["gelu_done"], 4 * i + n + 1)
                    act.activation(h2[i % 2][:, 0, e, 512 * th:512 * th + 512], g32[:, e, 512 * th:512 * th + 512],
                                   ACT.Copy, scale=col(SH2)).then_inc(S["h2_hi"], 1)
                wf_hi(i)
                if i >= 2:
                    source_hi(i - 2)
                if i >= CT and i % CT == 2:
                    copy_lora(i // CT - 1)
            wf_hi(NT)
            source_hi(NT - 2)
            for z in range(NT + 1, A_PIECES + WB_PIECES):
                wf_hi(z)
            source_hi(NT - 1)
            copy_lora(NC - 1)
            act.wait_ge(S["route"], 3)
            act.activation(le, le, ACT.Exp).then_inc(S["route_exp"], 1)

        @block.tensor
        def _(pe):
            mm = nc.tensor.matmul
            for c in range(NC):
                pe.wait_ge(x_in[c], 16)
                pe.wait_ge(wc_in[c], 16 * CB)
                for k in range(KT):
                    n = c * KT + k
                    if n >= len(cond_banks):
                        pe.wait_ge(S["cond_split"], n - len(cond_banks) + 1)
                    for i in range(CT):
                        last = mm(cond_bank(n)[:, P * i:P * (i + 1)], y[:, CT * c + i, P * k:P * (k + 1)],
                                  wc[:, CT * c + i, :], start=True, stop=True)
                    last.then_inc(S["cond_done"], 1)

            PARTS = ((0, 0), (0, 1), (1, 0))

            def project(p4, j):
                g, c = p4
                n = NU * NC * g + (NU * c + j)
                pe.wait_ge(S["w_ready"], PIECES * g + 2 * (j + 1))
                if j == 2:
                    pe.wait_ge(S["proj_read"], NU * NC * g + (NU * c + 1))
                elif not (isinstance(g, int) and g == c == 0):
                    if j == V_AT:
                        pe.wait_ge(S["y_added"], YT * NC * g + YT * c)
                    else:
                        pe.wait_ge(S["kt_read"], NKT * NC * g + (NKT * c - j))
                bank = unit_bank[j]
                if UNITS[j] == "v":
                    for i in range(CT):
                        for k in range(KT):
                            for lw, lh in PARTS:
                                last = mm(bank[:, P * i:P * (i + 1)], hid[:, lw, k, CH * c + P * i:CH * c + P * (i + 1)],
                                          w_qkv[:, j, lh, k, :], start=(k == 0 and (lw, lh) == (0, 0)),
                                          stop=(k == KT - 1 and (lw, lh) == (1, 0)))
                else:
                    for k in range(KT):
                        for lw, lh in PARTS:
                            last = mm(bank[:, :], w_qkv[:, j, lw, k, :], hid[:, lh, k, CH * c:CH * (c + 1)],
                                      start=(k == 0 and (lw, lh) == (0, 0)), stop=(k == KT - 1 and (lw, lh) == (1, 0)))
                last.then_inc(S["proj_done"], 1)

            def project_tile(p4, n):
                g, c = p4
                i, k = n // KT, n % KT
                first = isinstance(g, int) and g == c == 0
                if k % 4 == 0:
                    pe.wait_ge(S["int_ready"], INT_PIECES * g + (2 * i + k // 4 + 1))
                if n >= 2:
                    pe.wait_ge(S["kt_read"], NKT * NC * g + (NKT * c + n - 1))
                elif not first:
                    pe.wait_ge(S["proj_read"], NU * NC * g + (NU * c + 2 + n))
                bank = tile_bank(n, first)
                mm(bank[:, :], w_int[:, i, k, :], hid[:, 0, k, CH * c:CH * (c + 1)], start=True, stop=False)
                mm(bank[:, :], w_int[:, i, k, :], hid[:, 1, k, CH * c:CH * (c + 1)], start=False,
                   stop=True).then_inc(S["kt_done"], 1)

            def scores(g, c, h, early=False):
                pe.wait_ge(S["qk_ready"], 5 * NC * g + (5 * c + (3, 5)[h]))
                pe.wait_ge(S["y_added"], YT * NC * g + YT * c + (0 if early else (YT - 1, YT)[h]))
                for b in range(CB):
                    for lq, lk in PARTS:
                        last = mm(score_bank[h][:, SEQ * b:SEQ * (b + 1)], qb[:, h, lq, b, :, :].rearrange("p h s -> p (h s)"),
                                  kb[:, lk, SEQ * b:SEQ * (b + 1)], start=(lq, lk) == (0, 0), stop=(lq, lk) == (1, 0))
                last.then_inc(S["scores_done"], 1)

            def transpose_probs(g, c, h):
                r = 2 * NC * g + (2 * c + h)
                pe.wait_ge(S["probs_split"], r + 1 + 2)
                pe.wait_ge(S["pt_copied"], r + 2)
                for part in range(2):
                    for j in range(CT):
                        last = nc.tensor.transpose(tp[:, part, j, :], pp[:, part, P * j:P * (j + 1)], id16[:, :])
                last.then_inc(S["tp_done"], 1)

            def weigh_values(g, c, h):
                r = 2 * NC * g + (2 * c + h)
                pe.wait_ge(S["proj_read"], NU * NC * g + (NU * c + V_AT + 1))
                pe.wait_ge(S["pt_copied"], r + 1 + 2)
                pe.wait_ge(S["ctx_split"], r + 2)
                for j in range(CT):
                    for lv, lp in PARTS:
                        for e in range(2):
                            rows = slice(SEQ * e, SEQ * (e + 1))
                            last = mm(ctx_columns(e, j), vb[rows, lv, j, :],
                                      pt[rows, lp, j, :].rearrange("k (h s) -> k h s", h=2),
                                      start=(lv, lp) == (0, 0), stop=(lv, lp) == (1, 0))
                last.then_inc(S["pv_done"], 1)

            def project_out(g, c, ahead, early=False):
                banks = early_bank if early else out_bank
                for t in range(YT):
                    if ahead:
                        for n in tiles_at(t)[:2]:
                            project_tile(ahead, n)
                    if t == 0:
                        pe.wait_ge(S["ctx_split"], 2 * NC * g + (2 * c + 1 + 2 + int(early)))
                        if not early:
                            pe.wait_ge(S["masked"], 2 * NC * g + (2 * c + 2))
                    if t % CT == 0:
                        pe.wait_ge(S["w_ready"], PIECES * g + (QKV_PIECES + REP * (1 + t // CT)))
                    if t == 2 and ahead:
                        pe.wait_ge(S["proj_read"], NU * NC * g + NU * (c + 2))
                    if t == 0 or t >= len(banks):
                        pe.wait_ge(S["y_added"], YT * NC * g + (YT * c + YT + (t - len(banks) + 1 if t else -1)))
                    i, half = out_tile(t)
                    n0 = 512 * half
                    for h in range(REP):
                        if ahead and h == REP // 2:
                            for n in tiles_at(t)[2:]:
                                project_tile(ahead, n)
                        if t == 0 and h == REP // 2:
                            pe.wait_ge(S["ctx_split"], 2 * NC * g + (2 * c + 2 + 2))
                        for lc, lw in PARTS:
                            last = mm(banks[t % len(banks)][:, :], cb[:, lc, h, P * i:P * (i + 1)], w_out[:, h, lw, n0:n0 + 512],
                                      start=(h == 0 and (lc, lw) == (0, 0)), stop=(h == REP - 1 and (lc, lw) == (1, 0)))
                    last.then_inc(S["o_done"], 1)

            def step(g, c, ahead, early=False, scored=False):
                if not scored:
                    scores(g, c, 0)
                if ahead:
                    project(ahead, 0)
                scores(g, c, 1)
                if ahead:
                    project(ahead, 1)
                transpose_probs(g, c, 0)
                if ahead:
                    project(ahead, 2)
                weigh_values(g, c, 0)
                transpose_probs(g, c, 1)
                if ahead:
                    project(ahead, 3)
                    project_tile(ahead, 0)
                    project_tile(ahead, 1)
                weigh_values(g, c, 1)
                if early:
                    scores(*ahead, 0, early=True)
                project_out(g, c, ahead, early)

            def group(g, last=False):
                for c in range(NC):
                    step(g, c, (g, c + 1) if c + 1 < NC else (None if last else (g + 1, 0)),
                         early=last and c == NC - 2, scored=last and c == NC - 1)

            pe.wait_ge(S["consts_in"], 64)
            pe.wait_ge(S["cond_split"], NC * KT - 3)
            for j in range(NU):
                project((0, 0), j)
                if j == 0:
                    pe.wait_ge(S["cond_split"], NC * KT)
                for n in range(4 * j, 4 * j + 4):
                    project_tile((0, 0), n)
            pe.wait_ge(S["proj_read"], NU)
            with pe.Fori(0, NKV - 1) as g:
                group(g)
            group(NKV - 1, last=True)

            pe.wait_ge(S["onehot_made"], 1)
            pe.wait_ge(S["y_added"], YT * NC * NKV + YT - 2)
            mm(ex[:, 0:B], bs_t, hot_t, start=True, stop=True).then_inc(S["bias_done"], 1)
            pe.wait_ge(S["wsess_masked"], 1)

            def hidden2(i):
                for e in range(2):
                    rows = slice(SEQ * e, SEQ * (e + 1))
                    if i == 0 and e == 1:
                        pe.wait_ge(S["y_added"], YT * NC * NKV + YT)
                    for th in range(2):
                        if i:
                            pe.wait_ge(S["gelu_done"], 4 * (i - 1) + 2 * e + th + 1)
                        mm(h_bank[e][th][:, :], ws[rows, i, :], y[rows, i, 512 * th:512 * th + 512],
                           start=True, stop=True).then_inc(S["hid_done"], 1)

            def sources(i):
                pe.wait_ge(S["h2_split"], 4 * (i + 1))
                for kh in range(2):
                    if i:
                        pe.wait_ge(S["src_biased"], 2 * (i - 1) + kh + 1)
                    for kk in range(4):
                        for e in range(2):
                            k = 4 * kh + kk
                            at = SEQ * (2 * kk + e)
                            for lh, lw in PARTS:
                                last = mm(score_bank[kh][:, at:at + SEQ], h2[i % 2][:, lh, e, P * k:P * (k + 1)], w2h[:, lw, :],
                                          start=(lh, lw) == (0, 0), stop=(lh, lw) == (1, 0))
                    last.then_inc(S["src_done"], 1)

            def route_and_lora(i):
                c, i0 = i // CT, i % CT
                tokens = slice(P * i0, P * (i0 + 1))
                if i == 0:
                    pe.wait_ge(S["wf_split"], A_PIECES)
                pe.wait_ge(S["xf_split"], 2 * (i + 1))
                for k in range(KT):
                    for lx, lw in PARTS:
                        last = mm(lg_bank[:, NEXP * i:NEXP * (i + 1)], xpart(c, lx)[:, k, tokens], wrh[:, lw, k, :],
                                  start=(k == 0 and (lx, lw) == (0, 0)), stop=(k == KT - 1 and (lx, lw) == (1, 0)))
                last.then_inc(S["lg_done"], 1)
                if c and i0 == 0:
                    pe.wait_ge(S["lora_copied"], c)
                for k in range(KT):
                    for la, lx in PARTS:
                        last = mm(ex[:, tokens], a16[:, la, k, :], xpart(c, lx)[:, k, tokens],
                                  start=(k == 0 and (la, lx) == (0, 0)), stop=(k == KT - 1 and (la, lx) == (1, 0)))
                last.then_inc(S["lora_done"], 1)
            pe.wait_ge(S["small_split"], 2)
            hidden2(0)
            for i in range(NT):
                if i + 1 < NT:
                    hidden2(i + 1)
                sources(i)
                if i >= 2:
                    route_and_lora(i - 2)
            route_and_lora(NT - 2)
            route_and_lora(NT - 1)
            pe.wait_ge(S["wf_split"], WB_PIECES + A_PIECES)
            pe.wait_ge(S["bcat_in"], 16)

            def base(n):
                c, i, n0 = n // YT, (n // 2) % CT, 512 * (n % 2)
                if n >= 4:
                    pe.wait_ge(S["base_added"], n - 3)
                for k in range(KT):
                    for lx, lw in PARTS:
                        mm(base_bank[n % 4][:, :], xpart(c, lx)[:, k, P * i:P * (i + 1)], wb16[:, lw, k, n0:n0 + 512],
                           start=(k == 0 and (lx, lw) == (0, 0)), stop=False)

            def add_lora(n):
                t, n0 = n // 2, 512 * (n % 2)
                mm(base_bank[n % 4][:, :], hw[:, P * t:P * (t + 1)], bc_t[:, n0:n0 + 512], start=False,
                   stop=True).then_inc(S["base_done"], 1)
            for n in range(4):
                if n == 3:
                    pe.wait_ge(S["lora_copied"], NC)
                base(n)
            pe.wait_ge(S["route_ready"], 1)
            pe.wait_ge(S["lora_copied"], NC)
            for c in range(NC):
                if c >= 2:
                    pe.wait_ge(S["lora_ready"], c - 1)
                for i in range(CT):
                    last = mm(gate_bank[c % 2][:, P * i:P * (i + 1)], gates[:, CT * c + i, :, :].rearrange("p e r -> p (e r)"),
                              id32, start=True, stop=True)
                last.then_inc(S["wexp_done"], 1)
            for n in range(2 * NT):
                if n >= 4:
                    base(n)
                pe.wait_ge(S["lora_ready"], n // YT + 1)
                add_lora(n)


def kernel(x, itok_B_0_15, itok_B_0_7, itok_B_2182_4065, _lenS, L0_cond_weights, L0_attn_scales_q,
           L0_attn_scales_k, L0_attn_scales_v, L0_attn_scales_o, L0_attn_qw_q, L0_attn_qw_k, L0_attn_qw_v,
           L0_attn_qw_o, L0_cond2_W_sess, L0_cond2_b_sess, L0_cond2_W2, L0_cond2_b2, L0_ffn_W_base,
           L0_ffn_b_base, L0_ffn_W_router, L0_ffn_A, L0_ffn_B):
    import numpy as np
    import concourse.bacc as bacc
    from concourse.bass_utils import run_bass_kernel_spmd

    def lay(a):
        return np.ascontiguousarray(np.asarray(a))

    f4 = np.float32
    inv_freq = (f4(1.0) / np.power(f4(10000.0), np.arange(0, HD, 2, dtype=f4) / f4(HD))).astype(f4)
    angle = (np.arange(SEQ, dtype=f4)[None, :] * inv_freq[:, None]).astype(f4)
    cos = np.concatenate([np.cos(angle)] * 2, 0).astype(f4) * f4(QKV_DOWN)
    sin = np.concatenate([np.sin(angle), -np.sin(angle)], 0).astype(f4) * f4(QKV_DOWN)
    pos = np.arange(P)
    mask = np.where(pos[:, None] % SEQ >= np.arange(SEQ)[None, :], 0.0, -3.0e38).astype(f4)
    row = (pos % SEQ)[:, None].astype(f4)
    arrays = {
        "x_d": lay(x).reshape(TOK, H),
        "cond_d": lay(itok_B_0_15).reshape(1, B),
        "ids_d": lay(np.broadcast_to(np.asarray(itok_B_0_7), (NEXP, B))),
        "seq_d": lay(np.broadcast_to(np.asarray(itok_B_2182_4065), (P, B))),
        "len_d": lay(np.repeat(np.asarray(_lenS).reshape(NT, 2).T, SEQ, axis=0)),
        "cw_d": lay(L0_cond_weights),
        "sq_d": lay(L0_attn_scales_q),
        "sqc_d": lay(np.asarray(L0_attn_scales_q).reshape(KT, NKV, REP, HD)[:, :, REP - NI:].transpose(1, 3, 2, 0)).reshape(NKV * HD, NI * KT),
        "sk_d": lay(L0_attn_scales_k), "sv_d": lay(L0_attn_scales_v),
        "so_d": lay(L0_attn_scales_o),
        "qq_d": lay(L0_attn_qw_q), "qk_d": lay(L0_attn_qw_k), "qv_d": lay(L0_attn_qw_v), "qo_d": lay(L0_attn_qw_o),
        "wse_d": lay(L0_cond2_W_sess), "bse_d": lay(L0_cond2_b_sess), "w2_d": lay(L0_cond2_W2), "b2_d": lay(L0_cond2_b2),
        "wb_d": lay(np.asarray(L0_ffn_W_base).T), "bb_d": lay(L0_ffn_b_base),
        "wr_d": lay(np.asarray(L0_ffn_W_router).T),
        "a_d": lay(np.asarray(L0_ffn_A).reshape(NEXP * RANK, H).T),
        "bcat_d": lay(np.asarray(L0_ffn_B).transpose(0, 2, 1).reshape(NEXP * RANK, H)),
        "cos_d": cos, "sin_d": sin, "mask_d": mask, "id16_d": np.eye(P, dtype=np.float16),
        "id32_d": np.eye(P, dtype=f4), "row_d": row,
        "t_d": (pos[:, None] + P * np.arange(KT)[None, :]).astype(f4),
        "tri_d": lay(np.broadcast_to(np.tril(np.ones((NEXP, NEXP), f4), -1).reshape(1, -1), (P, NEXP * NEXP))),
    }
    nc = bacc.Bacc("TRN2", target_bir_lowering=False, num_devices=1, dynamic_dma_scratch_size=1024)
    args = [nc.dram_tensor(n, a.shape, mybir.dt.from_np(a.dtype), kind="ExternalInput").ap() for n, a in arrays.items()]
    out = nc.dram_tensor("out_d", (TOK, H), mybir.dt.float32, kind="ExternalOutput").ap()
    build(nc, *args, out)
    result = run_bass_kernel_spmd(nc, [arrays], core_ids=[0])
    return result.results[0]["out_d"].reshape(B, SEQ, H)
```
